# Optimizing a Trainium2 kernel written in Bass

```python
import numpy as np
import jax
import jax.numpy as jnp

def _softmax(x, axis=-1):
    return jax.nn.softmax(x, axis=axis)

def _gelu(x):
    return jax.nn.gelu(x, approximate=True)

def _silu(x):
    return jax.nn.silu(x)

def _sigmoid(x):
    return jax.nn.sigmoid(x)

def _layernorm(x, axis=-1, eps=1e-05):
    m = jnp.mean(x, axis=axis, keepdims=True)
    v = jnp.var(x, axis=axis, keepdims=True)
    return (x - m) / jnp.sqrt(v + eps)

def _scatter_add(tgt, idx, src, axis=0):
    return tgt.at[idx].add(src)

def _segment_sum(src, seg, n):
    return jax.ops.segment_sum(src, seg, n)
kernel_name = 'mk_gnn_preln_d4_gnn_r32_494246'

def setup_inputs(seed: int=0):
    np.random.seed(seed)
    _w = jnp.asarray

    def _rec_inputs():
        import jax
        import jax.numpy as jnp
        _gk = jax.random.key(seed)
        x = -0.0009044 + 1 * jax.random.normal(jax.random.fold_in(_gk, 1), (3125, 16), jnp.float32)
        _s = jax.random.randint(jax.random.fold_in(_gk, 2), (50000,), 0, 3125, jnp.int32)
        _d = jax.random.randint(jax.random.fold_in(_gk, 3), (50000,), 0, 3125, jnp.int32)
        _loop = jnp.arange(3125, dtype=jnp.int32)
        src = jnp.concatenate([_s, _d, _loop])
        dst = jnp.concatenate([_d, _s, _loop])
        _o = jnp.argsort(dst, stable=True)
        src = src[_o]
        dst = dst[_o]
        edge_attr_16 = -3.57403e-05 + 0.999761 * jax.random.normal(jax.random.fold_in(_gk, 12), (103125, 16), jnp.float32)
        edge_type_8 = jax.random.randint(jax.random.fold_in(_gk, 14), (103125,), 0, 8, jnp.int32)
        edge_weight = jax.random.uniform(jax.random.fold_in(_gk, 15), (103125,), jnp.float32, 0.0, 1)
        return (x, src, dst, edge_attr_16, edge_type_8, edge_weight)
    x, src, dst, edge_attr_16, edge_type_8, edge_weight = _rec_inputs()

    def _L0_gnn_setup():
        import jax, jax.numpy as jnp
        import numpy as np
        N, E, D_IN, D, D_OUT = (3125, 100000, 16, 128, 16)
        LN_EPS = 1e-05

        def _layer_norm(x, g, b):
            mu = jnp.mean(x, axis=-1, keepdims=True)
            var = jnp.mean((x - mu) ** 2, axis=-1, keepdims=True)
            return (x - mu) * jax.lax.rsqrt(var + LN_EPS) * g + b
        key = jax.random.key(seed)
        ks = jax.random.split(key, 10)
        s = lambda fan_in: 1.0 / np.sqrt(fan_in)
        return {'X': jax.random.normal(ks[0], (N, D_IN), jnp.float32), 'W_enc0': jax.random.uniform(ks[1], (D_IN, D), jnp.float32, -s(D_IN), s(D_IN)), 'b_enc0': jnp.zeros((D,), jnp.float32), 'W_enc1': jax.random.uniform(ks[2], (D, D), jnp.float32, -s(D), s(D)), 'b_enc1': jnp.zeros((D,), jnp.float32), 'W_conv': jax.random.uniform(ks[3], (D, D), jnp.float32, -s(D), s(D)), 'b_conv': jnp.zeros((D,), jnp.float32), 'ln_g': jnp.ones((D,), jnp.float32), 'ln_b': jnp.zeros((D,), jnp.float32), 'W_dec0': jax.random.uniform(ks[4], (D, D), jnp.float32, -s(D), s(D)), 'b_dec0': jnp.zeros((D,), jnp.float32), 'W_dec1': jax.random.uniform(ks[5], (D, D_OUT), jnp.float32, -s(D), s(D)), 'b_dec1': jnp.zeros((D_OUT,), jnp.float32), 'edge_index': jax.random.randint(ks[6], (2, E), 0, N, jnp.int64), 'msg_steps': 3}
    _L0_gnn_all = _L0_gnn_setup()
    _L0_gnn_in = {k: v for k, v in _L0_gnn_all.items() if k in ('W_enc0', 'b_enc0', 'W_enc1', 'b_enc1', 'W_conv', 'b_conv', 'ln_g', 'ln_b', 'W_dec0', 'b_dec0', 'W_dec1', 'b_dec1')}
    del _L0_gnn_all

    def _L1_gnn_setup():
        import jax, jax.numpy as jnp
        import numpy as np
        N_NODES = 30000
        N_EDGES = 9375
        IN_FEATS = 16
        OUT_FEATS = 16
        EDGE_DIM = 16
        key = jax.random.key(seed)
        ks = jax.random.split(key, 8)
        feat = jax.random.normal(ks[0], (N_NODES, IN_FEATS), dtype=jnp.float32)
        efeat = jax.random.normal(ks[1], (N_EDGES, EDGE_DIM), dtype=jnp.float32)
        W_msg = jax.random.normal(ks[2], (EDGE_DIM, IN_FEATS * OUT_FEATS), dtype=jnp.float32) * 0.1
        b_msg = jnp.zeros((IN_FEATS * OUT_FEATS,), dtype=jnp.float32)
        W_attn = jax.random.normal(ks[3], (EDGE_DIM, IN_FEATS * OUT_FEATS), dtype=jnp.float32) * 0.1
        b_attn = jnp.zeros((IN_FEATS * OUT_FEATS,), dtype=jnp.float32)
        src = jax.random.randint(ks[4], (N_EDGES,), 0, N_NODES, dtype=jnp.int32)
        dst = jax.random.randint(ks[5], (N_EDGES,), 0, N_NODES, dtype=jnp.int32)
        return {'feat': feat, 'efeat': efeat, 'W_msg': W_msg, 'b_msg': b_msg, 'W_attn': W_attn, 'b_attn': b_attn, 'src': src, 'dst': dst}
    _L1_gnn_all = _L1_gnn_setup()
    _L1_gnn_in = {k: v for k, v in _L1_gnn_all.items() if k in ('W_msg', 'b_msg', 'W_attn', 'b_attn')}
    del _L1_gnn_all

    def _L2_gnn_setup():
        import jax, jax.numpy as jnp
        import numpy as np
        NUM_ENTITIES = 3125
        NUM_RELATIONS = 8
        NUM_CLASSES = 16
        HIDDEN = 16
        NUM_EDGES = 100000

        def rgcn_conv(x, src, dst, edge_type, W, root, bias):
            num_nodes = x.shape[0]
            x_src = x[src]
            msg = jnp.zeros((src.shape[0], W.shape[2]), x.dtype)
            for r in range(NUM_RELATIONS):
                msg = msg + jnp.where((edge_type == r)[:, None], x_src @ W[r], jnp.zeros((), x.dtype))
            cnt = jnp.zeros((num_nodes, NUM_RELATIONS), x.dtype).at[dst, edge_type].add(1.0)
            norm = 1.0 / jnp.maximum(cnt[dst, edge_type], 1.0)
            agg = jax.ops.segment_sum(msg * norm[:, None], dst, num_segments=num_nodes)
            return agg + x @ root + bias
        key = jax.random.key(seed)
        ks = jax.random.split(key, 9)
        s = 1.0 / np.sqrt(HIDDEN)
        edge_index = jax.random.randint(ks[0], (2, NUM_EDGES), 0, NUM_ENTITIES, dtype=jnp.int32)
        edge_type = jax.random.randint(ks[1], (NUM_EDGES,), 0, NUM_RELATIONS, dtype=jnp.int32)
        return {'embed': jax.random.normal(ks[2], (NUM_ENTITIES, HIDDEN), jnp.float32), 'W1': jax.random.normal(ks[3], (NUM_RELATIONS, HIDDEN, HIDDEN), jnp.float32) * s, 'root1': jax.random.normal(ks[4], (HIDDEN, HIDDEN), jnp.float32) * s, 'b1': jnp.zeros((HIDDEN,), jnp.float32), 'W2': jax.random.normal(ks[5], (NUM_RELATIONS, HIDDEN, NUM_CLASSES), jnp.float32) * s, 'root2': jax.random.normal(ks[6], (HIDDEN, NUM_CLASSES), jnp.float32) * s, 'b2': jnp.zeros((NUM_CLASSES,), jnp.float32), 'edge_index': edge_index, 'edge_type': edge_type}
    _L2_gnn_all = _L2_gnn_setup()
    _L2_gnn_in = {k: v for k, v in _L2_gnn_all.items() if k in ('W1', 'root1', 'b1', 'W2', 'root2', 'b2')}
    del _L2_gnn_all

    def _L3_gnn_setup():
        import jax, jax.numpy as jnp
        import numpy as np
        N_NODES = 3125
        N_EDGES = 100000
        DIM = 16
        B, K, C, D, E, H = (0.1, 5.0, 1.0, 5.0, 0.9, 0.1)
        E_ = E
        key = jax.random.key(seed)
        k1, k2, k3, k4 = jax.random.split(key, 4)
        x = jax.random.uniform(k1, (N_NODES, DIM), dtype=jnp.float32)
        edge_src = jax.random.randint(k2, (N_EDGES,), 0, N_NODES, dtype=jnp.int32)
        edge_dst = jax.random.randint(k3, (N_EDGES,), 0, N_NODES, dtype=jnp.int32)
        edge_vals = jax.random.uniform(k4, (N_EDGES,), dtype=jnp.float32)
        return {'x': x, 'edge_src': edge_src, 'edge_dst': edge_dst, 'edge_vals': edge_vals}
    _L3_gnn_all = _L3_gnn_setup()
    _L3_gnn_in = {k: v for k, v in _L3_gnn_all.items() if k in ()}
    del _L3_gnn_all
    return {'x': x, 'src': src, 'dst': dst, 'edge_attr_16': edge_attr_16, 'edge_type_8': edge_type_8, 'edge_weight': edge_weight, 'L0_gnn_W_enc0': _L0_gnn_in['W_enc0'], 'L0_gnn_b_enc0': _L0_gnn_in['b_enc0'], 'L0_gnn_W_enc1': _L0_gnn_in['W_enc1'], 'L0_gnn_b_enc1': _L0_gnn_in['b_enc1'], 'L0_gnn_W_conv': _L0_gnn_in['W_conv'], 'L0_gnn_b_conv': _L0_gnn_in['b_conv'], 'L0_gnn_ln_g': _L0_gnn_in['ln_g'], 'L0_gnn_ln_b': _L0_gnn_in['ln_b'], 'L0_gnn_W_dec0': _L0_gnn_in['W_dec0'], 'L0_gnn_b_dec0': _L0_gnn_in['b_dec0'], 'L0_gnn_W_dec1': _L0_gnn_in['W_dec1'], 'L0_gnn_b_dec1': _L0_gnn_in['b_dec1'], 'L1_gnn_W_msg': _L1_gnn_in['W_msg'], 'L1_gnn_b_msg': _L1_gnn_in['b_msg'], 'L1_gnn_W_attn': _L1_gnn_in['W_attn'], 'L1_gnn_b_attn': _L1_gnn_in['b_attn'], 'L2_gnn_W1': _L2_gnn_in['W1'], 'L2_gnn_root1': _L2_gnn_in['root1'], 'L2_gnn_b1': _L2_gnn_in['b1'], 'L2_gnn_W2': _L2_gnn_in['W2'], 'L2_gnn_root2': _L2_gnn_in['root2'], 'L2_gnn_b2': _L2_gnn_in['b2']}

def reference(x, src, dst, edge_attr_16, edge_type_8, edge_weight, L0_gnn_W_enc0, L0_gnn_b_enc0, L0_gnn_W_enc1, L0_gnn_b_enc1, L0_gnn_W_conv, L0_gnn_b_conv, L0_gnn_ln_g, L0_gnn_ln_b, L0_gnn_W_dec0, L0_gnn_b_dec0, L0_gnn_W_dec1, L0_gnn_b_dec1, L1_gnn_W_msg, L1_gnn_b_msg, L1_gnn_W_attn, L1_gnn_b_attn, L2_gnn_W1, L2_gnn_root1, L2_gnn_b1, L2_gnn_W2, L2_gnn_root2, L2_gnn_b2):
    import jax
    import jax.numpy as jnp

    def _L0_gnn_ref(X, W_enc0, b_enc0, W_enc1, b_enc1, W_conv, b_conv, ln_g, ln_b, W_dec0, b_dec0, W_dec1, b_dec1, edge_index, msg_steps):
        import jax, jax.numpy as jnp
        import numpy as np
        N, E, D_IN, D, D_OUT = (3125, 100000, 16, 128, 16)
        LN_EPS = 1e-05

        def _layer_norm(x, g, b):
            mu = jnp.mean(x, axis=-1, keepdims=True)
            var = jnp.mean((x - mu) ** 2, axis=-1, keepdims=True)
            return (x - mu) * jax.lax.rsqrt(var + LN_EPS) * g + b
        n = X.shape[0]
        loops = jnp.arange(n, dtype=edge_index.dtype)
        row = jnp.concatenate([edge_index[0], loops])
        col = jnp.concatenate([edge_index[1], loops])
        deg = jax.ops.segment_sum(jnp.ones_like(col, jnp.float32), col, num_segments=n)
        dinv = jnp.where(deg > 0, jax.lax.rsqrt(deg), 0.0)
        norm = dinv[row] * dinv[col]
        x = jax.nn.relu(X @ W_enc0 + b_enc0)
        x = x @ W_enc1 + b_enc1
        for _ in range(msg_steps):
            h = x @ W_conv
            msg = h[row] * norm[:, None]
            agg = jax.ops.segment_sum(msg, col, num_segments=n) + b_conv
            x = _layer_norm(x + agg, ln_g, ln_b)
        x = jax.nn.relu(x @ W_dec0 + b_dec0)
        x = x @ W_dec1 + b_dec1
        return x

    def _L1_gnn_ref(feat, efeat, W_msg, b_msg, W_attn, b_attn, src, dst):
        import jax, jax.numpy as jnp
        import numpy as np
        N_NODES = 30000
        N_EDGES = 9375
        IN_FEATS = 16
        OUT_FEATS = 16
        EDGE_DIM = 16
        N, in_f = feat.shape
        E = efeat.shape[0]
        w_m = (efeat @ W_msg + b_msg).reshape(E, in_f, -1)
        w_a = (efeat @ W_attn + b_attn).reshape(E, in_f, -1)
        h_src = feat[src][:, :, None]
        e1 = w_m * h_src
        e2 = w_a * h_src
        seg_max = jax.ops.segment_max(e2, dst, num_segments=N)
        ex = jnp.exp(e2 - seg_max[dst])
        denom = jax.ops.segment_sum(ex, dst, num_segments=N)
        attn = ex / denom[dst]
        ft = jax.ops.segment_sum(e1 * attn, dst, num_segments=N)
        return ft.sum(axis=1)

    def _L2_gnn_ref(embed, W1, root1, b1, W2, root2, b2, edge_index, edge_type):
        import jax, jax.numpy as jnp
        import numpy as np
        NUM_ENTITIES = 3125
        NUM_RELATIONS = 8
        NUM_CLASSES = 16
        HIDDEN = 16
        NUM_EDGES = 100000

        def rgcn_conv(x, src, dst, edge_type, W, root, bias):
            num_nodes = x.shape[0]
            x_src = x[src]
            msg = jnp.zeros((src.shape[0], W.shape[2]), x.dtype)
            for r in range(NUM_RELATIONS):
                msg = msg + jnp.where((edge_type == r)[:, None], x_src @ W[r], jnp.zeros((), x.dtype))
            cnt = jnp.zeros((num_nodes, NUM_RELATIONS), x.dtype).at[dst, edge_type].add(1.0)
            norm = 1.0 / jnp.maximum(cnt[dst, edge_type], 1.0)
            agg = jax.ops.segment_sum(msg * norm[:, None], dst, num_segments=num_nodes)
            return agg + x @ root + bias
        src, dst = (edge_index[0], edge_index[1])
        h = rgcn_conv(embed, src, dst, edge_type, W1, root1, b1)
        h = jax.nn.relu(h)
        h = rgcn_conv(h, src, dst, edge_type, W2, root2, b2)
        return jax.nn.log_softmax(h, axis=1)

    def _L3_gnn_ref(x, edge_src, edge_dst, edge_vals):
        import jax, jax.numpy as jnp
        import numpy as np
        N_NODES = 3125
        N_EDGES = 100000
        DIM = 16
        B, K, C, D, E, H = (0.1, 5.0, 1.0, 5.0, 0.9, 0.1)
        E_ = E
        n = x.shape[0]
        f = B + x * (1.0 - x / K) * (x / C - 1.0)
        xi = x[edge_src]
        xj = x[edge_dst]
        msg = edge_vals[:, None] * xi * xj / (D + E_ * xi + H * xj)
        f = f + jax.ops.segment_sum(msg, edge_src, num_segments=n)
        return f
    edge_index = jnp.stack([src, dst])
    h = jnp.maximum(_layernorm(x, axis=-1), 0.0)
    x = x + _L0_gnn_ref(h, L0_gnn_W_enc0, L0_gnn_b_enc0, L0_gnn_W_enc1, L0_gnn_b_enc1, L0_gnn_W_conv, L0_gnn_b_conv, L0_gnn_ln_g, L0_gnn_ln_b, L0_gnn_W_dec0, L0_gnn_b_dec0, L0_gnn_W_dec1, L0_gnn_b_dec1, edge_index, 3)
    h = jnp.maximum(_layernorm(x, axis=-1), 0.0)
    x = x + _L1_gnn_ref(h, edge_attr_16, L1_gnn_W_msg, L1_gnn_b_msg, L1_gnn_W_attn, L1_gnn_b_attn, src, dst)
    h = jnp.maximum(_layernorm(x, axis=-1), 0.0)
    x = x + _L2_gnn_ref(h, L2_gnn_W1, L2_gnn_root1, L2_gnn_b1, L2_gnn_W2, L2_gnn_root2, L2_gnn_b2, edge_index, edge_type_8)
    h = jnp.maximum(_layernorm(x, axis=-1), 0.0)
    x = x + _L3_gnn_ref(h, src, dst, edge_weight)
    return x

_drawn_inputs = setup_inputs


def setup_inputs(seed=0):
    import zlib

    import numpy as np

    out = dict(_drawn_inputs(seed))
    spreads = {'L0_gnn_b_enc0': (0.0, 0.466),
     'L0_gnn_b_enc1': (0.0, 0.1),
     'L0_gnn_b_conv': (0.0, 0.1),
     'L0_gnn_ln_g': (1.0, 0.2),
     'L0_gnn_ln_b': (0.0, 0.1),
     'L0_gnn_b_dec0': (0.0, 0.1),
     'L0_gnn_b_dec1': (0.0, 0.1),
     'L1_gnn_b_msg': (0.0, 0.1),
     'L1_gnn_b_attn': (0.0, 0.395),
     'L2_gnn_b1': (0.0, 0.1),
     'L2_gnn_b2': (0.0, 0.284)}
    factors = {}
    for name, (base, spread) in spreads.items():
        noise = np.random.default_rng([zlib.crc32(name.encode()), seed]).standard_normal(out[name].shape)
        drawn = base * np.exp(spread * noise) if base else spread * noise
        out[name] = jnp.asarray(drawn.astype(out[name].dtype))
    for name, factor in factors.items():
        out[name] = (out[name] * factor).astype(out[name].dtype)
    return out
```

```python
from contextlib import ExitStack

import concourse.bass as bass
from concourse import mybir

ALU = mybir.AluOpType
ACT = mybir.ActivationFunctionType
AX = mybir.AxisListType
F32 = mybir.dt.float32
I32 = mybir.dt.int32

P = 128
N = 3125
E = 103125
BLOCKS = -(-N // P)
TILES = -(-E // P)
STEPS = -(-(TILES + BLOCKS - 1) // 8) * 8
ROWS = STEPS - BLOCKS + 1
SCH = -(-STEPS // P)
SPAD = SCH * P
FULL = E // P
TAIL = E - FULL * P
GRP = 4
PAIRS = STEPS // (2 * GRP)
REL = 8
CH = 16
HID = 128
ATT = CH * CH
LIT = 1
BIG = float(2.0 ** 127)
EPS = 1e-5


class Chain:

    def __init__(self, eng, sem):
        self.eng, self.sem, self.n, self.base = eng, sem, 0, None

    def value(self):
        return self.n if self.base is None else self.base + self.n

    def link(self, ins):
        ins.then_inc(self.sem, 1)
        self.n += 1
        self.eng.wait_ge(self.sem, self.value())

    def enter(self, i, per_trip):
        self.base, self.start, self.per = i * per_trip, self.n, per_trip

    def leave(self, trips):
        assert self.n - self.start == self.per, (self.n - self.start, self.per)
        self.n = self.start + self.per * trips
        self.base = None


def gnn_program(nc, x, src, dst, edge_attr_16, edge_type_8, edge_weight,
                W_enc0, b_enc0, W_enc1, b_enc1, W_conv, b_conv, ln_g, ln_b,
                W_dec0, b_dec0, W_dec1, b_dec1, W_msg, b_msg, W_attn, b_attn,
                W1, root1, b1, W2, root2, b2, out):
    with ExitStack() as ctx:
        def sb(name, shape, dt=F32):
            return ctx.enter_context(nc.sbuf_tensor(name, shape, dt))

        def sem(name):
            return ctx.enter_context(nc.semaphore(name))

        def dram(name, shape, dt=F32):
            return nc.dram_tensor(name, shape, dt).ap()

        ctx.enter_context(nc.allow_non_contiguous_dma(reason="last dst of each tile"))

        etab = dram("etab", [ROWS, 3, P], I32)
        wtab = dram("wtab", [ROWS, P])
        etab_flat = etab.rearrange("t k p -> t (k p)")
        efpad = dram("efpad", [ROWS * P, CH])
        dstflat = dram("dstflat", [SPAD * P + 2])
        startflat = dram("startflat", [SPAD, P])
        conv_tab = [dram(f"conv_tab{l}", [BLOCKS * P, HID]) for l in range(3)]
        h_tab = [dram(f"h_tab{l}", [BLOCKS * P, CH]) for l in range(4)]

        part_i = sb("part_i", [P, 1], I32)
        iota_f = sb("iota_f", [P, SPAD])
        part_f = sb("part_f", [P, 1])
        ident = sb("ident", [P, P])
        ones = sb("ones", [P, P])
        zeros = sb("zeros", [P, 400])
        padi = sb("padi", [1, 3 * P], I32)
        path = sb("path", [P, 4])
        tcol_f = sb("tcol_f", [P, SCH])
        tcol = sb("tcol", [P, SCH], I32)
        blk_row = sb("blk_row", [1, SPAD], I32)
        tile_row = sb("tile_row", [1, SPAD], I32)
        dstloc = sb("dstloc", [P, SPAD])
        inblk = sb("inblk", [P, SPAD])
        src_i = sb("src_i", [P, SPAD], I32)
        srclo = sb("srclo", [P, SPAD])
        srcblk = sb("srcblk", [P, SPAD])
        type_f = sb("type_f", [P, SPAD])
        weight = sb("weight", [P, SPAD])
        lastf = sb("lastf", [P, SPAD])
        cnt = sb("cnt", [P, BLOCKS, REL])
        invcnt = sb("invcnt", [P, BLOCKS, REL])
        dinv = sb("dinv", [P, BLOCKS])
        dtmp = sb("dtmp", [P, BLOCKS])
        stat = sb("stat", [P, 3, BLOCKS])
        xs = sb("xs", [P, BLOCKS, CH])
        hs = sb("hs", [P, BLOCKS, CH])
        ys = sb("ys", [P, BLOCKS, CH])
        zs = sb("zs", [P, BLOCKS, CH])
        big = sb("big", [P, 4 * BLOCKS * HID])
        quarter = BLOCKS * HID
        acc, state, hid, tmp = (big[:, q * quarter:(q + 1) * quarter].rearrange("p (b c) -> p b c", b=BLOCKS)
                                for q in range(4))
        att_acc = big[:, :].rearrange("p (b c) -> p b c", b=BLOCKS)
        att_max = sb("att_max", [P, BLOCKS, ATT])
        setup = att_max[:, :, :].rearrange("p b c -> p (b c)")
        iota_i = setup[:, 0:SPAD].bitcast(I32)
        past = setup[:, SPAD:2 * SPAD]
        stepblk = setup[:, 2 * SPAD:3 * SPAD]
        lastd_i = setup[0:1, 3 * SPAD:3 * SPAD + TILES].bitcast(I32)
        lastd_f = setup[0:1, 4 * SPAD:4 * SPAD + TILES]
        W = GRP * P
        hrep = big[:, 0:2 * W].rearrange("p (h e) -> p h e", h=2)
        runmax = big[:, 2 * W:4 * W].rearrange("p (h e) -> p h e", h=2)
        startrow = big[0:1, 4 * W:5 * W]
        hsT = big[0:CH, 5 * W:6 * W]
        hsrc = sb("hsrc", [P, STEPS, CH])
        stage = hsrc[:, :, :].rearrange("p s c -> p (s c)")
        st_i = stage[:, 0:3 * P * SCH].bitcast(I32).rearrange("p (c k e) -> p c k e", c=SCH, k=3)
        st_f = stage[:, 3 * P * SCH:8 * P * SCH].rearrange("p (c k e) -> p c k e", c=SCH, k=5)
        st_prev = stage[:, 8 * P * SCH:9 * P * SCH].rearrange("p (c e) -> p c e", c=SCH)
        st_next = stage[:, 9 * P * SCH:10 * P * SCH].rearrange("p (c e) -> p c e", c=SCH)
        rows_at = sb("rows_at", [P, 2, GRP], I32)
        gbuf = sb("gbuf", [P, 2, GRP, HID])
        onehot = sb("onehot", [P, 2, GRP, P])
        spread = sb("spread", [P, 2, GRP, HID])
        typeoh = sb("typeoh", [P, 2, GRP, REL])
        xT = sb("xT", [P, 5, P])
        hmask = sb("hmask", [P, GRP, CH])
        efrow = sb("efrow", [P, GRP, CH + 1])
        efT = sb("efT", [CH + 1, GRP * P])
        e2 = sb("e2", [P, 2, GRP * P])
        carry = sb("carry", [P, 2])
        maxE = spread
        wm = sb("wm", [CH + 1, 2 * ATT])
        rep = sb("rep", [CH, ATT])
        small = {}
        for name, shape in (("e0", [CH, HID]), ("e1", [HID, HID]), ("cv", [HID, HID]), ("d0", [HID, HID]),
                            ("d1", [HID, CH]), ("r1", [CH, CH]), ("r2", [CH, CH]), ("w1", [HID, CH]),
                            ("w2", [HID, CH]), ("be0", [1, HID]), ("be1", [1, HID]), ("bd0", [1, HID]),
                            ("bd1", [1, CH]), ("b1", [1, CH]), ("b2", [1, CH])):
            small[name] = sb("w_" + name, shape)
        for q, name in enumerate(("bcv", "lg", "lb")):
            small[name] = setup[:, 5 * SPAD + q * HID:5 * SPAD + (q + 1) * HID]
        ps = ctx.enter_context(nc.psum_tensor("ps", [P, 8, 512], F32))

        loaded = sem("loaded")
        iota_done = sem("iota_done")
        consts_done = sem("consts_done")
        pads_done = sem("pads_done")
        last_loaded = sem("last_loaded")
        etab_done = sem("etab_done")
        path_cmp, path_mm, path_blk, path_blk_mm, tcol_done = (sem(s) for s in (
            "path_cmp", "path_mm", "path_blk", "path_blk_mm", "tcol_done"))
        rows_got, dst_conv, dst_out, dst_back, start_made, start_out = (sem(s) for s in (
            "rows_got", "dst_conv", "dst_out", "dst_back", "start_made", "start_out"))
        idx_turned, idx_copied, idx_done = sem("idx_turned"), sem("idx_copied"), sem("idx_done")
        dense_in, dense_turned, dense_copied, dense_mul, dense_out = (sem(s) for s in (
            "dense_in", "dense_turned", "dense_copied", "dense_mul", "dense_out"))
        table_made, table_out = sem("table_made"), sem("table_out")
        acc_zero, pass_done = sem("acc_zero"), sem("pass_done")
        dve_step = sem("dve_step")
        lse_in, lse_exp, lse_sum, lse_ln = (sem(s) for s in ("lse_in", "lse_exp", "lse_sum", "lse_ln"))
        root_in, root_out = sem("root_in"), sem("root_out")
        rows_known = sem("rows_known")
        x_done, stored = sem("x_done"), sem("stored")

        passes = ["count", "conv0", "conv1", "conv2", "rel1", "rel2"]
        ps_sems = {p: {k: [sem(f"{p}_{k}{s}") for s in range(2)]
                       for k in ("oh_ready", "rhs_ready", "gathered", "mm_done", "added")} for p in passes}
        pass_chain = {p: sem(f"{p}_chain") for p in passes}
        lay_gathered = {l: [sem(f"{l}_gathered{s}") for s in range(2)] for l in ("att", "rea")}
        A = {k: sem("att_" + k) for k in (
            "feat_in", "start_in", "masked", "turned", "copied", "product", "replicated", "rep_copied",
            "e2_ready", "max_ready", "max_turned", "max_copied", "lastoh", "max_rows", "max_added", "chain",
            "b_feat_in", "b_turned", "b_copied", "b_product", "b_oh", "b_ohT", "b_ohT_copied", "b_shift",
            "b_diff", "b_exp", "b_weighted", "b_summed", "b_added", "b_chain", "zero", "swap")}
        R = {k: sem("rea_" + k) for k in ("oh", "ohT", "ohT_copied", "xj", "spread", "scattered", "chain",
                                          "all")}

        att_used = [sem(f"att_used{s}") for s in range(2)]
        rea_used = [sem(f"rea_used{s}") for s in range(2)]
        idx_raw = big[:, 0:5 * SPAD].rearrange("p (k s) -> p k s", k=5)
        rea_tmp = big[:, 2000:2000 + 2 * GRP * CH].rearrange("p (a c) -> p a c", a=2)
        blkoh = big[:, 1600:1600 + GRP * BLOCKS].rearrange("p (k b) -> p k b", k=GRP)
        rea_spread = big[:, 0:GRP * BLOCKS * CH].rearrange("p (k c) -> p k c", k=GRP)

        def spread_rea(k):
            return rea_spread[:, k, :]

        def gbuf_ohs(s):
            return spread[:, s, :, :]

        def gbuf_oh(s, k):
            return spread[:, s, k, :]

        N_ETAB = 2 * 3 + 2 + 2 + 3 * (1 + ROWS - TILES) + 1 + ROWS - TILES + -(-(ROWS * P - E) // P)
        N_LOADS = 2 + 9 + 6 + 3 + 4

        block = ctx.enter_context(nc.Block())

        NODES_FULL = N // P * P
        iota_row = iota_f[:, 0:P]

        def block_of(eng, step):
            return eng.value_load(blk_row[0:1, bass.ds(step, 1)], min_val=0, max_val=BLOCKS - 1)

        def write_table(eng, table, nodes, nth):
            eng.wait_ge(table_made, nth)
            eng.dma_start(table.rearrange("(b p) c -> p b c", p=P), nodes).then_inc(table_out, 16)

        lit = [q for S in ps_sems.values() for k in ("oh_ready", "rhs_ready", "mm_done", "added") for q in S[k]]
        lit += [q for k, q in A.items() if k not in ("feat_in", "start_in", "b_feat_in", "chain", "b_chain")]
        lit += [q for k, q in R.items() if k not in ("chain", "all")]
        lit += att_used + rea_used

        @block.sync
        def _(sp):
            for q in lit:
                sp.sem_inc(q, LIT)
            sp.dma_start(lastd_i[0:1, 0:FULL], dst[0:FULL * P].rearrange("(a t p) -> a t p", a=1, p=P)[:, :, P - 1]) \
              .then_inc(last_loaded, 16)
            sp.dma_start(lastd_i[0:1, FULL:TILES], dst[E - 1:E].rearrange("(a t) -> a t", a=1)) \
              .then_inc(last_loaded, 16)
            for k, flat in enumerate((src, dst, edge_type_8)):
                sp.dma_start(etab[0:FULL, k, :], flat[0:FULL * P].rearrange("(t p) -> t p", p=P)).then_inc(etab_done, 16)
                sp.dma_start(etab[FULL:TILES, k, 0:TAIL], flat[FULL * P:E].rearrange("(t p) -> t p", t=1)) \
                  .then_inc(etab_done, 16)
            sp.dma_start(wtab[0:FULL, :], edge_weight[0:FULL * P].rearrange("(t p) -> t p", p=P)).then_inc(etab_done, 16)
            sp.dma_start(wtab[FULL:TILES, 0:TAIL], edge_weight[FULL * P:E].rearrange("(t p) -> t p", t=1)) \
              .then_inc(etab_done, 16)
            sp.dma_start(efpad[0:FULL * P, :], edge_attr_16[0:FULL * P, :]).then_inc(etab_done, 16)
            sp.dma_start(efpad[FULL * P:E, :], edge_attr_16[FULL * P:E, :]).then_inc(etab_done, 16)
            sp.wait_ge(pads_done, 1)
            for k in range(3):
                pad = padi[0:1, k * P:(k + 1) * P]
                sp.dma_start(etab[FULL:TILES, k, TAIL:P], pad[:, 0:P - TAIL]).then_inc(etab_done, 16)
                for r in range(TILES, ROWS):
                    sp.dma_start(etab[r:r + 1, k, :], pad).then_inc(etab_done, 16)
            sp.dma_start(wtab[FULL:TILES, TAIL:P], zeros[0:1, 0:P - TAIL]).then_inc(etab_done, 16)
            for r in range(TILES, ROWS):
                sp.dma_start(wtab[r:r + 1, :], zeros[0:1, 0:P]).then_inc(etab_done, 16)
            at = E
            while at < ROWS * P:
                n = min(P, ROWS * P - at)
                sp.dma_start(efpad[at:at + n, :], zeros[0:n, 0:CH]).then_inc(etab_done, 16)
                at += n
            sp.dma_start(xs[:, 0:BLOCKS - 1, :], x[0:NODES_FULL, :].rearrange("(b p) c -> p b c", p=P)).then_inc(loaded, 16)
            sp.wait_ge(consts_done, 1)
            sp.dma_start(xs[0:N - NODES_FULL, BLOCKS - 1, :], x[NODES_FULL:N, :]).then_inc(loaded, 16)
            for name, w in (("e0", W_enc0), ("e1", W_enc1), ("cv", W_conv), ("d0", W_dec0), ("d1", W_dec1),
                            ("r1", root1), ("r2", root2), ("w1", W1.rearrange("r c o -> (r c) o")),
                            ("w2", W2.rearrange("r c o -> (r c) o"))):
                sp.dma_start(small[name][:, :], w).then_inc(loaded, 16)
            for name, b in (("be0", b_enc0), ("be1", b_enc1), ("bd0", b_dec0), ("bd1", b_dec1), ("b1", b1), ("b2", b2)):
                sp.dma_start(small[name][:, :], b.rearrange("(a c) -> a c", a=1)).then_inc(loaded, 16)
            for name, b in (("bcv", b_conv), ("lg", ln_g), ("lb", ln_b)):
                sp.dma_start(small[name][:, :], b.rearrange("(a c) -> a c", a=1).to_broadcast([P, HID])) \
                  .then_inc(loaded, 16)
            for q, (w, b) in enumerate(((W_attn, b_attn), (W_msg, b_msg))):
                sp.dma_start(wm[0:CH, q * ATT:(q + 1) * ATT], w).then_inc(loaded, 16)
                sp.dma_start(wm[CH:CH + 1, q * ATT:(q + 1) * ATT], b.rearrange("(a c) -> a c", a=1)).then_inc(loaded, 16)
            sp.wait_ge(dst_conv, 1)
            sp.dma_start(dstflat[1:SPAD * P + 1].rearrange("(c s e) -> s c e", s=P, e=P), st_f[:, :, 1, :]) \
              .then_inc(dst_out, 16)
            sp.dma_start(dstflat[0:1].rearrange("(a c) -> a c", a=1), path[0:1, 3:4]).then_inc(dst_out, 16)
            sp.dma_start(dstflat[SPAD * P + 1:SPAD * P + 2].rearrange("(a c) -> a c", a=1), path[0:1, 3:4]) \
              .then_inc(dst_out, 16)
            sp.wait_ge(dst_out, 48)
            sp.dma_start(st_prev, dstflat[0:SPAD * P].rearrange("(c s e) -> s c e", s=P, e=P)).then_inc(dst_back, 16)
            sp.dma_start(st_next, dstflat[2:SPAD * P + 2].rearrange("(c s e) -> s c e", s=P, e=P)).then_inc(dst_back, 16)
            sp.wait_ge(start_made, 1)
            sp.dma_start(startflat.rearrange("(c s) e -> s c e", s=P), st_prev).then_inc(start_out, 16)
            for l in range(3):
                write_table(sp, conv_tab[l], hid, l + 1)
            write_table(sp, h_tab[0], hs[:, :, :], 4)
            sp.wait_ge(start_out, 16)
            with sp.Fori(0, STEPS // GRP) as g:
                sp.wait_ge(A["turned"], g + LIT)
                for k in range(GRP):
                    t = sp.value_load(tile_row[0:1, bass.ds(g * GRP + k, 1)], min_val=0, max_val=ROWS - 1)
                    sp.dma_start(efrow[:, k, 0:CH], efpad[bass.ds(t * P, P), :]).then_inc(A["feat_in"], 16)
                sp.wait_ge(A["max_ready"], g + LIT)
                sp.dma_start(startrow[:, :], startflat[bass.ds(g * GRP, GRP), :].rearrange("(a s) e -> a (s e)", a=1)) \
                  .then_inc(A["start_in"], 16)
            sp.wait_ge(A["feat_in"], 16 * STEPS)
            sp.wait_ge(A["turned"], STEPS // GRP + LIT)
            with sp.Fori(0, STEPS // GRP) as g:
                sp.wait_ge(A["b_turned"], g + LIT)
                for k in range(GRP):
                    t = sp.value_load(tile_row[0:1, bass.ds(g * GRP + k, 1)], min_val=0, max_val=ROWS - 1)
                    sp.dma_start(efrow[:, k, 0:CH], efpad[bass.ds(t * P, P), :]).then_inc(A["b_feat_in"], 16)
            for l in range(1, 4):
                write_table(sp, h_tab[l], hs[:, :, :], 4 + l)
            sp.wait_ge(x_done, 1)
            sp.dma_start(out[0:NODES_FULL, :].rearrange("(b p) c -> p b c", p=P), xs[:, 0:BLOCKS - 1, :]).then_inc(stored, 16)
            sp.dma_start(out[NODES_FULL:N, :], xs[0:N - NODES_FULL, BLOCKS - 1, :]).then_inc(stored, 16)
            sp.wait_ge(stored, 32)
            sp.wait_ge(etab_done, 16 * N_ETAB)
            sp.wait_ge(start_out, 16)
            sp.wait_ge(table_out, 16 * 7)

        @block.gpsimd
        def _(pool):
            nc.gpsimd.iota(iota_i[:, :], [[1, SPAD]], base=0, channel_multiplier=0).then_inc(iota_done, 1)
            nc.gpsimd.iota(part_i[:, :], [[0, 1]], base=0, channel_multiplier=1).then_inc(iota_done, 1)
            pool.wait_ge(tcol_done, 1)
            pool.wait_ge(etab_done, 16 * N_ETAB)
            for c in range(SCH):
                at = bass.IndirectOffsetOnAxis(tcol[:, c:c + 1], axis=0)
                nc.gpsimd.indirect_dma_start(st_i[:, c, :, :].rearrange("p k e -> p (k e)"), None, etab_flat, at) \
                    .then_inc(rows_got, 16)
                nc.gpsimd.indirect_dma_start(st_f[:, c, 3, :], None, wtab, at).then_inc(rows_got, 16)
            pool.wait_ge(idx_done, 1)

            known = [0]

            def gather_rows(table, gathered, used, width):
                with pool.Fori(0, PAIRS) as j:
                    for s in range(2):
                        pool.wait_ge(used[s], j + LIT)
                        nc.gpsimd.tensor_copy(rows_at[:, s, :], src_i[:, bass.ds(j * (2 * GRP) + s * GRP, GRP)]) \
                            .then_inc(rows_known, 1)
                        pool.wait_ge(rows_known, known[0] + j * 2 + (s + 1))
                        pool.nop(nofuse=True)
                        for k in range(GRP):
                            nc.gpsimd.indirect_dma_start(
                                gbuf[:, s, k, 0:width], None, table,
                                bass.IndirectOffsetOnAxis(rows_at[:, s, k:k + 1], axis=0)).then_inc(gathered[s], 16)
                known[0] += 2 * PAIRS

            for l in range(3):
                pool.wait_ge(table_out, 16 * (l + 1))
                S = ps_sems[f"conv{l}"]
                gather_rows(conv_tab[l], S["gathered"], S["mm_done"], HID)
            pool.wait_ge(table_out, 16 * 4)
            gather_rows(h_tab[0], lay_gathered["att"], att_used, CH)
            for l in range(2):
                pool.wait_ge(table_out, 16 * (5 + l))
                S = ps_sems[f"rel{l + 1}"]
                gather_rows(h_tab[1 + l], S["gathered"], S["rhs_ready"], CH)
            pool.wait_ge(table_out, 16 * 7)
            gather_rows(h_tab[3], lay_gathered["rea"], rea_used, CH)

        @block.tensor
        def _(pe):
            pe.wait_ge(consts_done, 1)
            pe.wait_ge(path_cmp, 1)
            half = TILES // 2
            for q in range(2):
                mm = pe.matmul(ps[0:BLOCKS - 1, q, 0:half], ones[0:1, 0:BLOCKS - 1],
                               lastd_f[0:1, q * half:(q + 1) * half], start=True, stop=True)
            mm.then_inc(path_mm, 1)
            pe.wait_ge(path_cmp, 2)
            half = SPAD // 2
            for q in range(2):
                pe.matmul(ps[:, 2 + q, 0:half], ones[0:BLOCKS - 1, :], past[0:BLOCKS - 1, q * half:(q + 1) * half],
                          start=True, stop=True)
            for c in range(SCH):
                mm = pe.matmul(ps[:, 4, c:c + 1], past[0:BLOCKS - 1, c * P:(c + 1) * P], ones[0:BLOCKS - 1, 0:1],
                               start=True, stop=True)
            mm.then_inc(path_blk_mm, 1)
            pe.wait_ge(start_made, 1)
            for c in range(SCH):
                if c >= 2:
                    pe.wait_ge(idx_copied, c - 1)
                for k in range(5):
                    mm = pe.transpose(ps[:, 2 * (c % 2) + k // 4, (k % 4) * P:(k % 4 + 1) * P], st_f[:, c, k, :], ident[:, :])
                mm.then_inc(idx_turned, 1)
            pe.wait_ge(idx_copied, SCH)

            dense_count = [0]

            def dense(xin, K, w, bias, C, ready):
                n = dense_count[0]
                dense_count[0] += 1
                pe.wait_ge(*ready)
                for g in range(5):
                    if n or g:
                        pe.wait_ge(dense_copied, 5 * n + g)
                    for k in range(5):
                        mm = pe.transpose(ps[0:K, k // 4, (k % 4) * P:(k % 4 + 1) * P], xin[:, 5 * g + k, :], ident[:, :])
                    mm.then_inc(dense_turned, 1)
                    pe.wait_ge(dense_copied, 5 * n + g + 1)
                    if n or g:
                        pe.wait_ge(dense_out, 5 * n + g)
                    for k in range(5):
                        o = ps[:, 2 + k // 4, (k % 4) * C:(k % 4 + 1) * C]
                        mm = pe.matmul(o, xT[0:K, k, :], w, start=True, stop=bias is None)
                        if bias is not None:
                            mm = pe.matmul(o, ones[0:1, :], bias, start=False, stop=True)
                    mm.then_inc(dense_mul, 1)

            def seg_pass(name, rhs, C, ready):
                S = ps_sems[name]
                with pe.Fori(0, PAIRS) as j:
                    for s in range(2):
                        pe.wait_ge(S["oh_ready"][s], j + 1 + LIT)
                        if ready == "gathered":
                            pe.wait_ge(S["gathered"][s], (j + 1) * (16 * GRP))
                        else:
                            pe.wait_ge(S["rhs_ready"][s], j + 1 + LIT)
                        pe.wait_ge(S["added"][s], j + LIT)
                        for k in range(GRP):
                            mm = pe.matmul(ps[:, 4 + s, k * C:(k + 1) * C], onehot[:, s, k, :], rhs(s, k),
                                           start=True, stop=True)
                        mm.then_inc(S["mm_done"][s], 1)

            pe.wait_ge(idx_done, 1)
            seg_pass("count", lambda s, k: typeoh[:, s, k, :], REL, "rhs_ready")
            pe.wait_ge(loaded, 16 * N_LOADS)
            dense(hs, CH, small["e0"][:, :], small["be0"][:, :], HID, (dense_in, 1))
            dense(hid, HID, small["e1"][:, :], small["be1"][:, :], HID, (dense_out, 5))
            for l in range(3):
                dense(state, HID, small["cv"][:, :], None, HID, (dense_in, 1 + l) if l else (dense_out, 10))
                seg_pass(f"conv{l}", lambda s, k: gbuf[:, s, k, :], HID, "gathered")
            dense(state, HID, small["d0"][:, :], small["bd0"][:, :], HID, (dense_in, 4))
            dense(hid, HID, small["d1"][:, :], small["bd1"][:, :], CH, (dense_out, 5 * 6))

            pe.wait_ge(dense_out, 5 * dense_count[0])
            with pe.Fori(0, STEPS // GRP) as g:
                pe.wait_ge(A["feat_in"], (g + 1) * (16 * GRP))
                pe.wait_ge(A["masked"], g + 1 + LIT)
                pe.wait_ge(A["copied"], g + LIT)
                for k in range(GRP):
                    pe.transpose(ps[0:CH + 1, 0, k * P:(k + 1) * P], efrow[:, k, :], ident[:, :])
                for k in range(GRP):
                    mm = pe.transpose(ps[0:CH, 1, k * P:(k + 1) * P],
                                      hmask[:, k, :], ident[:, :])
                mm.then_inc(A["turned"], 1)
                pe.wait_ge(A["copied"], g + 1 + LIT)
                pe.wait_ge(A["max_copied"], g + LIT)
                pe.wait_ge(A["max_added"], g + LIT)
                pe.wait_ge(A["start_in"], (g + 1) * 16)
                for h in range(2):
                    pe.matmul(ps[:, 4 + h, :], rep[:, h * P:(h + 1) * P], hsT[:, :], start=True, stop=True)
                pe.matmul(ps[:, 6, :], ones[0:1, :], startrow[:, :], start=True, stop=True)
                for h in range(2):
                    mm = pe.matmul(ps[:, 2 + h, :], wm[:, h * P:(h + 1) * P], efT[:, :], start=True, stop=True)
                mm.then_inc(A["product"], 1)
                pe.wait_ge(A["max_ready"], g + 1 + LIT)
                for k in range(GRP):
                    for h in range(2):
                        mm = pe.transpose(ps[:, 2 + k // 2, (k % 2) * ATT + h * P:(k % 2) * ATT + (h + 1) * P],
                                          runmax[:, h, k * P:(k + 1) * P], ident[:, :])
                mm.then_inc(A["max_turned"], 1)
                pe.wait_ge(A["max_copied"], g + 1 + LIT)
                pe.wait_ge(A["lastoh"], g + 1 + LIT)
                for k in range(GRP):
                    mm = pe.matmul(ps[:, 4 + k // 2, (k % 2) * ATT:(k % 2 + 1) * ATT], onehot[:, 0, k, :],
                                   maxE[:, k // 2, 2 * (k % 2):2 * (k % 2) + 2, :].rearrange("p a c -> p (a c)"),
                                   start=True, stop=True)
                mm.then_inc(A["max_rows"], 1)

            pe.wait_ge(A["max_added"], STEPS // GRP + LIT)
            with pe.Fori(0, STEPS // GRP) as g:
                pe.wait_ge(A["b_feat_in"], (g + 1) * (16 * GRP))
                pe.wait_ge(A["b_copied"], g + LIT)
                for k in range(GRP):
                    mm = pe.transpose(ps[0:CH + 1, 0, k * P:(k + 1) * P], efrow[:, k, :], ident[:, :])
                mm.then_inc(A["b_turned"], 1)
                pe.wait_ge(A["b_oh"], g + 1 + LIT)
                pe.wait_ge(A["b_ohT_copied"], g + LIT)
                for k in range(GRP):
                    mm = pe.transpose(ps[:, 1, k * P:(k + 1) * P], onehot[:, 0, k, :], ident[:, :])
                mm.then_inc(A["b_ohT"], 1)
                pe.wait_ge(A["b_copied"], g + 1 + LIT)
                pe.wait_ge(A["b_ohT_copied"], g + 1 + LIT)

                def sums(k):
                    pe.wait_ge(A["b_weighted"], g * GRP + (k + 1) + LIT)
                    if k >= 2:
                        pe.wait_ge(A["b_added"], g * GRP + (k - 1) + LIT)
                    else:
                        pe.wait_ge(A["b_added"], g * GRP + LIT)
                    pe.matmul(ps[:, 6 + k % 2, :], onehot[:, 0, k, :],
                              spread[:, k % 2, :, :].rearrange("p a c -> p (a c)"),
                              start=True, stop=True).then_inc(A["b_summed"], 1)

                for k in range(GRP):
                    if k >= 2:
                        pe.wait_ge(A["b_diff"], g * GRP + (k - 1) + LIT)
                    b = block_of(pe, g * GRP + k)
                    pe.matmul(ps[:, 2 + k % 2, :], efT[:, k * P:(k + 1) * P], wm[:, :], start=True, stop=True) \
                      .then_inc(A["b_product"], 1)
                    pe.matmul(ps[:, 4 + k % 2, 0:ATT], xT[:, k, :],
                              att_max[:, bass.ds(b, 1), :].rearrange("p a c -> p (a c)"),
                              start=True, stop=True).then_inc(A["b_shift"], 1)
                    if k >= 1:
                        sums(k - 1)
                sums(GRP - 1)

            pe.wait_ge(A["b_added"], STEPS + LIT)
            for l in range(2):
                seg_pass(f"rel{l + 1}", lambda s, k: spread[:, s, k, :], HID, "rhs_ready")
                dense(hid, HID, small[f"w{l + 1}"][:, :], small[f"b{l + 1}"][:, :], CH, (dense_in, 5 + l))
                dense(hs, CH, small[f"r{l + 1}"][:, :], None, CH, (table_made, 5 + l))

            pe.wait_ge(dense_out, 5 * dense_count[0])
            pe.matmul(ps[:, 6, 0:BLOCKS * CH], zeros[:, 0:P], zeros[:, 0:BLOCKS * CH], start=True, stop=False,
                      skip_group_check=True)
            with pe.Fori(0, PAIRS) as j:
                for s in range(2):
                    pe.wait_ge(R["oh"], j * 2 + (s + 1) + LIT)
                    pe.wait_ge(R["ohT_copied"], j * 2 + s + LIT)
                    for k in range(GRP):
                        mm = pe.transpose(ps[:, 1, k * P:(k + 1) * P], onehot[:, s, k, :], ident[:, :])
                    mm.then_inc(R["ohT"], 1)
                    pe.wait_ge(R["ohT_copied"], j * 2 + (s + 1) + LIT)
                    for k in range(GRP):
                        b = block_of(pe, j * (2 * GRP) + s * GRP + k)
                        mm = pe.matmul(ps[:, 2, k * CH:(k + 1) * CH], xT[:, k, :],
                                       hs[:, bass.ds(b, 1), :].rearrange("p a c -> p (a c)"), start=True, stop=True)
                    mm.then_inc(R["xj"], 1)
                    for k in range(GRP):
                        pe.wait_ge(R["spread"], (j * 2 + s) * GRP + (k + 1) + LIT)
                        pe.matmul(ps[:, 6, 0:BLOCKS * CH], gbuf_oh(s, k), spread_rea(k), start=False, stop=False,
                                  skip_group_check=True).then_inc(R["scattered"], 1)
            pe.matmul(ps[:, 6, 0:BLOCKS * CH], zeros[:, 0:P], zeros[:, 0:BLOCKS * CH], start=False, stop=True,
                      skip_group_check=True).then_inc(R["all"], 1)

        @block.scalar
        def _(act):
            for c in range(SCH):
                act.wait_ge(idx_turned, c + 1)
                nc.scalar.copy(idx_raw[:, 0:4, c * P:(c + 1) * P],
                               ps[:, 2 * (c % 2), :].rearrange("p (k e) -> p k e", k=4))
                nc.scalar.copy(idx_raw[:, 4, c * P:(c + 1) * P], ps[:, 2 * (c % 2) + 1, 0:P]).then_inc(idx_copied, 1)

            dense_count = [0]

            def dense(K, C, func, dest):
                n = dense_count[0]
                dense_count[0] += 1
                for g in range(5):
                    act.wait_ge(dense_turned, 5 * n + g + 1)
                    if n or g:
                        act.wait_ge(dense_mul, 5 * n + g)
                    nc.scalar.copy(xT[0:K, 0:4, :], ps[0:K, 0, :].rearrange("p (k e) -> p k e", k=4))
                    nc.scalar.copy(xT[0:K, 4, :], ps[0:K, 1, 0:P]).then_inc(dense_copied, 1)
                    act.wait_ge(dense_mul, 5 * n + g + 1)
                    nc.scalar.activation(dest[:, 5 * g:5 * g + 4, :],
                                         ps[:, 2, 0:4 * C].rearrange("p (k c) -> p k c", k=4), func)
                    nc.scalar.activation(dest[:, 5 * g + 4, :], ps[:, 3, 0:C], func).then_inc(dense_out, 1)

            roots = [0]

            def root():
                roots[0] += 1
                act.wait_ge(root_in, roots[0])
                nc.scalar.activation(stat[:, 1, :], stat[:, 1, :], ACT.Sqrt).then_inc(root_out, 1)

            root()
            root()
            dense(CH, HID, ACT.Relu, hid)
            dense(HID, HID, ACT.Copy, state)
            for l in range(3):
                dense(HID, HID, ACT.Copy, hid)
                root()
            dense(HID, HID, ACT.Relu, hid)
            dense(HID, CH, ACT.Copy, ys)
            root()

            with act.Fori(0, STEPS // GRP) as g:
                act.wait_ge(A["turned"], g + 1 + LIT)
                act.wait_ge(A["product"], g + LIT)
                nc.scalar.copy(efT[:, :], ps[0:CH + 1, 0, :])
                nc.scalar.copy(hsT[:, :], ps[0:CH, 1, :]).then_inc(A["copied"], 1)
                act.wait_ge(A["product"], g + 1 + LIT)
                act.wait_ge(A["e2_ready"], g + LIT)
                for h in range(2):
                    ins = nc.scalar.copy(hrep[:, h, :], ps[:, 4 + h, :])
                ins.then_inc(A["rep_copied"], 1)
                act.wait_ge(A["max_turned"], g + 1 + LIT)
                act.wait_ge(A["max_rows"], g + LIT)
                for q in range(2):
                    ins = nc.scalar.copy(maxE[:, q, :, :].rearrange("p a c -> p (a c)"), ps[:, 2 + q, :])
                ins.then_inc(A["max_copied"], 1)

            with act.Fori(0, STEPS // GRP) as g:
                act.wait_ge(A["b_turned"], g + 1 + LIT)
                act.wait_ge(A["b_shift"], g * GRP + LIT)
                nc.scalar.copy(efT[:, :], ps[0:CH + 1, 0, :]).then_inc(A["b_copied"], 1)
                act.wait_ge(A["b_ohT"], g + 1 + LIT)
                nc.scalar.copy(xT[:, 0:GRP, :].rearrange("p k e -> p (k e)"), ps[:, 1, :]).then_inc(A["b_ohT_copied"], 1)
                for k in range(GRP):
                    act.wait_ge(A["b_diff"], g * GRP + (k + 1) + LIT)
                    if k >= 2:
                        act.wait_ge(A["b_summed"], g * GRP + (k - 1) + LIT)
                    else:
                        act.wait_ge(A["b_summed"], g * GRP + LIT)
                    nc.scalar.activation(spread[:, k % 2, 0:2, :], e2[:, k % 2, 0:ATT].rearrange("p (a c) -> p a c", a=2),
                                         ACT.Exp).then_inc(A["b_exp"], 1)

            root()
            for l in range(2):
                dense(HID, CH, ACT.Copy, ys)
                dense(CH, CH, ACT.Copy, zs)
            act.wait_ge(lse_in, 1)
            nc.scalar.activation(zs[:, :, :], ys[:, :, :], ACT.Exp).then_inc(lse_exp, 1)
            act.wait_ge(lse_sum, 1)
            nc.scalar.activation(stat[:, 2, :], stat[:, 1, :], ACT.Ln).then_inc(lse_ln, 1)
            root()

            with act.Fori(0, PAIRS * 2) as g:
                act.wait_ge(R["ohT"], g + 1 + LIT)
                act.wait_ge(R["xj"], g + LIT)
                nc.scalar.copy(xT[:, 0:GRP, :].rearrange("p k e -> p (k e)"), ps[:, 1, :]).then_inc(R["ohT_copied"], 1)

        @block.vector
        def _(dve):
            v = nc.vector
            ch = Chain(dve, dve_step)

            def bc(ap, shape):
                return ap.to_broadcast(shape)

            v.memset(ones[:, :], 1.0)
            v.memset(zeros[:, :], 0.0)
            v.memset(padi[:, :], 0)
            ch.link(v.memset(xs[:, BLOCKS - 1, :], 0.0))
            v.memset(padi[0:1, P:2 * P], -1).then_inc(pads_done, 1)
            v.memset(path[:, 3:4], -2.0)
            ch.link(v.memset(efrow[:, :, :], 1.0))
            dve.wait_ge(iota_done, 2)
            v.tensor_copy(iota_f[:, :], iota_i[:, :])
            ch.link(v.tensor_copy(part_f[:, :], part_i[:, :]))
            v.tensor_scalar(ident[:, :], iota_row, part_f[:, 0:1], None, ALU.is_equal)
            v.tensor_scalar(rep[:, :].rearrange("p (i o) -> p i o", i=CH),
                            bc(iota_f[0:CH, 0:CH].unsqueeze(2), [CH, CH, CH]),
                            part_f[0:CH, 0:1], None, ALU.is_equal)
            v.tensor_scalar(path[:, 0:1], part_f[:, :], 1.0, float(P), ALU.add, ALU.mult).then_inc(consts_done, 1)
            dve.wait_ge(last_loaded, 32)
            v.tensor_copy(lastd_f[:, :], lastd_i[:, :]).then_inc(path_cmp, 1)
            dve.wait_ge(consts_done, 1)
            dve.wait_ge(path_mm, 1)
            half = TILES // 2
            for q in range(2):
                ins = v.tensor_scalar(stepblk[0:BLOCKS - 1, q * half:(q + 1) * half], ps[0:BLOCKS - 1, q, 0:half],
                                      path[0:BLOCKS - 1, 0:1], None, ALU.is_lt)
            ch.link(ins)
            ch.link(v.tensor_reduce(dtmp[0:BLOCKS - 1, 0:1], stepblk[0:BLOCKS - 1, 0:TILES], AX.X, ALU.add))
            ch.link(v.tensor_tensor(path[0:BLOCKS - 1, 2:3], dtmp[0:BLOCKS - 1, 0:1], part_f[0:BLOCKS - 1, :], ALU.add))
            ins = v.tensor_scalar(past[0:BLOCKS - 1, :], iota_f[0:BLOCKS - 1, :], path[0:BLOCKS - 1, 2:3], None, ALU.is_gt)
            ins.then_inc(path_cmp, 1)
            dve.wait_ge(path_blk_mm, 1)
            half = SPAD // 2
            for q in range(2):
                ins = v.tensor_copy(stepblk[:, q * half:(q + 1) * half], ps[:, 2 + q, 0:half])
            ch.link(v.tensor_scalar(tcol_f[:, :], iota_f[:, 0:SPAD:P], part_f[:, 0:1], None, ALU.add))
            ch.link(v.tensor_tensor(tcol_f[:, :], tcol_f[:, :], ps[:, 4, 0:SCH], ALU.subtract))
            ch.link(v.tensor_scalar(tcol_f[:, :], tcol_f[:, :], float(ROWS - 1), None, ALU.min))
            v.tensor_copy(tcol[:, :], tcol_f[:, :]).then_inc(tcol_done, 1)
            v.tensor_copy(blk_row[:, :], stepblk[0:1, :])
            ch.link(v.tensor_tensor(past[0:1, :], iota_f[0:1, :], stepblk[0:1, :], ALU.subtract))
            ch.link(v.tensor_copy(tile_row[:, :], past[0:1, :]))
            dve.wait_ge(rows_got, 16 * 2 * SCH)
            v.tensor_copy(st_f[:, :, 0:3, :], st_i).then_inc(dst_conv, 1)
            dve.wait_ge(dst_back, 32)
            dve.wait_ge(dst_conv, 1)
            ch.link(v.tensor_tensor(st_f[:, :, 4, :], st_f[:, :, 1, :], st_next, ALU.not_equal))
            ch.link(v.tensor_tensor(st_prev, st_f[:, :, 1, :], st_prev, ALU.not_equal))
            v.tensor_scalar(st_prev, st_prev, -BIG, None, ALU.mult).then_inc(start_made, 1)
            dve.wait_ge(idx_copied, SCH)
            ch.link(v.scalar_tensor_tensor(dstloc[:, :], stepblk[:, :], -float(P), idx_raw[:, 1, :], ALU.mult, ALU.add))
            ch.link(v.tensor_scalar(past[:, :], dstloc[:, :], 0.0, None, ALU.is_ge))
            ch.link(v.scalar_tensor_tensor(inblk[:, :], dstloc[:, :], float(P), past[:, :], ALU.is_lt, ALU.mult))
            ch.link(v.tensor_copy(src_i[:, :], idx_raw[:, 0, :]))
            v.tensor_copy(type_f[:, :], idx_raw[:, 2, :])
            v.tensor_tensor(weight[:, :], idx_raw[:, 3, :], inblk[:, :], ALU.mult)
            v.tensor_copy(lastf[:, :], idx_raw[:, 4, :])
            ch.link(v.tensor_single_scalar(iota_i[:, :], src_i[:, :], 7, ALU.arith_shift_right))
            ch.link(v.tensor_copy(srcblk[:, :], iota_i[:, :]))
            ch.link(v.scalar_tensor_tensor(srclo[:, :], srcblk[:, :], -float(P), idx_raw[:, 0, :], ALU.mult, ALU.add))
            v.memset(cnt[:, :, :], 0.0).then_inc(idx_done, 1)
            dve.wait_ge(idx_done, 1)

            def make_onehot(s, step):
                return v.tensor_tensor(onehot[:, s, :, :], bc(iota_row.unsqueeze(1), [P, GRP, P]),
                                       bc(dstloc[:, bass.ds(step, GRP)].unsqueeze(2), [P, GRP, P]), ALU.is_equal)

            def add_rows(chain, added, turn, k, row, sums):
                ins = v.tensor_tensor(row, row, sums, ALU.add)
                if k < GRP - 1:
                    chain.link(ins)
                else:
                    ins.then_inc(added, 1)
                    dve.wait_ge(added, turn + 1 + LIT)

            def count_pass():
                S, c2 = ps_sems["count"], Chain(dve, pass_chain["count"])
                with dve.Fori(0, PAIRS) as j:
                    c2.enter(j, 2 * (GRP - 1))
                    for s in range(2):
                        first = j * (2 * GRP) + s * GRP
                        dve.wait_ge(S["mm_done"][s], j + LIT)
                        make_onehot(s, first).then_inc(S["oh_ready"][s], 1)
                        v.tensor_tensor(typeoh[:, s, :, :], bc(iota_f[:, 0:REL].unsqueeze(1), [P, GRP, REL]),
                                        bc(type_f[:, bass.ds(first, GRP)].unsqueeze(2), [P, GRP, REL]),
                                        ALU.is_equal).then_inc(S["rhs_ready"][s], 1)
                    for s in range(2):
                        dve.wait_ge(S["mm_done"][s], j + 1 + LIT)
                        for k in range(GRP):
                            b = block_of(dve, j * (2 * GRP) + s * GRP + k)
                            row = cnt[:, bass.ds(b, 1), :].rearrange("p a c -> p (a c)")
                            add_rows(c2, S["added"][s], j, k, row, ps[:, 4 + s, k * REL:(k + 1) * REL])
                c2.leave(PAIRS)

            roots = [0]

            def inverse_root(to):
                roots[0] += 1
                dve.wait_ge(root_out, roots[0])
                ch.link(v.reciprocal(to, stat[:, 1, :]))

            count_pass()
            ch.link(v.tensor_reduce(dtmp[:, :], cnt[:, :, :], AX.X, ALU.add))
            v.tensor_scalar(stat[:, 1, :], dtmp[:, :], 1.0, None, ALU.add).then_inc(root_in, 1)
            inverse_root(dinv[:, :])
            ch.link(v.tensor_scalar(invcnt[:, :, :], cnt[:, :, :], 1.0, None, ALU.max))
            ch.link(v.reciprocal(invcnt[:, :, :], invcnt[:, :, :]))
            dve.wait_ge(loaded, 16 * N_LOADS)

            def per_node(ap, C):
                return bc(ap.unsqueeze(2), [P, BLOCKS, C])

            def layer_norm(xin, xc, C):
                sq = tmp[:, :, 0:C] if C == HID else zs[:, :, :]
                ch.link(v.tensor_reduce(stat[:, 0, :], xin, AX.X, ALU.add))
                ch.link(v.tensor_scalar(stat[:, 0, :], stat[:, 0, :], 1.0 / C, None, ALU.mult))
                ch.link(v.tensor_tensor(xc, xin, per_node(stat[:, 0, :], C), ALU.subtract))
                ch.link(v.tensor_tensor(sq, xc, xc, ALU.mult))
                ch.link(v.tensor_reduce(stat[:, 1, :], sq, AX.X, ALU.add))
                v.tensor_scalar(stat[:, 1, :], stat[:, 1, :], 1.0 / C, EPS, ALU.mult, ALU.add).then_inc(root_in, 1)
                inverse_root(stat[:, 1, :])
                ch.link(v.tensor_tensor(xc, xc, per_node(stat[:, 1, :], C), ALU.mult))

            def layer_input(signal):
                layer_norm(xs[:, :, :], hs[:, :, :], CH)
                v.tensor_scalar(hs[:, :, :], hs[:, :, :], 0.0, None, ALU.max).then_inc(signal, 1)

            layer_input(dense_in)
            for l in range(3):
                dve.wait_ge(dense_out, 5 * (3 + l))
                v.tensor_tensor(hid, hid, per_node(dinv[:, :], HID), ALU.mult).then_inc(table_made, 1)
                dve.wait_ge(table_made, l + 1)
                ch.link(v.tensor_copy(acc, hid))
                S, c2 = ps_sems[f"conv{l}"], Chain(dve, pass_chain[f"conv{l}"])
                with dve.Fori(0, PAIRS) as j:
                    c2.enter(j, 2 * (GRP - 1))
                    for s in range(2):
                        dve.wait_ge(S["mm_done"][s], j + LIT)
                        make_onehot(s, j * (2 * GRP) + s * GRP).then_inc(S["oh_ready"][s], 1)
                    for s in range(2):
                        dve.wait_ge(S["mm_done"][s], j + 1 + LIT)
                        for k in range(GRP):
                            b = block_of(dve, j * (2 * GRP) + s * GRP + k)
                            row = acc[:, bass.ds(b, 1), :].rearrange("p a c -> p (a c)")
                            add_rows(c2, S["added"][s], j, k, row, ps[:, 4 + s, k * HID:(k + 1) * HID])
                c2.leave(PAIRS)
                ch.link(v.tensor_tensor(acc, acc, per_node(dinv[:, :], HID), ALU.mult))
                ch.link(v.tensor_tensor(acc, acc, bc(small["bcv"][:, :].unsqueeze(1), [P, BLOCKS, HID]), ALU.add))
                ch.link(v.tensor_tensor(acc, acc, state, ALU.add))
                layer_norm(acc, state, HID)
                ch.link(v.tensor_tensor(state, state, bc(small["lg"][:, :].unsqueeze(1), [P, BLOCKS, HID]), ALU.mult))
                v.tensor_tensor(state, state, bc(small["lb"][:, :].unsqueeze(1), [P, BLOCKS, HID]), ALU.add) \
                 .then_inc(dense_in, 1)
            dve.wait_ge(dense_out, 5 * 7)
            ch.link(v.tensor_tensor(xs[:, :, :], xs[:, :, :], ys[:, :, :], ALU.add))
            layer_input(table_made)
            v.memset(carry[:, :], -BIG)
            ch.link(v.memset(att_max[:, :, :], 0.0))
            c2 = Chain(dve, A["chain"])
            with dve.Fori(0, PAIRS) as j:
                c2.enter(j, 2 * (2 + GRP - 1))
                for s in range(2):
                    g = j * 2 + s
                    first = j * (2 * GRP) + s * GRP
                    rows = hsrc[:, bass.ds(first, GRP), :]
                    dve.wait_ge(lay_gathered["att"][s], (j + 1) * (16 * GRP))
                    dve.wait_ge(A["turned"], g + LIT)
                    v.tensor_tensor(hmask[:, :, :], gbuf[:, s, :, 0:CH],
                                    bc(inblk[:, bass.ds(first, GRP)].unsqueeze(2), [P, GRP, CH]),
                                    ALU.mult).then_inc(A["masked"], 1)
                    dve.wait_ge(A["masked"], g + 1 + LIT)
                    v.tensor_copy(rows, hmask[:, :, :]).then_inc(att_used[s], 1)
                    dve.wait_ge(A["max_rows"], g + LIT)
                    c2.link(make_onehot(0, first))
                    v.tensor_tensor(onehot[:, 0, :, :], onehot[:, 0, :, :],
                                    bc(lastf[:, bass.ds(first, GRP)].unsqueeze(2), [P, GRP, P]), ALU.mult) \
                     .then_inc(A["lastoh"], 1)
                    dve.wait_ge(A["rep_copied"], g + 1 + LIT)
                    for h in range(2):
                        ins = v.tensor_tensor(e2[:, h, :], ps[:, 2 + h, :], hrep[:, h, :], ALU.mult)
                    ins.then_inc(A["e2_ready"], 1)
                    dve.wait_ge(A["e2_ready"], g + 1 + LIT)
                    dve.wait_ge(A["max_turned"], g + LIT)
                    for h in range(2):
                        ins = v.tensor_tensor_scan(runmax[:, h, :], ps[:, 6, :], e2[:, h, :], carry[:, h:h + 1],
                                                   ALU.add, ALU.max)
                    ins.then_inc(A["max_ready"], 1)
                    dve.wait_ge(A["max_ready"], g + 1 + LIT)
                    c2.link(v.tensor_copy(carry[:, :], runmax[:, :, GRP * P - 1]))
                    dve.wait_ge(A["max_rows"], g + 1 + LIT)
                    for k in range(GRP):
                        b = block_of(dve, first + k)
                        row = att_max[:, bass.ds(b, 1), :].rearrange("p a c -> p (a c)")
                        add_rows(c2, A["max_added"], g, k, row, ps[:, 4 + k // 2, (k % 2) * ATT:(k % 2 + 1) * ATT])
            c2.leave(PAIRS)
            ch.link(v.memset(big[:, :], 0.0))
            c3 = Chain(dve, A["b_chain"])
            with dve.Fori(0, STEPS // GRP) as g:
                c3.enter(g, GRP)
                dve.wait_ge(A["b_summed"], g * GRP + LIT)
                make_onehot(0, g * GRP).then_inc(A["b_oh"], 1)
                dve.wait_ge(A["b_oh"], g + 1 + LIT)

                def add_sums(k):
                    dve.wait_ge(A["b_summed"], g * GRP + (k + 1) + LIT)
                    b = block_of(dve, g * GRP + k)
                    row = att_acc[:, bass.ds(b, 1), :].rearrange("p a c -> p (a c)")
                    v.tensor_tensor(row, row, ps[:, 6 + k % 2, :], ALU.add).then_inc(A["b_added"], 1)
                    dve.wait_ge(A["b_added"], g * GRP + (k + 1) + LIT)

                for k in range(GRP):
                    dve.wait_ge(A["b_product"], g * GRP + (k + 1) + LIT)
                    if k >= 2:
                        dve.wait_ge(A["b_exp"], g * GRP + (k - 1) + LIT)
                        dve.wait_ge(A["b_weighted"], g * GRP + (k - 1) + LIT)
                    c3.link(v.tensor_tensor(
                        e2[:, k % 2, :].rearrange("p (q i o) -> p q i o", q=2, i=CH),
                        ps[:, 2 + k % 2, :].rearrange("p (q i o) -> p q i o", q=2, i=CH),
                        bc(hsrc[:, bass.ds(g * GRP + k, 1), :].rearrange("p a c -> p (a c)").unsqueeze(1).unsqueeze(3),
                           [P, 2, CH, CH]), ALU.mult))
                    dve.wait_ge(A["b_shift"], g * GRP + (k + 1) + LIT)
                    v.tensor_tensor(e2[:, k % 2, 0:ATT], e2[:, k % 2, 0:ATT], ps[:, 4 + k % 2, 0:ATT], ALU.subtract) \
                     .then_inc(A["b_diff"], 1)
                    dve.wait_ge(A["b_exp"], g * GRP + (k + 1) + LIT)
                    v.tensor_tensor(spread[:, k % 2, 2:4, :], spread[:, k % 2, 0:2, :],
                                    e2[:, k % 2, ATT:2 * ATT].rearrange("p (a c) -> p a c", a=2), ALU.mult) \
                     .then_inc(A["b_weighted"], 1)
                    if k >= 1:
                        add_sums(k - 1)
                add_sums(GRP - 1)
            c3.leave(STEPS // GRP)
            den, num = att_acc[:, :, 0:ATT], att_acc[:, :, ATT:2 * ATT]
            ch.link(v.tensor_scalar(den, den, 1e-30, None, ALU.max))
            ch.link(v.reciprocal(den, den))
            ch.link(v.tensor_tensor(num, num, den, ALU.mult))
            ch.link(v.tensor_reduce(ys[:, :, :], num.rearrange("p b (i o) -> p b o i", i=CH), AX.X, ALU.add))
            ch.link(v.tensor_tensor(xs[:, :, :], xs[:, :, :], ys[:, :, :], ALU.add))
            layer_input(table_made)
            dve.wait_ge(table_made, 5)
            for l in range(2):
                ch.link(v.memset(acc, 0.0))
                S, c2 = ps_sems[f"rel{l + 1}"], Chain(dve, pass_chain[f"rel{l + 1}"])
                with dve.Fori(0, PAIRS) as j:
                    c2.enter(j, 2 * (GRP - 1) + 2)
                    for s in range(2):
                        first = j * (2 * GRP) + s * GRP
                        dve.wait_ge(S["mm_done"][s], j + LIT)
                        make_onehot(s, first).then_inc(S["oh_ready"][s], 1)
                        c2.link(v.tensor_tensor(typeoh[:, s, :, :], bc(iota_f[:, 0:REL].unsqueeze(1), [P, GRP, REL]),
                                                bc(type_f[:, bass.ds(first, GRP)].unsqueeze(2), [P, GRP, REL]),
                                                ALU.is_equal))
                        dve.wait_ge(S["gathered"][s], (j + 1) * (16 * GRP))
                        v.tensor_tensor(spread[:, s, :, :].rearrange("p k (r c) -> p k r c", r=REL),
                                        bc(typeoh[:, s, :, :].unsqueeze(3), [P, GRP, REL, CH]),
                                        bc(gbuf[:, s, :, 0:CH].unsqueeze(2), [P, GRP, REL, CH]),
                                        ALU.mult).then_inc(S["rhs_ready"][s], 1)
                    for s in range(2):
                        dve.wait_ge(S["mm_done"][s], j + 1 + LIT)
                        for k in range(GRP):
                            b = block_of(dve, j * (2 * GRP) + s * GRP + k)
                            row = acc[:, bass.ds(b, 1), :].rearrange("p a c -> p (a c)")
                            add_rows(c2, S["added"][s], j, k, row, ps[:, 4 + s, k * HID:(k + 1) * HID])
                c2.leave(PAIRS)
                v.tensor_tensor(hid.rearrange("p b (r c) -> p b r c", r=REL), acc.rearrange("p b (r c) -> p b r c", r=REL),
                                bc(invcnt[:, :, :].unsqueeze(3), [P, BLOCKS, REL, CH]), ALU.mult).then_inc(dense_in, 1)
                dve.wait_ge(dense_out, 5 * (9 + 2 * l))
                ch.link(v.tensor_tensor(ys[:, :, :], ys[:, :, :], zs[:, :, :], ALU.add))
                if l == 0:
                    v.tensor_scalar(hs[:, :, :], ys[:, :, :], 0.0, None, ALU.max).then_inc(table_made, 1)
                    dve.wait_ge(table_made, 6)
            ch.link(v.tensor_reduce(stat[:, 0, :], ys[:, :, :], AX.X, ALU.max))
            v.tensor_tensor(ys[:, :, :], ys[:, :, :], per_node(stat[:, 0, :], CH), ALU.subtract).then_inc(lse_in, 1)
            dve.wait_ge(lse_exp, 1)
            v.tensor_reduce(stat[:, 1, :], zs[:, :, :], AX.X, ALU.add).then_inc(lse_sum, 1)
            dve.wait_ge(lse_ln, 1)
            dve.wait_ge(lse_in, 1)
            ch.link(v.tensor_tensor(ys[:, :, :], ys[:, :, :], per_node(stat[:, 2, :], CH), ALU.subtract))
            ch.link(v.tensor_tensor(xs[:, :, :], xs[:, :, :], ys[:, :, :], ALU.add))
            layer_input(table_made)
            c4 = Chain(dve, R["chain"])
            with dve.Fori(0, PAIRS) as j:
                c4.enter(j, 2 * 5 + 2 * GRP)
                for s in range(2):
                    first = j * (2 * GRP) + s * GRP
                    g = j * 2 + s
                    dve.wait_ge(R["scattered"], g * GRP + LIT)
                    make_onehot(s, first).then_inc(R["oh"], 1)
                    c4.link(v.tensor_tensor(gbuf_ohs(s), bc(iota_row.unsqueeze(1), [P, GRP, P]),
                                            bc(srclo[:, bass.ds(first, GRP)].unsqueeze(2), [P, GRP, P]), ALU.is_equal))
                    dve.wait_ge(lay_gathered["rea"][s], (j + 1) * (16 * GRP))
                    dve.wait_ge(R["xj"], g + 1 + LIT)
                    xi = gbuf[:, s, :, 0:CH]
                    xj = ps[:, 2, 0:GRP * CH].rearrange("p (k c) -> p k c", k=GRP)
                    t0, t1 = (rea_tmp[:, q, :].rearrange("p (k c) -> p k c", k=GRP) for q in range(2))
                    c4.link(v.tensor_scalar(t0, xj, 0.1, 5.0, ALU.mult, ALU.add))
                    c4.link(v.scalar_tensor_tensor(t0, xi, 0.9, t0, ALU.mult, ALU.add))
                    v.tensor_tensor(t1, xi, xj, ALU.mult)
                    c4.link(v.reciprocal(t0, t0))
                    c4.link(v.tensor_tensor(t1, t1, t0, ALU.mult))
                    v.tensor_tensor(t1, t1, bc(weight[:, bass.ds(first, GRP)].unsqueeze(2), [P, GRP, CH]),
                                    ALU.mult).then_inc(rea_used[s], 1)
                    dve.wait_ge(rea_used[s], j + 1 + LIT)
                    for k in range(GRP):
                        c4.link(v.tensor_scalar(blkoh[:, k, :], iota_f[:, 0:BLOCKS], srcblk[:, bass.ds(first + k, 1)], None,
                                                ALU.is_equal))
                        v.tensor_tensor(spread_rea(k).rearrange("p (b c) -> p b c", b=BLOCKS),
                                        bc(blkoh[:, k, :].unsqueeze(2), [P, BLOCKS, CH]),
                                        bc(t1[:, k, :].unsqueeze(1), [P, BLOCKS, CH]), ALU.mult).then_inc(R["spread"], 1)
            c4.leave(PAIRS)
            ch.link(v.tensor_scalar(ys[:, :, :], hs[:, :, :], -1.0 / 5.0, 1.0, ALU.mult, ALU.add))
            ch.link(v.tensor_tensor(ys[:, :, :], ys[:, :, :], hs[:, :, :], ALU.mult))
            ch.link(v.scalar_tensor_tensor(zs[:, :, :], hs[:, :, :], -1.0, ys[:, :, :], ALU.add, ALU.mult))
            ch.link(v.scalar_tensor_tensor(xs[:, :, :], zs[:, :, :], 0.1, xs[:, :, :], ALU.add, ALU.add))
            dve.wait_ge(R["all"], 1)
            v.tensor_tensor(xs[:, :, :], xs[:, :, :], ps[:, 6, 0:BLOCKS * CH].rearrange("p (b c) -> p b c", b=BLOCKS),
                            ALU.add).then_inc(x_done, 1)


_INS = ['x', 'src', 'dst', 'edge_attr_16', 'edge_type_8', 'edge_weight',
        'L0_gnn_W_enc0', 'L0_gnn_b_enc0', 'L0_gnn_W_enc1', 'L0_gnn_b_enc1', 'L0_gnn_W_conv', 'L0_gnn_b_conv',
        'L0_gnn_ln_g', 'L0_gnn_ln_b', 'L0_gnn_W_dec0', 'L0_gnn_b_dec0', 'L0_gnn_W_dec1', 'L0_gnn_b_dec1',
        'L1_gnn_W_msg', 'L1_gnn_b_msg', 'L1_gnn_W_attn', 'L1_gnn_b_attn',
        'L2_gnn_W1', 'L2_gnn_root1', 'L2_gnn_b1', 'L2_gnn_W2', 'L2_gnn_root2', 'L2_gnn_b2']
_OUTS = [((3125, 16), 'float32')]


def kernel(**inputs):
    import numpy as _np
    import concourse.bacc as _bacc
    from concourse import mybir as _mybir
    from concourse.bass_utils import run_bass_kernel_spmd as _run

    nc = _bacc.Bacc("TRN2", target_bir_lowering=False, num_devices=1)
    arrays, args = {}, []
    for name in _INS:
        a = _np.ascontiguousarray(inputs[name])
        arrays[f"in_{name}_dram"] = a
        args.append(nc.dram_tensor(f"in_{name}_dram", a.shape, _mybir.dt.from_np(a.dtype), kind="ExternalInput").ap())
    for i, (shape, dtype) in enumerate(_OUTS):
        dt = _mybir.dt.from_np(_np.dtype(dtype))
        args.append(nc.dram_tensor(f"out_{i}_dram", shape, dt, kind="ExternalOutput").ap())
    gnn_program(nc, *args)
    r = _run(nc, [arrays], core_ids=[0])
    return r.results[0]["out_0_dram"]
```

```python
from contextlib import ExitStack

import concourse.bass as bass
from concourse import mybir

ALU = mybir.AluOpType
ACT = mybir.ActivationFunctionType
AX = mybir.AxisListType
F32 = mybir.dt.float32
BF16 = mybir.dt.bfloat16
I32 = mybir.dt.int32

P = 128
GRP = 4
T = GRP * P
N = 3125
E = 103125
BLOCKS = -(-N // P)
TILES = -(-E // T)
FULL = E // T
TAIL = E - FULL * T
TURNS = TILES + BLOCKS - 1
TRIPS = TURNS // 2
ROWS = TILES + 1
SCH = -(-TURNS // P)
TPAD = SCH * P
COLS = TURNS * GRP
REL = 8
CH = 16
HID = 128
ATT = CH * CH
KS = 6 * CH + 3
BIG = float(2.0 ** 127)
EPS = 1e-5
LIT = 2


class Chain:

    def __init__(self, eng, sem):
        self.eng, self.sem, self.n, self.base = eng, sem, 0, None

    def value(self):
        return self.n if self.base is None else self.base + self.n

    def link(self, ins):
        ins.then_inc(self.sem, 1)
        self.n += 1
        self.eng.wait_ge(self.sem, self.value())

    def enter(self, i, per_trip):
        self.base, self.start, self.per = i * per_trip, self.n, per_trip

    def leave(self, trips):
        assert self.n - self.start == self.per, (self.n - self.start, self.per)
        self.n = self.start + self.per * trips
        self.base = None


def gnn_program(nc, x, src, dst, edge_attr_16, edge_type_8, edge_weight,
                W_enc0, b_enc0, W_enc1, b_enc1, W_conv, b_conv, ln_g, ln_b,
                W_dec0, b_dec0, W_dec1, b_dec1, W_msg, b_msg, W_attn, b_attn,
                W1, root1, b1, W2, root2, b2, out):
    with ExitStack() as ctx:
        def sb(name, shape, dt=F32):
            return ctx.enter_context(nc.sbuf_tensor(name, shape, dt))

        def sem(name):
            return ctx.enter_context(nc.semaphore(name))

        def dram(name, shape, dt=F32):
            return nc.dram_tensor(name, shape, dt).ap()

        ctx.enter_context(nc.allow_non_contiguous_dma(reason="last dst of each tile"))

        etab = dram("etab", [ROWS, 3, T], I32)
        wtab = dram("wtab", [ROWS, T])
        etab_flat = etab.rearrange("t k e -> t (k e)")
        efpad = dram("efpad", [TURNS * T, CH])
        parts = dram("parts", [TURNS, KS, T], BF16)
        dstflat = dram("dstflat", [TPAD * T + 2])
        startflat = dram("startflat", [TPAD, T], BF16)
        conv_tab = [dram(f"conv_tab{l}", [BLOCKS * P, HID]) for l in range(3)]
        h_tab = [dram(f"h_tab{l}", [BLOCKS * P, CH]) for l in range(4)]
        max_tab = dram("max_tab", [BLOCKS * P + 1, ATT])

        part_i = sb("part_i", [P, 1], I32)
        iota_f = sb("iota_f", [P, TPAD])
        part_f = sb("part_f", [P, 1])
        ident = sb("ident", [P, P])
        ident_b = sb("ident_b", [P, P], BF16)
        ones = sb("ones", [P, P])
        zeros = sb("zeros", [P, BLOCKS * CH])
        path = sb("path", [P, 4])
        tcol_f = sb("tcol_f", [P, SCH])
        tcol = sb("tcol", [P, SCH], I32)
        blk_row = sb("blk_row", [1, TPAD], I32)
        tile_row = sb("tile_row", [1, TPAD], I32)
        dstloc = sb("dstloc", [P, COLS], BF16)
        lastloc = sb("lastloc", [P, COLS], BF16)
        inblk = sb("inblk", [P, COLS], BF16)
        srclo = sb("srclo", [P, COLS], BF16)
        srcblk = sb("srcblk", [P, COLS], BF16)
        type_f = sb("type_f", [P, COLS], BF16)
        src_i = sb("src_i", [P, COLS], I32)
        dst_i = sb("dst_i", [P, COLS], I32)
        weight = sb("weight", [P, COLS])
        cnt = sb("cnt", [P, BLOCKS, REL])
        invcnt = sb("invcnt", [P, BLOCKS, REL])
        dinv = sb("dinv", [P, BLOCKS])
        dtmp = sb("dtmp", [P, BLOCKS])
        stat = sb("stat", [P, 3, BLOCKS])
        xs = sb("xs", [P, BLOCKS, CH])
        hs = sb("hs", [P, BLOCKS, CH])
        ys = sb("ys", [P, BLOCKS, CH])
        zs = sb("zs", [P, BLOCKS, CH])
        big = sb("big", [P, 4 * BLOCKS * HID])
        quarter = BLOCKS * HID
        acc, state, hid, tmp = (big[:, q * quarter:(q + 1) * quarter].rearrange("p (b c) -> p b c", b=BLOCKS)
                                for q in range(4))
        att_acc = big[:, :].rearrange("p (b c) -> p b c", b=BLOCKS)
        hrep = big[:, 0:2 * T].rearrange("p (h e) -> p h e", h=2)
        runmax = big[:, 2 * T:6 * T].rearrange("p (s h e) -> p s h e", s=2, h=2)
        e2 = big[:, 6 * T:8 * T].rearrange("p (h e) -> p h e", h=2)
        maxE = big[:, 8 * T:10 * T].rearrange("p (k c) -> p k c", k=GRP)
        rea_spread = big[:, 0:2 * GRP * BLOCKS * CH].rearrange("p (s k c) -> p s k c", s=2, k=GRP)
        rea_tmp = big[:, 4000:4000 + 2 * GRP * CH].rearrange("p (a c) -> p a c", a=2)
        blkoh = big[:, 3600:3600 + GRP * BLOCKS].rearrange("p (k b) -> p k b", k=GRP)
        maxima = sb("maxima", [P, BLOCKS * ATT])
        att_max = maxima[:, :].rearrange("p (b c) -> p b c", b=BLOCKS)
        terms = maxima[:, 0:2 * GRP * T].rearrange("p (s c) -> p s c", s=2)
        gmax = maxima[:, 2 * GRP * T:2 * GRP * (T + ATT)].rearrange("p (s k c) -> p s k c", s=2, k=GRP)
        iota_i = maxima[:, 0:TPAD].bitcast(I32)
        past = maxima[:, TPAD:2 * TPAD]
        stepblk = maxima[:, 2 * TPAD:3 * TPAD]
        lastd_i = maxima[0:1, 3 * TPAD:3 * TPAD + TILES].bitcast(I32)
        lastd_f = maxima[0:1, 4 * TPAD:4 * TPAD + TILES]
        setup_tmp = maxima[:, 5 * TPAD:5 * TPAD + COLS]
        padi = maxima[0:1, 3088:3088 + 3 * T].bitcast(I32)
        wres = maxima[0:CH + 1, 4624:4624 + T]
        wpart = maxima[0:CH + 1, 5136:5136 + 3 * T // 2].bitcast(BF16).rearrange("p (q c) -> p q c", q=3)
        setup_tmp2 = maxima[:, 5 * TPAD + COLS:5 * TPAD + 2 * COLS]
        hsrc = sb("hsrc", [P, COLS, CH])
        stage = hsrc[:, :, :].rearrange("p s c -> p (s c)")
        st_i = stage[:, 0:3 * SCH * T].bitcast(I32).rearrange("p (c k e) -> p c k e", c=SCH, k=3)
        st_f = stage[:, 3 * SCH * T:8 * SCH * T].rearrange("p (c k e) -> p c k e", c=SCH, k=5)
        st_prev = stage[:, 8 * SCH * T:9 * SCH * T].rearrange("p (c e) -> p c e", c=SCH)
        st_next = stage[:, 9 * SCH * T:10 * SCH * T].rearrange("p (c e) -> p c e", c=SCH)
        st_neg = stage[:, 10 * SCH * T:11 * SCH * T].bitcast(BF16)[:, 0:SCH * T].rearrange("p (c e) -> p c e", c=SCH)
        rows_at = sb("rows_at", [P, 2, GRP], I32)
        gbuf = sb("gbuf", [P, 2, GRP, HID])
        onehot = sb("onehot", [P, 2, GRP, P])
        spread = sb("spread", [P, 2, GRP, HID])
        typeoh = sb("typeoh", [P, 2, GRP, REL])
        xT = sb("xT", [P, 5, P])
        efrow = sb("efrow", [P, 2, GRP, CH])
        efres = sb("efres", [P, GRP, CH])
        stack = sb("stack", [P, GRP, KS], BF16)
        stackT = sb("stackT", [KS, 2, T], BF16)
        starts = sb("starts", [P, 2, T], BF16)
        hparts = sb("hparts", [P, GRP, P], BF16)
        hpartsT = sb("hpartsT", [3 * CH, T], BF16)
        carry = sb("carry", [P, 2])
        wm = sb("wm", [CH + 1, 2 * ATT])
        wstack = sb("wstack", [KS, 2 * ATT], BF16)
        wmix = sb("wmix", [KS, 2 * ATT], BF16)
        rep = sb("rep", [CH, ATT], BF16)
        rep3 = sb("rep3", [3 * CH, ATT], BF16)
        small = {}
        for name, shape in (("e0", [CH, HID]), ("e1", [HID, HID]), ("cv", [HID, HID]), ("d0", [HID, HID]),
                            ("d1", [HID, CH]), ("r1", [CH, CH]), ("r2", [CH, CH]), ("w1", [HID, CH]),
                            ("w2", [HID, CH]), ("be0", [1, HID]), ("be1", [1, HID]), ("bd0", [1, HID]),
                            ("bd1", [1, CH]), ("b1", [1, CH]), ("b2", [1, CH])):
            small[name] = sb("w_" + name, shape)
        for q, name in enumerate(("bcv", "lg", "lb")):
            small[name] = maxima[:, 6000 + q * HID:6000 + (q + 1) * HID]
        ps = ctx.enter_context(nc.psum_tensor("ps", [P, 8, 512], F32))

        loaded, iota_done, consts_done, pads_done = (sem(q) for q in ("loaded", "iota_done", "consts_done", "pads_done"))
        last_loaded, etab_done, tcol_done = sem("last_loaded"), sem("etab_done"), sem("tcol_done")
        path_cmp, path_mm, path_blk_mm = sem("path_cmp"), sem("path_mm"), sem("path_blk_mm")
        rows_got, dst_conv, dst_out, dst_back, start_made, start_out = (sem(q) for q in (
            "rows_got", "dst_conv", "dst_out", "dst_back", "start_made", "start_out"))
        idx_turned, idx_copied, idx_done = sem("idx_turned"), sem("idx_copied"), sem("idx_done")
        wparts_made, wstack_in, wmix_done = sem("wparts_made"), sem("wstack_in"), sem("wmix_done")
        dense_in, dense_turned, dense_copied, dense_mul, dense_out = (sem(q) for q in (
            "dense_in", "dense_turned", "dense_copied", "dense_mul", "dense_out"))
        table_made, table_out = sem("table_made"), sem("table_out")
        max_made, max_out = sem("max_made"), sem("max_out")
        dve_step, root_in, root_out, rows_known = (sem(q) for q in ("dve_step", "root_in", "root_out", "rows_known"))
        lse_in, lse_exp, lse_sum, lse_ln = (sem(q) for q in ("lse_in", "lse_exp", "lse_sum", "lse_ln"))
        x_done, stored = sem("x_done"), sem("stored")

        def pair(name):
            return [sem(f"{name}{q}") for q in range(2)]

        def table(prefix, names):
            return {k: sem(prefix + k) for k in names.split()}

        passes = ["count", "conv0", "conv1", "conv2", "rel1", "rel2"]
        S = {p: {k: pair(f"{p}_{k}") for k in ("oh_ready", "rhs_ready", "mm_done", "added")} for p in passes}
        gathered = {p: pair(p + "_gathered") for p in passes[1:] + ["att", "max", "rea"]}
        used = {"att": pair("att_used"), "rea": pair("rea_used")}
        F = table("parts_", "split turned copied")
        parts_in, parts_out = pair("parts_in"), pair("parts_out")
        A = table("att_", "split turned copied product rep_copied e2_made scanned max_turned max_copied "
                          "lastoh max_rows max_added")
        att_in = pair("att_in")
        B = table("sum_", "product made diff exp weighted oh summed added")
        sum_in = pair("sum_in")
        R = table("rea_", "oh turned copied xj srcoh spread scattered")
        rea_all = sem("rea_all")
        chains = {k: sem(k + "_chain") for k in ("conv0", "rel1", "rel2", "att", "rea")}

        idx_raw = big[:, 0:5 * COLS].rearrange("p (k s) -> p k s", k=5)
        N_ETAB = 8 + 2 + 6 + 2 + -(-(TURNS * T - E) // T)
        N_LOADS = 2 + 9 + 6 + 3 + 4

        lit_sems = [q for t in S.values() for two in t.values() for q in two]
        lit_sems += [q for two in used.values() for q in two]
        lit_sems += [q for t in (F, A, B, R) for q in t.values()]

        def lit(eng, q, n):
            eng.wait_ge(q, n + LIT)

        def bank_b(n):
            return ps[:, n, :].bitcast(BF16)

        def flat(ap):
            return ap.rearrange("p a c -> p (a c)")

        efpad_rows = efpad.rearrange("(t k p) c -> t p k c", k=GRP, p=P)
        NODES_FULL = N // P * P
        iota_row = iota_f[:, 0:P]

        block = ctx.enter_context(nc.Block())

        def block_of(eng, turn):
            return eng.value_load(blk_row[0:1, bass.ds(turn, 1)], min_val=0, max_val=BLOCKS - 1)

        def tile_of(eng, turn):
            return eng.value_load(tile_row[0:1, bass.ds(turn, 1)], min_val=0, max_val=ROWS - 1)

        @block.sync
        def _(sp):
            for q in lit_sems:
                sp.sem_inc(q, LIT)
            sp.dma_start(lastd_i[0:1, 0:FULL], dst[0:FULL * T].rearrange("(a t e) -> a t e", a=1, e=T)[:, :, T - 1]) \
              .then_inc(last_loaded, 16)
            sp.dma_start(lastd_i[0:1, FULL:TILES], dst[E - 1:E].rearrange("(a t) -> a t", a=1)) \
              .then_inc(last_loaded, 16)
            for k, column in enumerate((src, dst, edge_type_8)):
                sp.dma_start(etab[0:FULL, k, :], column[0:FULL * T].rearrange("(t e) -> t e", e=T)).then_inc(etab_done, 16)
                sp.dma_start(etab[FULL:TILES, k, 0:TAIL], column[FULL * T:E].rearrange("(t e) -> t e", t=1)) \
                  .then_inc(etab_done, 16)
            sp.dma_start(wtab[0:FULL, :], edge_weight[0:FULL * T].rearrange("(t e) -> t e", e=T)).then_inc(etab_done, 16)
            sp.dma_start(wtab[FULL:TILES, 0:TAIL], edge_weight[FULL * T:E].rearrange("(t e) -> t e", t=1)) \
              .then_inc(etab_done, 16)
            sp.wait_ge(pads_done, 1)
            for k in range(3):
                pad = padi[0:1, k * T:(k + 1) * T]
                sp.dma_start(etab[FULL:TILES, k, TAIL:T], pad[:, 0:T - TAIL]).then_inc(etab_done, 16)
                sp.dma_start(etab[TILES:ROWS, k, :], pad).then_inc(etab_done, 16)
            sp.dma_start(wtab[FULL:TILES, TAIL:T], padi[0:1, 0:T - TAIL].bitcast(F32)).then_inc(etab_done, 16)
            sp.dma_start(wtab[TILES:ROWS, :], padi[0:1, 0:T].bitcast(F32)).then_inc(etab_done, 16)
            sp.dma_start(xs[:, 0:BLOCKS - 1, :], x[0:NODES_FULL, :].rearrange("(b p) c -> p b c", p=P)).then_inc(loaded, 16)
            sp.wait_ge(consts_done, 1)
            sp.dma_start(xs[0:N - NODES_FULL, BLOCKS - 1, :], x[NODES_FULL:N, :]).then_inc(loaded, 16)
            for name, w in (("e0", W_enc0), ("e1", W_enc1), ("cv", W_conv), ("d0", W_dec0), ("d1", W_dec1),
                            ("r1", root1), ("r2", root2), ("w1", W1.rearrange("r c o -> (r c) o")),
                            ("w2", W2.rearrange("r c o -> (r c) o"))):
                sp.dma_start(small[name][:, :], w).then_inc(loaded, 16)
            for name, b in (("be0", b_enc0), ("be1", b_enc1), ("bd0", b_dec0), ("bd1", b_dec1), ("b1", b1), ("b2", b2)):
                sp.dma_start(small[name][:, :], b.rearrange("(a c) -> a c", a=1)).then_inc(loaded, 16)
            for name, b in (("bcv", b_conv), ("lg", ln_g), ("lb", ln_b)):
                sp.dma_start(small[name], b.rearrange("(a c) -> a c", a=1).to_broadcast([P, HID])).then_inc(loaded, 16)
            for q, (w, b) in enumerate(((W_attn, b_attn), (W_msg, b_msg))):
                sp.dma_start(wm[0:CH, q * ATT:(q + 1) * ATT], w).then_inc(loaded, 16)
                sp.dma_start(wm[CH:CH + 1, q * ATT:(q + 1) * ATT], b.rearrange("(a c) -> a c", a=1)).then_inc(loaded, 16)
            sp.dma_start(efpad[0:FULL * T, :], edge_attr_16[0:FULL * T, :]).then_inc(etab_done, 16)
            sp.dma_start(efpad[FULL * T:E, :], edge_attr_16[FULL * T:E, :]).then_inc(etab_done, 16)
            at = E
            while at < TURNS * T:
                n = min(T, TURNS * T - at)
                rows = next(r for r in range(P, 0, -1) if n % r == 0)
                sp.dma_start(efpad[at:at + n, :].rearrange("(p r) c -> p (r c)", p=rows), zeros[0:rows, 0:n // rows * CH]) \
                  .then_inc(etab_done, 16)
                at += n
            sp.wait_ge(dst_conv, 1)
            sp.dma_start(dstflat[1:TPAD * T + 1].rearrange("(c s e) -> s c e", s=P, e=T), st_f[:, :, 1, :]) \
              .then_inc(dst_out, 16)
            sp.dma_start(dstflat[0:1].rearrange("(a c) -> a c", a=1), path[0:1, 3:4]).then_inc(dst_out, 16)
            sp.dma_start(dstflat[TPAD * T + 1:TPAD * T + 2].rearrange("(a c) -> a c", a=1), path[0:1, 3:4]) \
              .then_inc(dst_out, 16)
            sp.wait_ge(dst_out, 48)
            sp.dma_start(st_prev, dstflat[0:TPAD * T].rearrange("(c s e) -> s c e", s=P, e=T)).then_inc(dst_back, 16)
            sp.dma_start(st_next, dstflat[2:TPAD * T + 2].rearrange("(c s e) -> s c e", s=P, e=T)).then_inc(dst_back, 16)
            sp.wait_ge(start_made, 1)
            sp.dma_start(startflat.rearrange("(c s) e -> s c e", s=P), st_neg).then_inc(start_out, 16)
            sp.wait_ge(wparts_made, 1)
            at = 0
            for q, rows in ((0, CH + 1), (1, CH + 1), (2, CH + 1), (0, CH), (1, CH), (0, CH)):
                sp.dma_start(wstack[at:at + rows, :], wpart[0:rows, q, :]).then_inc(wstack_in, 16)
                at += rows
            for q in range(3):
                sp.dma_start(rep3[q * CH:(q + 1) * CH, :], rep[:, :]).then_inc(wstack_in, 16)

            def write_table(to, nodes, nth):
                sp.wait_ge(table_made, nth)
                sp.dma_start(to.rearrange("(b p) c -> p b c", p=P), nodes).then_inc(table_out, 16)

            write_table(conv_tab[0], hid, 1)
            sp.wait_ge(etab_done, 16 * N_ETAB)
            with sp.Fori(0, TRIPS) as j:
                tiles = [sp.snap(j * 2), sp.snap(j * 2 + 1)]
                for s in range(2):
                    lit(sp, F["split"], j * 2 + (s - 1))
                    sp.nop(nofuse=True)
                    sp.dma_start(efrow[:, s, :, :],
                                 efpad_rows[bass.ds(tiles[s], 1), :, :, :].rearrange("a p k c -> (a p) k c")) \
                      .then_inc(parts_in[s], 16)
                for s in range(2):
                    lit(sp, F["copied"], j * 2 + (s + 1))
                    sp.nop(nofuse=True)
                    sp.dma_start(parts[bass.ds(tiles[s], 1), :, :].rearrange("a r e -> (a r) e"), stackT[:, s, :]) \
                      .then_inc(parts_out[s], 16)
                for s in range(2):
                    sp.wait_ge(parts_out[s], (j + 1) * 16)
                    sp.nop(nofuse=True)
            write_table(conv_tab[1], hid, 2)
            write_table(conv_tab[2], hid, 3)
            write_table(h_tab[0], hs[:, :, :], 4)
            sp.wait_ge(start_out, 16)
            with sp.Fori(0, TRIPS) as j:
                for s in range(2):
                    g = sp.snap(j * 2 + s)
                    t = tile_of(sp, g)
                    lit(sp, A["product"], g - 1)
                    sp.nop(nofuse=True)
                    sp.dma_start(stackT[:, s, :], parts[bass.ds(t, 1), :, :].rearrange("a r e -> (a r) e")) \
                      .then_inc(att_in[s], 16)
                    lit(sp, A["scanned"], g - 1)
                    sp.nop(nofuse=True)
                    sp.dma_start(starts[:, s, :], startflat[bass.ds(g, 1), :].to_broadcast([P, T])) \
                      .then_inc(att_in[s], 16)
            sp.wait_ge(max_made, 1)
            sp.dma_start(max_tab[0:BLOCKS * P, :].rearrange("(b p) c -> p b c", p=P), att_max).then_inc(max_out, 16)
            sp.dma_start(max_tab[BLOCKS * P:BLOCKS * P + 1, :], zeros[0:1, 0:ATT]).then_inc(max_out, 16)
            sp.wait_ge(att_in[0], 32 * TRIPS)
            sp.wait_ge(att_in[1], 32 * TRIPS)
            lit(sp, A["product"], TURNS)
            sp.nop(nofuse=True)
            with sp.Fori(0, TRIPS) as j:
                for s in range(2):
                    g = sp.snap(j * 2 + s)
                    t = tile_of(sp, g)
                    lit(sp, B["product"], g * 2 - 1)
                    sp.nop(nofuse=True)
                    sp.dma_start(stackT[:, s, :], parts[bass.ds(t, 1), :, :].rearrange("a r e -> (a r) e")) \
                      .then_inc(sum_in[s], 16)
            for l in range(1, 4):
                write_table(h_tab[l], hs[:, :, :], 4 + l)
            sp.wait_ge(x_done, 1)
            sp.dma_start(out[0:NODES_FULL, :].rearrange("(b p) c -> p b c", p=P), xs[:, 0:BLOCKS - 1, :]).then_inc(stored, 16)
            sp.dma_start(out[NODES_FULL:N, :], xs[0:N - NODES_FULL, BLOCKS - 1, :]).then_inc(stored, 16)
            sp.wait_ge(stored, 32)
            sp.wait_ge(table_out, 16 * 7)
            sp.wait_ge(max_out, 32)
            sp.wait_ge(start_out, 16)

        @block.gpsimd
        def _(pool):
            nc.gpsimd.iota(iota_i, [[1, TPAD]], base=0, channel_multiplier=0).then_inc(iota_done, 1)
            nc.gpsimd.iota(part_i[:, :], [[0, 1]], base=0, channel_multiplier=1).then_inc(iota_done, 1)
            pool.wait_ge(tcol_done, 1)
            pool.wait_ge(etab_done, 16 * N_ETAB)
            for c in range(SCH):
                at = bass.IndirectOffsetOnAxis(tcol[:, c:c + 1], axis=0)
                nc.gpsimd.indirect_dma_start(st_i[:, c, :, :].rearrange("p k e -> p (k e)"), None, etab_flat, at) \
                    .then_inc(rows_got, 16)
                nc.gpsimd.indirect_dma_start(st_f[:, c, 3, :], None, wtab, at).then_inc(rows_got, 16)
            pool.wait_ge(idx_done, 1)
            known = [0]

            def gather_rows(rows, index, dest, got, free):
                with pool.Fori(0, TRIPS) as j:
                    for s in range(2):
                        if free is None:
                            lit(pool, B["diff"], j * 2 + (s - 1))
                        else:
                            lit(pool, free[s], j)
                        nc.gpsimd.tensor_copy(rows_at[:, s, :], index[:, bass.ds(j * (2 * GRP) + s * GRP, GRP)]) \
                            .then_inc(rows_known, 1)
                        pool.wait_ge(rows_known, known[0] + j * 2 + (s + 1))
                        pool.nop(nofuse=True)
                        for k in range(GRP):
                            nc.gpsimd.indirect_dma_start(
                                dest(s, k), None, rows,
                                bass.IndirectOffsetOnAxis(rows_at[:, s, k:k + 1], axis=0)).then_inc(got[s], 16)
                known[0] += 2 * TRIPS

            def wide(s, k):
                return gbuf[:, s, k, :]

            def narrow(s, k):
                return gbuf[:, s, k, 0:CH]

            for l in range(3):
                pool.wait_ge(table_out, 16 * (l + 1))
                gather_rows(conv_tab[l], src_i, wide, gathered[f"conv{l}"], S[f"conv{l}"]["mm_done"])
            pool.wait_ge(table_out, 16 * 4)
            gather_rows(h_tab[0], src_i, narrow, gathered["att"], used["att"])
            pool.wait_ge(max_out, 32)
            gather_rows(max_tab, dst_i, lambda s, k: gmax[:, s, k, :], gathered["max"], None)
            for l in range(2):
                pool.wait_ge(table_out, 16 * (5 + l))
                gather_rows(h_tab[1 + l], src_i, narrow, gathered[f"rel{l + 1}"], S[f"rel{l + 1}"]["rhs_ready"])
            pool.wait_ge(table_out, 16 * 7)
            gather_rows(h_tab[3], src_i, narrow, gathered["rea"], used["rea"])

        @block.tensor
        def _(pe):
            pe.wait_ge(consts_done, 1)
            pe.wait_ge(path_cmp, 1)
            pe.matmul(ps[0:BLOCKS - 1, 0, 0:TILES], ones[0:1, 0:BLOCKS - 1], lastd_f, start=True, stop=True) \
              .then_inc(path_mm, 1)
            pe.wait_ge(path_cmp, 2)
            pe.matmul(ps[:, 2, 0:TPAD], ones[0:BLOCKS - 1, :], past[0:BLOCKS - 1, :], start=True, stop=True)
            for c in range(SCH):
                mm = pe.matmul(ps[:, 4, c:c + 1], past[0:BLOCKS - 1, c * P:(c + 1) * P], ones[0:BLOCKS - 1, 0:1],
                               start=True, stop=True)
            mm.then_inc(path_blk_mm, 1)
            pe.wait_ge(start_made, 1)
            for n in range(5 * SCH):
                if n >= 2:
                    pe.wait_ge(idx_copied, n - 1)
                for k in range(GRP):
                    mm = pe.transpose(ps[:, n % 2, k * P:(k + 1) * P], st_f[:, n // 5, n % 5, k * P:(k + 1) * P], ident[:, :])
                mm.then_inc(idx_turned, 1)
            pe.wait_ge(idx_copied, 5 * SCH)

            dense_count = [0]

            def dense(xin, K, w, bias, C, ready):
                n = dense_count[0]
                dense_count[0] += 1
                pe.wait_ge(*ready)
                for g in range(5):
                    if n or g:
                        pe.wait_ge(dense_copied, 5 * n + g)
                    for k in range(5):
                        mm = pe.transpose(ps[0:K, k // 4, (k % 4) * P:(k % 4 + 1) * P], xin[:, 5 * g + k, :], ident[:, :])
                    mm.then_inc(dense_turned, 1)
                    pe.wait_ge(dense_copied, 5 * n + g + 1)
                    if n or g:
                        pe.wait_ge(dense_out, 5 * n + g)
                    for k in range(5):
                        o = ps[:, 2 + k // 4, (k % 4) * C:(k % 4 + 1) * C]
                        mm = pe.matmul(o, xT[0:K, k, :], w, start=True, stop=bias is None)
                        if bias is not None:
                            mm = pe.matmul(o, ones[0:1, :], bias, start=False, stop=True)
                    mm.then_inc(dense_mul, 1)

            def seg_sum(name, j, s, rhs, C):
                q = S[name]
                lit(pe, q["oh_ready"][s], j + 1)
                if name.startswith("conv"):
                    pe.wait_ge(gathered[name][s], (j + 1) * (16 * GRP))
                else:
                    lit(pe, q["rhs_ready"][s], j + 1)
                lit(pe, q["added"][s], j)
                for k in range(GRP):
                    mm = pe.matmul(ps[:, 4 + s, 0:C], onehot[:, s, k, :], rhs(s, k), start=k == 0, stop=k == GRP - 1)
                mm.then_inc(q["mm_done"][s], 1)

            pe.wait_ge(idx_done, 1)
            with pe.Fori(0, TRIPS) as j:
                for s in range(2):
                    seg_sum("count", j, s, lambda s, k: typeoh[:, s, k, :], REL)
            pe.wait_ge(loaded, 16 * N_LOADS)
            dense(hs, CH, small["e0"][:, :], small["be0"][:, :], HID, (dense_in, 1))
            dense(hid, HID, small["e1"][:, :], small["be1"][:, :], HID, (dense_out, 5))
            for l in range(3):
                dense(state, HID, small["cv"][:, :], None, HID, (dense_in, 1 + l) if l else (dense_out, 10))
                with pe.Fori(0, TRIPS) as j:
                    for s in range(2):
                        if l == 0:
                            t = j * 2 + s
                            lit(pe, F["split"], t + 1)
                            lit(pe, F["copied"], t - 1)
                            for k in range(GRP):
                                mm = pe.transpose(bank_b(6 + s)[0:KS, k * P:(k + 1) * P], stack[:, k, :], ident_b[:, :])
                            mm.then_inc(F["turned"], 1)
                        seg_sum(f"conv{l}", j, s, lambda s, k: gbuf[:, s, k, :], HID)
            dense(state, HID, small["d0"][:, :], small["bd0"][:, :], HID, (dense_in, 4))
            dense(hid, HID, small["d1"][:, :], small["bd1"][:, :], CH, (dense_out, 5 * 6))

            def products(g, j, s):
                lit(pe, A["split"], g + 1)
                lit(pe, A["copied"], g)
                for k in range(GRP):
                    mm = pe.transpose(bank_b(0)[:, k * P:(k + 1) * P], hparts[:, k, :], ident_b[:, :])
                mm.then_inc(A["turned"], 1)
                pe.wait_ge(att_in[s], (j + 1) * 32)
                lit(pe, A["copied"], g + 1)
                lit(pe, A["rep_copied"], g)
                lit(pe, A["e2_made"], g)
                for h in range(2):
                    pe.matmul(ps[:, 1 + h, :], rep3[:, h * P:(h + 1) * P], hpartsT[:, :], start=True, stop=True)
                for h in range(2):
                    mm = pe.matmul(ps[:, 3 + h, :], wstack[:, h * P:(h + 1) * P], stackT[:, s, :], start=True, stop=True)
                mm.then_inc(A["product"], 1)

            def max_rows(g, s):
                lit(pe, A["scanned"], g + 1)
                lit(pe, A["max_copied"], g)
                for k in range(GRP):
                    for h in range(2):
                        at = (k % 2) * ATT + h * P
                        mm = pe.transpose(ps[:, 5 + k // 2, at:at + P], runmax[:, s, h, k * P:(k + 1) * P], ident[:, :])
                mm.then_inc(A["max_turned"], 1)
                lit(pe, A["max_copied"], g + 1)
                lit(pe, A["lastoh"], g + 1)
                lit(pe, A["max_added"], g)
                for k in range(GRP):
                    mm = pe.matmul(ps[:, 7, 0:ATT], onehot[:, s, k, :], maxE[:, k, :], start=k == 0, stop=k == GRP - 1)
                mm.then_inc(A["max_rows"], 1)

            pe.wait_ge(wstack_in, 16 * 9)
            pe.wait_ge(dense_out, 5 * dense_count[0])
            products(0, 0, 0)
            with pe.Fori(0, TRIPS - 1) as j:
                products(j * 2 + 1, j, 1)
                max_rows(j * 2, 0)
                products(j * 2 + 2, j + 1, 0)
                max_rows(j * 2 + 1, 1)
            products(TURNS - 1, TRIPS - 1, 1)
            max_rows(TURNS - 2, 0)
            max_rows(TURNS - 1, 1)

            def weights(g, j, s):
                pe.wait_ge(sum_in[s], (j + 1) * 16)
                for q in range(2):
                    lit(pe, B["made"], g * 2 + (q - 1))
                    for k in (2 * q, 2 * q + 1):
                        mm = pe.matmul(ps[:, k, :], stackT[:, s, k * P:(k + 1) * P], wmix[:, :], start=True, stop=True)
                    mm.then_inc(B["product"], 1)

            def node_sums(g, s):
                lit(pe, B["weighted"], g + 1)
                lit(pe, B["added"], g - 1)
                for k in range(GRP):
                    mm = pe.matmul(ps[:, 4 + s, :], onehot[:, s, k, :], terms[:, s, k * T:(k + 1) * T],
                                   start=k == 0, stop=k == GRP - 1)
                mm.then_inc(B["summed"], 1)

            pe.wait_ge(wmix_done, 1)
            weights(0, 0, 0)
            with pe.Fori(0, TRIPS - 1) as j:
                weights(j * 2 + 1, j, 1)
                node_sums(j * 2, 0)
                weights(j * 2 + 2, j + 1, 0)
                node_sums(j * 2 + 1, 1)
            weights(TURNS - 1, TRIPS - 1, 1)
            node_sums(TURNS - 2, 0)
            node_sums(TURNS - 1, 1)

            lit(pe, B["added"], TURNS)
            for l in range(2):
                with pe.Fori(0, TRIPS) as j:
                    for s in range(2):
                        seg_sum(f"rel{l + 1}", j, s, lambda s, k: spread[:, s, k, :], HID)
                dense(hid, HID, small[f"w{l + 1}"][:, :], small[f"b{l + 1}"][:, :], CH, (dense_in, 5 + l))
                dense(hs, CH, small[f"r{l + 1}"][:, :], None, CH, (table_made, 5 + l))

            def dst_rows(g, s):
                lit(pe, R["oh"], g + 1)
                lit(pe, R["copied"], g)
                for k in range(GRP):
                    mm = pe.transpose(ps[:, 0, k * P:(k + 1) * P], onehot[:, s, k, :], ident[:, :])
                mm.then_inc(R["turned"], 1)
                lit(pe, R["copied"], g + 1)
                lit(pe, R["spread"], g)
                b = block_of(pe, g)
                for k in range(GRP):
                    mm = pe.matmul(ps[:, 2, k * CH:(k + 1) * CH], xT[:, k, :], flat(hs[:, bass.ds(b, 1), :]),
                                   start=True, stop=True)
                mm.then_inc(R["xj"], 1)

            def scatter(g, s):
                lit(pe, R["spread"], g + 1)
                for k in range(GRP):
                    mm = pe.matmul(ps[:, 6, 0:BLOCKS * CH], spread[:, s, k, :], rea_spread[:, s, k, :],
                                   start=False, stop=False, skip_group_check=True)
                mm.then_inc(R["scattered"], 1)

            pe.wait_ge(dense_out, 5 * dense_count[0])
            pe.matmul(ps[:, 6, 0:BLOCKS * CH], zeros[:, 0:P], zeros[:, 0:BLOCKS * CH], start=True, stop=False,
                      skip_group_check=True)
            dst_rows(0, 0)
            with pe.Fori(0, TRIPS - 1) as j:
                dst_rows(j * 2 + 1, 1)
                scatter(j * 2, 0)
                dst_rows(j * 2 + 2, 0)
                scatter(j * 2 + 1, 1)
            dst_rows(TURNS - 1, 1)
            scatter(TURNS - 2, 0)
            scatter(TURNS - 1, 1)
            pe.matmul(ps[:, 6, 0:BLOCKS * CH], zeros[:, 0:P], zeros[:, 0:BLOCKS * CH], start=False, stop=True,
                      skip_group_check=True).then_inc(rea_all, 1)

        @block.scalar
        def _(act):
            for n in range(5 * SCH):
                turns = min(P, TURNS - n // 5 * P)
                to = idx_raw[:, n % 5, :].rearrange("p (i k) -> p k i", k=GRP)[:, :, n // 5 * P:n // 5 * P + turns]
                act.wait_ge(idx_turned, n + 1)
                nc.scalar.copy(to, ps[:, n % 2, :].rearrange("p (k i) -> p k i", k=GRP)[:, :, 0:turns]) \
                    .then_inc(idx_copied, 1)

            dense_count = [0]

            def dense(K, C, func, dest):
                n = dense_count[0]
                dense_count[0] += 1
                for g in range(5):
                    act.wait_ge(dense_turned, 5 * n + g + 1)
                    if n or g:
                        act.wait_ge(dense_mul, 5 * n + g)
                    nc.scalar.copy(xT[0:K, 0:4, :], ps[0:K, 0, :].rearrange("p (k e) -> p k e", k=4))
                    nc.scalar.copy(xT[0:K, 4, :], ps[0:K, 1, 0:P]).then_inc(dense_copied, 1)
                    act.wait_ge(dense_mul, 5 * n + g + 1)
                    nc.scalar.activation(dest[:, 5 * g:5 * g + 4, :],
                                         ps[:, 2, 0:4 * C].rearrange("p (k c) -> p k c", k=4), func)
                    nc.scalar.activation(dest[:, 5 * g + 4, :], ps[:, 3, 0:C], func).then_inc(dense_out, 1)

            roots = [0]

            def root():
                roots[0] += 1
                act.wait_ge(root_in, roots[0])
                nc.scalar.activation(stat[:, 1, :], stat[:, 1, :], ACT.Sqrt).then_inc(root_out, 1)

            root()
            root()
            dense(CH, HID, ACT.Relu, hid)
            dense(HID, HID, ACT.Copy, state)
            for l in range(3):
                dense(HID, HID, ACT.Copy, hid)
                if l == 0:
                    with act.Fori(0, TRIPS) as j:
                        for s in range(2):
                            t = j * 2 + s
                            lit(act, F["turned"], t + 1)
                            nc.scalar.copy(stackT[:, s, :], bank_b(6 + s)[0:KS, 0:T]).then_inc(F["copied"], 1)
                root()
            dense(HID, HID, ACT.Relu, hid)
            dense(HID, CH, ACT.Copy, ys)
            root()

            def copy_products(g):
                lit(act, A["turned"], g + 1)
                lit(act, A["product"], g)
                nc.scalar.copy(hpartsT[:, :], bank_b(0)[0:3 * CH, 0:T]).then_inc(A["copied"], 1)
                lit(act, A["product"], g + 1)
                lit(act, A["e2_made"], g)
                nc.scalar.copy(hrep, ps[:, 1:3, :]).then_inc(A["rep_copied"], 1)

            def copy_max(g):
                lit(act, A["max_turned"], g + 1)
                lit(act, A["max_rows"], g)
                nc.scalar.copy(maxE.rearrange("p (q k) c -> p q (k c)", q=2), ps[:, 5:7, :]).then_inc(A["max_copied"], 1)

            copy_products(0)
            with act.Fori(0, TRIPS - 1) as j:
                copy_products(j * 2 + 1)
                copy_max(j * 2)
                copy_products(j * 2 + 2)
                copy_max(j * 2 + 1)
            copy_products(TURNS - 1)
            copy_max(TURNS - 2)
            copy_max(TURNS - 1)

            with act.Fori(0, TRIPS) as j:
                for s in range(2):
                    lit(act, B["diff"], j * 2 + (s + 1))
                    logits = terms[:, s, :].rearrange("p (ki q o) -> p ki q o", q=2, o=CH)[:, :, 0, :]
                    nc.scalar.activation(logits, logits, ACT.Exp).then_inc(B["exp"], 1)
            root()

            for l in range(2):
                dense(HID, CH, ACT.Copy, ys)
                dense(CH, CH, ACT.Copy, zs)
            act.wait_ge(lse_in, 1)
            nc.scalar.activation(zs[:, :, :], ys[:, :, :], ACT.Exp).then_inc(lse_exp, 1)
            act.wait_ge(lse_sum, 1)
            nc.scalar.activation(stat[:, 2, :], stat[:, 1, :], ACT.Ln).then_inc(lse_ln, 1)
            root()

            with act.Fori(0, TURNS) as g:
                lit(act, R["turned"], g + 1)
                lit(act, R["xj"], g)
                nc.scalar.copy(flat(xT[:, 0:GRP, :]), ps[:, 0, :]).then_inc(R["copied"], 1)

        @block.vector
        def _(dve):
            v = nc.vector
            ch = Chain(dve, dve_step)

            def bc(ap, shape):
                return ap.to_broadcast(shape)

            v.memset(ones[:, :], 1.0)
            v.memset(zeros[:, :], 0.0)
            v.memset(stack[:, :, :], 1.0)
            v.memset(hparts[:, :, :], 0.0)
            v.memset(padi, 0)
            ch.link(v.memset(xs[:, BLOCKS - 1, :], 0.0))
            v.memset(padi[0:1, T:2 * T], -1).then_inc(pads_done, 1)
            v.memset(path[:, 3:4], -2.0)
            dve.wait_ge(iota_done, 2)
            v.tensor_copy(iota_f[:, :], iota_i)
            ch.link(v.tensor_copy(part_f[:, :], part_i[:, :]))
            v.tensor_scalar(ident[:, :], iota_row, part_f[:, 0:1], None, ALU.is_equal)
            v.tensor_scalar(ident_b[:, :], iota_row, part_f[:, 0:1], None, ALU.is_equal)
            v.tensor_scalar(rep[:, :].rearrange("p (i o) -> p i o", i=CH),
                            bc(iota_f[0:CH, 0:CH].unsqueeze(2), [CH, CH, CH]),
                            part_f[0:CH, 0:1], None, ALU.is_equal)
            v.tensor_scalar(path[:, 0:1], part_f[:, :], 1.0, float(P), ALU.add, ALU.mult).then_inc(consts_done, 1)
            dve.wait_ge(last_loaded, 32)
            v.tensor_copy(lastd_f, lastd_i).then_inc(path_cmp, 1)
            dve.wait_ge(consts_done, 1)
            dve.wait_ge(path_mm, 1)
            ch.link(v.tensor_scalar(stepblk[0:BLOCKS - 1, 0:TILES], ps[0:BLOCKS - 1, 0, 0:TILES],
                                    path[0:BLOCKS - 1, 0:1], None, ALU.is_lt))
            ch.link(v.tensor_reduce(dtmp[0:BLOCKS - 1, 0:1], stepblk[0:BLOCKS - 1, 0:TILES], AX.X, ALU.add))
            ch.link(v.tensor_tensor(path[0:BLOCKS - 1, 2:3], dtmp[0:BLOCKS - 1, 0:1], part_f[0:BLOCKS - 1, :], ALU.add))
            v.tensor_scalar(past[0:BLOCKS - 1, :], iota_f[0:BLOCKS - 1, :], path[0:BLOCKS - 1, 2:3], None, ALU.is_gt) \
             .then_inc(path_cmp, 1)
            dve.wait_ge(path_blk_mm, 1)
            v.tensor_copy(stepblk, ps[:, 2, 0:TPAD])
            ch.link(v.tensor_scalar(tcol_f[:, :], iota_f[:, 0:TPAD:P], part_f[:, 0:1], None, ALU.add))
            ch.link(v.tensor_tensor(tcol_f[:, :], tcol_f[:, :], ps[:, 4, 0:SCH], ALU.subtract))
            ch.link(v.tensor_scalar(tcol_f[:, :], tcol_f[:, :], float(ROWS - 1), None, ALU.min))
            v.tensor_copy(tcol[:, :], tcol_f[:, :]).then_inc(tcol_done, 1)
            v.tensor_copy(blk_row[:, :], stepblk[0:1, :])
            ch.link(v.tensor_tensor(past[0:1, :], iota_f[0:1, :], stepblk[0:1, :], ALU.subtract))
            ch.link(v.tensor_copy(tile_row[:, :], past[0:1, :]))
            dve.wait_ge(rows_got, 16 * 2 * SCH)
            v.tensor_copy(st_f[:, :, 0:3, :], st_i).then_inc(dst_conv, 1)
            dve.wait_ge(dst_back, 32)
            dve.wait_ge(dst_conv, 1)
            ch.link(v.tensor_tensor(st_f[:, :, 4, :], st_f[:, :, 1, :], st_next, ALU.not_equal))
            ch.link(v.tensor_tensor(st_prev, st_f[:, :, 1, :], st_prev, ALU.not_equal))
            v.tensor_scalar(st_neg, st_prev, -BIG, None, ALU.mult).then_inc(start_made, 1)
            dve.wait_ge(loaded, 16 * N_LOADS)
            ch.link(v.tensor_copy(wpart[:, 0, :], wm[:, :]))
            ch.link(v.tensor_tensor(wres, wm[:, :], wpart[:, 0, :], ALU.subtract))
            ch.link(v.tensor_copy(wpart[:, 1, :], wres))
            ch.link(v.tensor_tensor(wres, wres, wpart[:, 1, :], ALU.subtract))
            v.tensor_copy(wpart[:, 2, :], wres).then_inc(wparts_made, 1)
            dve.wait_ge(wstack_in, 16 * 9)
            for q in range(2):
                ins = v.tensor_copy(wmix[:, :].rearrange("p (i q o) -> p i q o", q=2, o=CH)[:, :, q, :],
                                    wstack[:, q * ATT:(q + 1) * ATT].rearrange("p (i o) -> p i o", o=CH))
            ins.then_inc(wmix_done, 1)
            dve.wait_ge(idx_copied, 5 * SCH)
            ch.link(v.scalar_tensor_tensor(setup_tmp.rearrange("p (i k) -> p i k", k=GRP),
                                           bc(stepblk[:, 0:TURNS].unsqueeze(2), [P, TURNS, GRP]), -float(P),
                                           idx_raw[:, 1, :].rearrange("p (i k) -> p i k", k=GRP), ALU.mult, ALU.add))
            v.tensor_copy(dstloc[:, :], setup_tmp)
            ch.link(v.tensor_scalar(setup_tmp2, setup_tmp, 0.0, None, ALU.is_ge))
            ch.link(v.scalar_tensor_tensor(setup_tmp2, setup_tmp, float(P), setup_tmp2, ALU.is_lt, ALU.mult))
            v.tensor_copy(inblk[:, :], setup_tmp2)
            ch.link(v.scalar_tensor_tensor(setup_tmp, setup_tmp, 1.0, idx_raw[:, 4, :], ALU.add, ALU.mult))
            v.tensor_scalar(lastloc[:, :], setup_tmp, -1.0, None, ALU.add)
            ch.link(v.scalar_tensor_tensor(idx_raw[:, 1, :], idx_raw[:, 1, :], -float(BLOCKS * P), setup_tmp2,
                                           ALU.add, ALU.mult))
            ch.link(v.tensor_scalar(dst_i[:, :], idx_raw[:, 1, :], float(BLOCKS * P), None, ALU.add))
            ch.link(v.tensor_copy(src_i[:, :], idx_raw[:, 0, :]))
            v.tensor_copy(type_f[:, :], idx_raw[:, 2, :])
            v.tensor_tensor(weight[:, :], idx_raw[:, 3, :], setup_tmp2, ALU.mult)
            shifted = setup_tmp.bitcast(I32)
            ch.link(v.tensor_single_scalar(shifted, src_i[:, :], 7, ALU.arith_shift_right))
            ch.link(v.tensor_copy(setup_tmp2, shifted))
            v.tensor_copy(srcblk[:, :], setup_tmp2)
            ch.link(v.scalar_tensor_tensor(srclo[:, :], setup_tmp2, -float(P), idx_raw[:, 0, :], ALU.mult, ALU.add))
            v.memset(cnt[:, :, :], 0.0).then_inc(idx_done, 1)
            dve.wait_ge(idx_done, 1)

            def equal_to(to, index, turn):
                return v.tensor_tensor(to, bc(iota_row.unsqueeze(1), [P, GRP, P]),
                                       bc(index[:, bass.ds(turn * GRP, GRP)].unsqueeze(2), [P, GRP, P]), ALU.is_equal)

            def types(s, g):
                return v.tensor_tensor(typeoh[:, s, :, :], bc(iota_f[:, 0:REL].unsqueeze(1), [P, GRP, REL]),
                                       bc(type_f[:, bass.ds(g * GRP, GRP)].unsqueeze(2), [P, GRP, REL]), ALU.is_equal)

            def make_onehot(name, j, s):
                lit(dve, S[name]["mm_done"][s], j)
                equal_to(onehot[:, s, :, :], dstloc, j * 2 + s).then_inc(S[name]["oh_ready"][s], 1)

            def add_block(name, j, s, into, C):
                lit(dve, S[name]["mm_done"][s], j + 1)
                b = block_of(dve, j * 2 + s)
                row = flat(into[:, bass.ds(b, 1), :])
                v.tensor_tensor(row, row, ps[:, 4 + s, 0:C], ALU.add).then_inc(S[name]["added"][s], 1)
                lit(dve, S[name]["added"][s], j + 1)

            with dve.Fori(0, TRIPS) as j:
                for s in range(2):
                    make_onehot("count", j, s)
                    types(s, j * 2 + s).then_inc(S["count"]["rhs_ready"][s], 1)
                for s in range(2):
                    add_block("count", j, s, cnt, REL)

            roots = [0]

            def inverse_root(to):
                roots[0] += 1
                dve.wait_ge(root_out, roots[0])
                ch.link(v.reciprocal(to, stat[:, 1, :]))

            ch.link(v.tensor_reduce(dtmp[:, :], cnt[:, :, :], AX.X, ALU.add))
            v.tensor_scalar(stat[:, 1, :], dtmp[:, :], 1.0, None, ALU.add).then_inc(root_in, 1)
            inverse_root(dinv[:, :])
            ch.link(v.tensor_scalar(invcnt[:, :, :], cnt[:, :, :], 1.0, None, ALU.max))
            ch.link(v.reciprocal(invcnt[:, :, :], invcnt[:, :, :]))

            def per_node(ap, C):
                return bc(ap.unsqueeze(2), [P, BLOCKS, C])

            def layer_norm(xin, xc, C):
                sq = tmp[:, :, 0:C] if C == HID else zs[:, :, :]
                ch.link(v.tensor_reduce(stat[:, 0, :], xin, AX.X, ALU.add))
                ch.link(v.tensor_scalar(stat[:, 0, :], stat[:, 0, :], 1.0 / C, None, ALU.mult))
                ch.link(v.tensor_tensor(xc, xin, per_node(stat[:, 0, :], C), ALU.subtract))
                ch.link(v.tensor_tensor(sq, xc, xc, ALU.mult))
                ch.link(v.tensor_reduce(stat[:, 1, :], sq, AX.X, ALU.add))
                v.tensor_scalar(stat[:, 1, :], stat[:, 1, :], 1.0 / C, EPS, ALU.mult, ALU.add).then_inc(root_in, 1)
                inverse_root(stat[:, 1, :])
                ch.link(v.tensor_tensor(xc, xc, per_node(stat[:, 1, :], C), ALU.mult))

            def layer_input(signal):
                layer_norm(xs[:, :, :], hs[:, :, :], CH)
                v.tensor_scalar(hs[:, :, :], hs[:, :, :], 0.0, None, ALU.max).then_inc(signal, 1)

            layer_input(dense_in)
            for l in range(3):
                name = f"conv{l}"
                dve.wait_ge(dense_out, 5 * (3 + l))
                v.tensor_tensor(hid, hid, per_node(dinv[:, :], HID), ALU.mult).then_inc(table_made, 1)
                dve.wait_ge(table_made, l + 1)
                ch.link(v.tensor_copy(acc, hid))
                cf = Chain(dve, chains["conv0"])
                with dve.Fori(0, TRIPS) as j:
                    if l == 0:
                        cf.enter(j, 2 * 4)
                    for s in range(2):
                        make_onehot(name, j, s)
                        if l == 0:
                            row = efrow[:, s, :, :]
                            first = stack[:, :, 0:3 * (CH + 1)].rearrange("p k (r c) -> p k r c", r=3)[:, :, :, 0:CH]
                            second = stack[:, :, 3 * (CH + 1):KS - CH].rearrange("p k (r c) -> p k r c", r=2)
                            dve.wait_ge(parts_in[s], (j + 1) * 16)
                            lit(dve, F["turned"], j * 2 + s)
                            cf.link(v.tensor_copy(first, bc(row.unsqueeze(2), [P, GRP, 3, CH])))
                            cf.link(v.tensor_tensor(efres[:, :, :], row, stack[:, :, 0:CH], ALU.subtract))
                            cf.link(v.tensor_copy(second, bc(efres[:, :, :].unsqueeze(2), [P, GRP, 2, CH])))
                            cf.link(v.tensor_tensor(efres[:, :, :], efres[:, :, :], second[:, :, 0, :], ALU.subtract))
                            v.tensor_copy(stack[:, :, KS - CH:KS], efres[:, :, :]).then_inc(F["split"], 1)
                            lit(dve, F["split"], j * 2 + (s + 1))
                    for s in range(2):
                        add_block(name, j, s, acc, HID)
                ch.link(v.tensor_tensor(acc, acc, per_node(dinv[:, :], HID), ALU.mult))
                ch.link(v.tensor_tensor(acc, acc, bc(small["bcv"].unsqueeze(1), [P, BLOCKS, HID]), ALU.add))
                ch.link(v.tensor_tensor(acc, acc, state, ALU.add))
                layer_norm(acc, state, HID)
                ch.link(v.tensor_tensor(state, state, bc(small["lg"].unsqueeze(1), [P, BLOCKS, HID]), ALU.mult))
                v.tensor_tensor(state, state, bc(small["lb"].unsqueeze(1), [P, BLOCKS, HID]), ALU.add) \
                 .then_inc(dense_in, 1)
            dve.wait_ge(dense_out, 5 * 7)
            ch.link(v.tensor_tensor(xs[:, :, :], xs[:, :, :], ys[:, :, :], ALU.add))
            layer_input(table_made)

            v.memset(runmax[:, 1, :, :], -BIG)
            ch.link(v.memset(att_max, 0.0))
            ca = Chain(dve, chains["att"])

            def split_rows(g, j, s):
                dve.wait_ge(gathered["att"][s], (j + 1) * (16 * GRP))
                rows = hsrc[:, bass.ds(g * GRP, GRP), :]
                inside = bc(inblk[:, bass.ds(g * GRP, GRP)].unsqueeze(2), [P, GRP, CH])
                v.tensor_tensor(rows, gbuf[:, s, :, 0:CH], inside, ALU.mult)
                lit(dve, A["turned"], g)
                v.tensor_tensor(hparts[:, :, 0:CH], gbuf[:, s, :, 0:CH], inside, ALU.mult).then_inc(used["att"][s], 1)
                lit(dve, used["att"][s], j + 1)
                ca.link(v.tensor_tensor(efres[:, :, :], rows, hparts[:, :, 0:CH], ALU.subtract))
                ca.link(v.tensor_copy(hparts[:, :, CH:2 * CH], efres[:, :, :]))
                ca.link(v.tensor_tensor(efres[:, :, :], efres[:, :, :], hparts[:, :, CH:2 * CH], ALU.subtract))
                v.tensor_copy(hparts[:, :, 2 * CH:3 * CH], efres[:, :, :]).then_inc(A["split"], 1)
                lit(dve, A["split"], g + 1)

            def scan(g, j, s):
                lit(dve, A["rep_copied"], g + 1)
                v.tensor_tensor(e2, ps[:, 3:5, :], hrep, ALU.mult).then_inc(A["e2_made"], 1)
                lit(dve, A["e2_made"], g + 1)
                lit(dve, A["max_turned"], g - 1)
                dve.wait_ge(att_in[s], (j + 1) * 32)
                for h in range(2):
                    ins = v.tensor_tensor_scan(runmax[:, s, h, :], starts[:, s, :], e2[:, h, :],
                                               runmax[:, 1 - s, h, T - 1:T], ALU.add, ALU.max)
                ins.then_inc(A["scanned"], 1)
                lit(dve, A["scanned"], g + 1)
                lit(dve, A["max_rows"], g - 1)
                equal_to(onehot[:, s, :, :], lastloc, g).then_inc(A["lastoh"], 1)

            def add_max(g):
                lit(dve, A["max_rows"], g + 1)
                b = block_of(dve, g)
                row = flat(att_max[:, bass.ds(b, 1), :])
                v.tensor_tensor(row, row, ps[:, 7, 0:ATT], ALU.add).then_inc(A["max_added"], 1)
                lit(dve, A["max_added"], g + 1)

            split_rows(0, 0, 0)
            split_rows(1, 0, 1)
            scan(0, 0, 0)
            with dve.Fori(0, TRIPS - 1) as j:
                ca.enter(j, 6)
                split_rows(j * 2 + 2, j + 1, 0)
                scan(j * 2 + 1, j, 1)
                add_max(j * 2)
                split_rows(j * 2 + 3, j + 1, 1)
                scan(j * 2 + 2, j + 1, 0)
                add_max(j * 2 + 1)
            ca.leave(TRIPS - 1)
            scan(TURNS - 1, TRIPS - 1, 1)
            add_max(TURNS - 2)
            lit(dve, A["max_rows"], TURNS)
            ch.link(v.tensor_copy(dtmp[:, :], dinv[:, :]))
            b = block_of(dve, TURNS - 1)
            row = flat(att_max[:, bass.ds(b, 1), :])
            v.tensor_tensor(row, row, ps[:, 7, 0:ATT], ALU.add).then_inc(max_made, 1)

            dve.wait_ge(max_made, 1)
            ch.link(v.memset(big[:, :], 0.0))
            dve.wait_ge(max_out, 32)

            def edge_terms(g, j, s, before):
                parts_of = terms[:, s, :].rearrange("p (ki q o) -> p ki q o", q=2, o=CH)
                lit(dve, B["summed"], g - 1)
                for q in range(2):
                    lit(dve, B["product"], g * 2 + (q + 1))
                    v.tensor_tensor(terms[:, s, 2 * q * T:2 * (q + 1) * T].rearrange("p (k i c) -> p k i c", k=2, i=CH),
                                    ps[:, 2 * q:2 * q + 2, :].rearrange("p k (i c) -> p k i c", i=CH),
                                    bc(hsrc[:, bass.ds(g * GRP + 2 * q, 2), :].unsqueeze(3), [P, 2, CH, 2 * CH]),
                                    ALU.mult).then_inc(B["made"], 1)
                lit(dve, B["made"], g * 2 + 2)
                dve.wait_ge(gathered["max"][s], (j + 1) * (16 * GRP))
                v.tensor_tensor(parts_of[:, :, 0, :], parts_of[:, :, 0, :],
                                gmax[:, s, :, :].rearrange("p k (i o) -> p (k i) o", o=CH), ALU.subtract) \
                 .then_inc(B["diff"], 1)
                equal_to(onehot[:, s, :, :], dstloc, g).then_inc(B["oh"], 1)
                if before is not None:
                    add_sums(before, 1 - s)
                lit(dve, B["exp"], g + 1)
                v.tensor_tensor(parts_of[:, :, 1, :], parts_of[:, :, 1, :], parts_of[:, :, 0, :], ALU.mult) \
                 .then_inc(B["weighted"], 1)

            def add_sums(g, s):
                lit(dve, B["summed"], g + 1)
                b = block_of(dve, g)
                row = flat(att_acc[:, bass.ds(b, 1), :])
                v.tensor_tensor(row, row, ps[:, 4 + s, :], ALU.add).then_inc(B["added"], 1)
                lit(dve, B["added"], g + 1)

            edge_terms(0, 0, 0, None)
            with dve.Fori(0, TRIPS - 1) as j:
                edge_terms(j * 2 + 1, j, 1, j * 2)
                edge_terms(j * 2 + 2, j + 1, 0, j * 2 + 1)
            edge_terms(TURNS - 1, TRIPS - 1, 1, TURNS - 2)
            add_sums(TURNS - 1, 1)
            sums = big[:, :].rearrange("p (bi q o) -> p bi q o", q=2, o=CH)
            den, num = sums[:, :, 0, :], sums[:, :, 1, :]
            ch.link(v.tensor_scalar(den, den, 1e-30, None, ALU.max))
            ch.link(v.reciprocal(den, den))
            ch.link(v.tensor_tensor(num, num, den, ALU.mult))
            ch.link(v.tensor_reduce(ys[:, :, :],
                                    big[:, :].rearrange("p (b i q o) -> p b q o i", b=BLOCKS, i=CH, q=2)[:, :, 1, :, :],
                                    AX.X, ALU.add))
            ch.link(v.tensor_tensor(xs[:, :, :], xs[:, :, :], ys[:, :, :], ALU.add))
            layer_input(table_made)
            dve.wait_ge(table_made, 5)

            for l in range(2):
                name = f"rel{l + 1}"
                ch.link(v.memset(acc, 0.0))
                cr = Chain(dve, chains[name])
                with dve.Fori(0, TRIPS) as j:
                    cr.enter(j, 2)
                    for s in range(2):
                        make_onehot(name, j, s)
                        cr.link(types(s, j * 2 + s))
                        dve.wait_ge(gathered[name][s], (j + 1) * (16 * GRP))
                        v.tensor_tensor(spread[:, s, :, :].rearrange("p k (r c) -> p k r c", r=REL),
                                        bc(typeoh[:, s, :, :].unsqueeze(3), [P, GRP, REL, CH]),
                                        bc(gbuf[:, s, :, 0:CH].unsqueeze(2), [P, GRP, REL, CH]),
                                        ALU.mult).then_inc(S[name]["rhs_ready"][s], 1)
                    for s in range(2):
                        add_block(name, j, s, acc, HID)
                v.tensor_tensor(hid.rearrange("p b (r c) -> p b r c", r=REL), acc.rearrange("p b (r c) -> p b r c", r=REL),
                                bc(invcnt[:, :, :].unsqueeze(3), [P, BLOCKS, REL, CH]), ALU.mult).then_inc(dense_in, 1)
                dve.wait_ge(dense_in, 5 + l)
                dve.wait_ge(dense_out, 5 * (9 + 2 * l))
                ch.link(v.tensor_tensor(ys[:, :, :], ys[:, :, :], zs[:, :, :], ALU.add))
                if l == 0:
                    v.tensor_scalar(hs[:, :, :], ys[:, :, :], 0.0, None, ALU.max).then_inc(table_made, 1)
                    dve.wait_ge(table_made, 6)
            ch.link(v.tensor_reduce(stat[:, 0, :], ys[:, :, :], AX.X, ALU.max))
            v.tensor_tensor(ys[:, :, :], ys[:, :, :], per_node(stat[:, 0, :], CH), ALU.subtract).then_inc(lse_in, 1)
            dve.wait_ge(lse_exp, 1)
            v.tensor_reduce(stat[:, 1, :], zs[:, :, :], AX.X, ALU.add).then_inc(lse_sum, 1)
            dve.wait_ge(lse_ln, 1)
            dve.wait_ge(lse_in, 1)
            ch.link(v.tensor_tensor(ys[:, :, :], ys[:, :, :], per_node(stat[:, 2, :], CH), ALU.subtract))
            ch.link(v.tensor_tensor(xs[:, :, :], xs[:, :, :], ys[:, :, :], ALU.add))
            layer_input(table_made)

            cx = Chain(dve, chains["rea"])

            def both_onehots(g, s):
                lit(dve, R["scattered"], g - 1)
                equal_to(onehot[:, s, :, :], dstloc, g).then_inc(R["oh"], 1)
                equal_to(spread[:, s, :, :], srclo, g).then_inc(R["srcoh"], 1)

            def messages(g, j, s):
                dve.wait_ge(gathered["rea"][s], (j + 1) * (16 * GRP))
                lit(dve, R["xj"], g + 1)
                xi = gbuf[:, s, :, 0:CH]
                xj = ps[:, 2, 0:GRP * CH].rearrange("p (k c) -> p k c", k=GRP)
                t0, t1 = (rea_tmp[:, q, :].rearrange("p (k c) -> p k c", k=GRP) for q in range(2))
                cx.link(v.tensor_scalar(t0, xj, 0.1, 5.0, ALU.mult, ALU.add))
                cx.link(v.scalar_tensor_tensor(t0, xi, 0.9, t0, ALU.mult, ALU.add))
                v.tensor_tensor(t1, xi, xj, ALU.mult).then_inc(used["rea"][s], 1)
                cx.link(v.reciprocal(t0, t0))
                cx.link(v.tensor_tensor(t1, t1, t0, ALU.mult))
                v.tensor_tensor(blkoh, bc(iota_f[:, 0:BLOCKS].unsqueeze(1), [P, GRP, BLOCKS]),
                                bc(srcblk[:, bass.ds(g * GRP, GRP)].unsqueeze(2), [P, GRP, BLOCKS]), ALU.is_equal)
                cx.link(v.tensor_tensor(t1, t1, bc(weight[:, bass.ds(g * GRP, GRP)].unsqueeze(2), [P, GRP, CH]), ALU.mult))
                v.tensor_tensor(rea_spread[:, s, :, :].rearrange("p k (b c) -> p k b c", b=BLOCKS),
                                bc(blkoh.unsqueeze(3), [P, GRP, BLOCKS, CH]),
                                bc(t1.unsqueeze(2), [P, GRP, BLOCKS, CH]), ALU.mult).then_inc(R["spread"], 1)
                lit(dve, R["spread"], g + 1)

            both_onehots(0, 0)
            both_onehots(1, 1)
            messages(0, 0, 0)
            with dve.Fori(0, TRIPS - 1) as j:
                cx.enter(j, 2 * 5)
                both_onehots(j * 2 + 2, 0)
                messages(j * 2 + 1, j, 1)
                both_onehots(j * 2 + 3, 1)
                messages(j * 2 + 2, j + 1, 0)
            cx.leave(TRIPS - 1)
            messages(TURNS - 1, TRIPS - 1, 1)
            ch.link(v.tensor_scalar(ys[:, :, :], hs[:, :, :], -1.0 / 5.0, 1.0, ALU.mult, ALU.add))
            ch.link(v.tensor_tensor(ys[:, :, :], ys[:, :, :], hs[:, :, :], ALU.mult))
            ch.link(v.scalar_tensor_tensor(zs[:, :, :], hs[:, :, :], -1.0, ys[:, :, :], ALU.add, ALU.mult))
            ch.link(v.scalar_tensor_tensor(xs[:, :, :], zs[:, :, :], 0.1, xs[:, :, :], ALU.add, ALU.add))
            dve.wait_ge(rea_all, 1)
            v.tensor_tensor(xs[:, :, :], xs[:, :, :], ps[:, 6, 0:BLOCKS * CH].rearrange("p (b c) -> p b c", b=BLOCKS),
                            ALU.add).then_inc(x_done, 1)


_INS = ['x', 'src', 'dst', 'edge_attr_16', 'edge_type_8', 'edge_weight',
        'L0_gnn_W_enc0', 'L0_gnn_b_enc0', 'L0_gnn_W_enc1', 'L0_gnn_b_enc1', 'L0_gnn_W_conv', 'L0_gnn_b_conv',
        'L0_gnn_ln_g', 'L0_gnn_ln_b', 'L0_gnn_W_dec0', 'L0_gnn_b_dec0', 'L0_gnn_W_dec1', 'L0_gnn_b_dec1',
        'L1_gnn_W_msg', 'L1_gnn_b_msg', 'L1_gnn_W_attn', 'L1_gnn_b_attn',
        'L2_gnn_W1', 'L2_gnn_root1', 'L2_gnn_b1', 'L2_gnn_W2', 'L2_gnn_root2', 'L2_gnn_b2']
_OUTS = [((3125, 16), 'float32')]


def kernel(**inputs):
    import numpy as _np
    import concourse.bacc as _bacc
    from concourse import mybir as _mybir
    from concourse.bass_utils import run_bass_kernel_spmd as _run

    nc = _bacc.Bacc("TRN2", target_bir_lowering=False, num_devices=1)
    arrays, args = {}, []
    for name in _INS:
        a = _np.ascontiguousarray(inputs[name])
        arrays[f"in_{name}_dram"] = a
        args.append(nc.dram_tensor(f"in_{name}_dram", a.shape, _mybir.dt.from_np(a.dtype), kind="ExternalInput").ap())
    for i, (shape, dtype) in enumerate(_OUTS):
        dt = _mybir.dt.from_np(_np.dtype(dtype))
        args.append(nc.dram_tensor(f"out_{i}_dram", shape, dt, kind="ExternalOutput").ap())
    gnn_program(nc, *args)
    r = _run(nc, [arrays], core_ids=[0])
    return r.results[0]["out_0_dram"]
```

```python
from contextlib import ExitStack

import concourse.bass as bass
from concourse import mybir

ALU = mybir.AluOpType
ACT = mybir.ActivationFunctionType
AX = mybir.AxisListType
F32 = mybir.dt.float32
BF16 = mybir.dt.bfloat16
I32 = mybir.dt.int32

P = 128
GRP = 4
T = GRP * P
N = 3125
E = 103125
BLOCKS = -(-N // P)
TILES = -(-E // T)
FULL = E // T
TAIL = E - FULL * T
TURNS = TILES + BLOCKS - 1
TRIPS = TURNS // 2
ROWS = TILES + 1
SCH = -(-TURNS // P)
TPAD = SCH * P
COLS = TURNS * GRP
REL = 8
CH = 16
HID = 128
ATT = CH * CH
ROW = CH + P // 2
KS = 6 * CH + 3
BIG = float(2.0 ** 127)
EPS = 1e-5
LIT = 2


class Chain:

    def __init__(self, eng, sem):
        self.eng, self.sem, self.n, self.base = eng, sem, 0, None

    def value(self):
        return self.n if self.base is None else self.base + self.n

    def step(self, ins):
        ins.then_inc(self.sem, 1)
        self.n += 1

    def wait(self):
        self.eng.wait_ge(self.sem, self.value())

    def link(self, ins):
        self.step(ins)
        self.wait()

    def enter(self, i, per_trip):
        self.base, self.start, self.per = i * per_trip, self.n, per_trip

    def leave(self, trips):
        assert self.n - self.start == self.per, (self.n - self.start, self.per)
        self.n = self.start + self.per * trips
        self.base = None


def gnn_program(nc, x, src, dst, edge_attr_16, edge_type_8, edge_weight,
                W_enc0, b_enc0, W_enc1, b_enc1, W_conv, b_conv, ln_g, ln_b,
                W_dec0, b_dec0, W_dec1, b_dec1, W_msg, b_msg, W_attn, b_attn,
                W1, root1, b1, W2, root2, b2, out):
    with ExitStack() as ctx:
        def sb(name, shape, dt=F32):
            return ctx.enter_context(nc.sbuf_tensor(name, shape, dt))

        def sem(name):
            return ctx.enter_context(nc.semaphore(name))

        def dram(name, shape, dt=F32):
            return nc.dram_tensor(name, shape, dt).ap()

        ctx.enter_context(nc.allow_non_contiguous_dma(reason="last dst of each tile"))

        etab = dram("etab", [ROWS, 3, T], I32)
        wtab = dram("wtab", [ROWS, T])
        etab_flat = etab.rearrange("t k e -> t (k e)")
        efpad = dram("efpad", [TURNS * T, CH])
        parts = dram("parts", [TURNS, KS, T], BF16)
        dstflat = dram("dstflat", [TPAD * T + 2])
        startflat = dram("startflat", [TPAD, T], BF16)
        conv_tab = [dram(f"conv_tab{l}", [BLOCKS * P, HID]) for l in range(3)]
        h_tab = [dram(f"h_tab{l}", [BLOCKS * P, CH if l else ROW]) for l in range(4)]
        max_tab = dram("max_tab", [BLOCKS * P + 1, ATT])

        part_i = sb("part_i", [P, 1], I32)
        iota_f = sb("iota_f", [P, TPAD])
        part_f = sb("part_f", [P, 1])
        ident = sb("ident", [P, P])
        ident_b = sb("ident_b", [P, P], BF16)
        iota_b = sb("iota_b", [P, P], BF16)
        ones = sb("ones", [P, P])
        zeros = sb("zeros", [P, BLOCKS * CH])
        path = sb("path", [P, 4])
        tcol_f = sb("tcol_f", [P, SCH])
        tcol = sb("tcol", [P, SCH], I32)
        blk_row = sb("blk_row", [1, TPAD], I32)
        tile_row = sb("tile_row", [1, TPAD], I32)
        dstloc = sb("dstloc", [P, COLS], BF16)
        lastloc = sb("lastloc", [P, COLS], BF16)
        inblk = sb("inblk", [P, COLS], BF16)
        srclo = sb("srclo", [P, COLS], BF16)
        srcblk = sb("srcblk", [P, COLS], BF16)
        type_f = sb("type_f", [P, COLS], BF16)
        src_i = sb("src_i", [P, COLS], I32)
        dst_i = sb("dst_i", [P, COLS], I32)
        weight = sb("weight", [P, COLS])
        cnt = sb("cnt", [P, BLOCKS, REL])
        invcnt = sb("invcnt", [P, BLOCKS, REL])
        dinv = sb("dinv", [P, BLOCKS])
        dtmp = sb("dtmp", [P, BLOCKS])
        stat = sb("stat", [P, 3, BLOCKS])
        xs = sb("xs", [P, BLOCKS, CH])
        hs = sb("hs", [P, BLOCKS, CH])
        ys = sb("ys", [P, BLOCKS, CH])
        zs = sb("zs", [P, BLOCKS, CH])
        big = sb("big", [P, 4 * BLOCKS * HID])
        quarter = BLOCKS * HID
        acc, _, hid, tmp = (big[:, q * quarter:(q + 1) * quarter].rearrange("p (b c) -> p b c", b=BLOCKS)
                            for q in range(4))
        att_acc = big[:, :].rearrange("p (b c) -> p b c", b=BLOCKS)
        hrep = big[:, 0:2 * T].rearrange("p (h e) -> p h e", h=2)
        runmax = big[:, 2 * T:6 * T].rearrange("p (s h e) -> p s h e", s=2, h=2)
        e2 = big[:, 6 * T:8 * T].rearrange("p (h e) -> p h e", h=2)
        maxE = big[:, 8 * T:10 * T].rearrange("p (k c) -> p k c", k=GRP)
        count_dst = big[:, 9600:9600 + GRP * P].bitcast(BF16).rearrange("p (s k c) -> p s k c", s=2, k=GRP)
        count_type = big[:, 10200:10200 + GRP * REL].bitcast(BF16).rearrange("p (s k c) -> p s k c", s=2, k=GRP)
        count_distance = big[:, 10300:10300 + T].rearrange("p (k e) -> p k e", k=GRP)
        att_rows = big[:, 10 * T:10 * T + BLOCKS * ROW].rearrange("p (b c) -> p b c", b=BLOCKS)
        att_parts = att_rows[:, :, CH:ROW].bitcast(BF16)
        rea_spread = big[:, 0:2 * GRP * BLOCKS * CH].rearrange("p (s k c) -> p s k c", s=2, k=GRP)
        rea_tmp = big[:, 4000:4000 + 2 * GRP * CH].rearrange("p (a c) -> p a c", a=2)
        blkoh = big[:, 3600:3600 + GRP * BLOCKS].rearrange("p (k b) -> p k b", k=GRP)
        rea_onehotT = big[:, 4200:4200 + 2 * T].rearrange("p (s e) -> p s e", s=2)
        rea_distance = big[:, 5400:5400 + T].rearrange("p (k e) -> p k e", k=GRP)
        rea_rows = big[:, 5300:5300 + 2 * CH].rearrange("p (s c) -> p s c", s=2)
        maxima = sb("maxima", [P, BLOCKS * ATT])
        att_max = maxima[:, :].rearrange("p (b c) -> p b c", b=BLOCKS)
        terms = maxima[:, 0:2 * GRP * T].rearrange("p (s c) -> p s c", s=2)
        gmax = maxima[:, 2 * GRP * T:2 * GRP * (T + ATT)].rearrange("p (s k c) -> p s k c", s=2, k=GRP)
        iota_i = maxima[:, 0:TPAD].bitcast(I32)
        past = maxima[:, TPAD:2 * TPAD]
        stepblk = maxima[:, 2 * TPAD:3 * TPAD]
        lastd_i = maxima[0:1, 3 * TPAD:3 * TPAD + TILES].bitcast(I32)
        lastd_f = maxima[0:1, 4 * TPAD:4 * TPAD + TILES]
        setup_tmp = maxima[:, 5 * TPAD:5 * TPAD + COLS]
        padi = maxima[0:1, 3088:3088 + 3 * T].bitcast(I32)
        wres = maxima[0:CH + 1, 4624:4624 + T]
        wpart = maxima[0:CH + 1, 5136:5136 + 3 * T // 2].bitcast(BF16).rearrange("p (q c) -> p q c", q=3)
        setup_tmp2 = maxima[:, 5 * TPAD + COLS:5 * TPAD + 2 * COLS]
        hsrc = sb("hsrc", [P, COLS, CH])
        stage = hsrc[:, :, :].rearrange("p s c -> p (s c)")
        st_i = stage[:, 0:3 * SCH * T].bitcast(I32).rearrange("p (c k e) -> p c k e", c=SCH, k=3)
        st_f = stage[:, 3 * SCH * T:8 * SCH * T].rearrange("p (c k e) -> p c k e", c=SCH, k=5)
        st_prev = stage[:, 8 * SCH * T:9 * SCH * T].rearrange("p (c e) -> p c e", c=SCH)
        st_next = stage[:, 9 * SCH * T:10 * SCH * T].rearrange("p (c e) -> p c e", c=SCH)
        st_neg = stage[:, 10 * SCH * T:11 * SCH * T].bitcast(BF16)[:, 0:SCH * T].rearrange("p (c e) -> p c e", c=SCH)
        state = stage[:, 11 * SCH * T:11 * SCH * T + quarter].rearrange("p (b c) -> p b c", b=BLOCKS)
        rows_at = sb("rows_at", [P, 2, GRP], I32)
        gbuf = sb("gbuf", [P, 2, GRP, HID])
        onehot = sb("onehot", [P, 2, GRP, P])
        spread = sb("spread", [P, 2, GRP, HID])
        typeoh = sb("typeoh", [P, 2, GRP, REL])
        xT = sb("xT", [P, 5, P])
        efrow = sb("efrow", [P, 2, GRP, CH])
        efres = sb("efres", [P, GRP, CH])
        stack = sb("stack", [P, GRP, KS], BF16)
        stackT = sb("stackT", [KS, 2, T], BF16)
        starts = sb("starts", [P, 2, T], BF16)
        hpartsT = sb("hpartsT", [3 * CH, T], BF16)
        carry = sb("carry", [P, 2])
        wm = sb("wm", [CH + 1, 2 * ATT])
        wstack = sb("wstack", [KS, 2 * ATT], BF16)
        wmix = sb("wmix", [KS, 2 * ATT], BF16)
        rep = sb("rep", [CH, ATT], BF16)
        rep3 = sb("rep3", [3 * CH, ATT], BF16)
        small = {}
        for name, shape in (("e0", [CH, HID]), ("e1", [HID, HID]), ("cv", [HID, HID]), ("d0", [HID, HID]),
                            ("d1", [HID, CH]), ("r1", [CH, CH]), ("r2", [CH, CH]), ("w1", [HID, CH]),
                            ("w2", [HID, CH]), ("be0", [1, HID]), ("be1", [1, HID]), ("bd0", [1, HID]),
                            ("bd1", [1, CH]), ("b1", [1, CH]), ("b2", [1, CH])):
            small[name] = sb("w_" + name, shape)
        for q, name in enumerate(("bcv", "lg", "lb")):
            small[name] = maxima[:, 6000 + q * HID:6000 + (q + 1) * HID]
        ps = ctx.enter_context(nc.psum_tensor("ps", [P, 8, 512], F32))

        loaded, iota_done, consts_done, pads_done = (sem(q) for q in ("loaded", "iota_done", "consts_done", "pads_done"))
        last_loaded, etab_done, tcol_done = sem("last_loaded"), sem("etab_done"), sem("tcol_done")
        path_taken, count_measured = sem("path_taken"), sem("count_measured")
        path_cmp, path_mm, path_blk_mm = sem("path_cmp"), sem("path_mm"), sem("path_blk_mm")
        rows_got, dst_conv, dst_out, dst_back, start_made, start_out = (sem(q) for q in (
            "rows_got", "dst_conv", "dst_out", "dst_back", "start_made", "start_out"))
        idx_turned, idx_copied, idx_done = sem("idx_turned"), sem("idx_copied"), sem("idx_done")
        wparts_made, wstack_in, wmix_done = sem("wparts_made"), sem("wstack_in"), sem("wmix_done")
        dense_in, dense_turned, dense_copied, dense_mul, dense_out = (sem(q) for q in (
            "dense_in", "dense_turned", "dense_copied", "dense_mul", "dense_out"))
        table_made, table_out = sem("table_made"), sem("table_out")
        max_made, max_out, att_input = sem("max_made"), sem("max_out"), sem("att_input")
        dve_step, root_in, root_out, rows_known, rows_laid = (sem(q) for q in (
            "dve_step", "root_in", "root_out", "rows_known", "rows_laid"))
        lse_in, lse_exp, lse_sum, lse_ln = (sem(q) for q in ("lse_in", "lse_exp", "lse_sum", "lse_ln"))
        x_done, stored = sem("x_done"), sem("stored")

        def pair(name):
            return [sem(f"{name}{q}") for q in range(2)]

        def table(prefix, names):
            return {k: sem(prefix + k) for k in names.split()}

        passes = ["count", "conv0", "conv1", "conv2", "rel1", "rel2"]
        S = {p: {k: pair(f"{p}_{k}") for k in ("oh_ready", "rhs_ready", "mm_done", "added")} for p in passes}
        gathered = {p: pair(p + "_gathered") for p in passes[1:] + ["att", "max", "rea"]}
        used = {"att": pair("att_used"), "rea": pair("rea_used")}
        F = table("parts_", "split turned copied")
        parts_in, parts_out = pair("parts_in"), pair("parts_out")
        A = table("att_", "turned copied product rep_copied e2_made scanned max_turned max_copied "
                          "lastoh max_rows max_added")
        att_in = pair("att_in")
        B = table("sum_", "product made diff exp weighted distance oh summed added")
        sum_in = pair("sum_in")
        R = table("rea_", "oh turned copied xj distance srcoh spread scattered")
        rea_all = sem("rea_all")
        chains = {k: sem(k + "_chain") for k in ("conv0", "rel1", "rel2", "rea")}

        idx_raw = big[:, 0:5 * COLS].rearrange("p (k s) -> p k s", k=5)
        N_ETAB = 8 + 2 + 6 + 2 + -(-(TURNS * T - E) // T)
        N_LOADS = 2 + 9 + 6 + 3 + 4

        lit_sems = [q for t in S.values() for two in t.values() for q in two]
        lit_sems += [q for two in used.values() for q in two] + parts_out
        lit_sems += [q for t in (F, A, B, R) for q in t.values()] + [count_measured]

        def lit(eng, q, n):
            eng.wait_ge(q, n + LIT)

        def bank_b(n):
            return ps[:, n, :].bitcast(BF16)

        def flat(ap):
            return ap.rearrange("p a c -> p (a c)")

        efpad_rows = efpad.rearrange("(t k p) c -> t p k c", k=GRP, p=P)
        NODES_FULL = N // P * P
        iota_row = iota_f[:, 0:P]

        block = ctx.enter_context(nc.Block())

        def block_of(eng, turn):
            return eng.value_load(blk_row[0:1, bass.ds(turn, 1)], min_val=0, max_val=BLOCKS - 1)

        def tile_of(eng, turn):
            return eng.value_load(tile_row[0:1, bass.ds(turn, 1)], min_val=0, max_val=ROWS - 1)

        @block.sync
        def _(sp):
            for q in lit_sems:
                sp.sem_inc(q, LIT)
            sp.dma_start(lastd_i[0:1, 0:FULL], dst[0:FULL * T].rearrange("(a t e) -> a t e", a=1, e=T)[:, :, T - 1]) \
              .then_inc(last_loaded, 16)
            sp.dma_start(lastd_i[0:1, FULL:TILES], dst[E - 1:E].rearrange("(a t) -> a t", a=1)) \
              .then_inc(last_loaded, 16)
            for k, column in enumerate((src, dst, edge_type_8)):
                sp.dma_start(etab[0:FULL, k, :], column[0:FULL * T].rearrange("(t e) -> t e", e=T)).then_inc(etab_done, 16)
                sp.dma_start(etab[FULL:TILES, k, 0:TAIL], column[FULL * T:E].rearrange("(t e) -> t e", t=1)) \
                  .then_inc(etab_done, 16)
            sp.dma_start(wtab[0:FULL, :], edge_weight[0:FULL * T].rearrange("(t e) -> t e", e=T)).then_inc(etab_done, 16)
            sp.dma_start(wtab[FULL:TILES, 0:TAIL], edge_weight[FULL * T:E].rearrange("(t e) -> t e", t=1)) \
              .then_inc(etab_done, 16)
            sp.wait_ge(pads_done, 1)
            for k in range(3):
                pad = padi[0:1, k * T:(k + 1) * T]
                sp.dma_start(etab[FULL:TILES, k, TAIL:T], pad[:, 0:T - TAIL]).then_inc(etab_done, 16)
                sp.dma_start(etab[TILES:ROWS, k, :], pad).then_inc(etab_done, 16)
            sp.dma_start(wtab[FULL:TILES, TAIL:T], padi[0:1, 0:T - TAIL].bitcast(F32)).then_inc(etab_done, 16)
            sp.dma_start(wtab[TILES:ROWS, :], padi[0:1, 0:T].bitcast(F32)).then_inc(etab_done, 16)
            sp.dma_start(xs[:, 0:BLOCKS - 1, :], x[0:NODES_FULL, :].rearrange("(b p) c -> p b c", p=P)).then_inc(loaded, 16)
            sp.wait_ge(consts_done, 1)
            sp.dma_start(xs[0:N - NODES_FULL, BLOCKS - 1, :], x[NODES_FULL:N, :]).then_inc(loaded, 16)
            for name, w in (("e0", W_enc0), ("e1", W_enc1), ("cv", W_conv), ("d0", W_dec0), ("d1", W_dec1),
                            ("r1", root1), ("r2", root2), ("w1", W1.rearrange("r c o -> (r c) o")),
                            ("w2", W2.rearrange("r c o -> (r c) o"))):
                sp.dma_start(small[name][:, :], w).then_inc(loaded, 16)
            for name, b in (("be0", b_enc0), ("be1", b_enc1), ("bd0", b_dec0), ("bd1", b_dec1), ("b1", b1), ("b2", b2)):
                sp.dma_start(small[name][:, :], b.rearrange("(a c) -> a c", a=1)).then_inc(loaded, 16)
            for name, b in (("bcv", b_conv), ("lg", ln_g), ("lb", ln_b)):
                sp.dma_start(small[name], b.rearrange("(a c) -> a c", a=1).to_broadcast([P, HID])).then_inc(loaded, 16)
            for q, (w, b) in enumerate(((W_attn, b_attn), (W_msg, b_msg))):
                sp.dma_start(wm[0:CH, q * ATT:(q + 1) * ATT], w).then_inc(loaded, 16)
                sp.dma_start(wm[CH:CH + 1, q * ATT:(q + 1) * ATT], b.rearrange("(a c) -> a c", a=1)).then_inc(loaded, 16)
            sp.dma_start(efpad[0:FULL * T, :], edge_attr_16[0:FULL * T, :]).then_inc(etab_done, 16)
            sp.dma_start(efpad[FULL * T:E, :], edge_attr_16[FULL * T:E, :]).then_inc(etab_done, 16)
            at = E
            while at < TURNS * T:
                n = min(T, TURNS * T - at)
                rows = next(r for r in range(P, 0, -1) if n % r == 0)
                sp.dma_start(efpad[at:at + n, :].rearrange("(p r) c -> p (r c)", p=rows), zeros[0:rows, 0:n // rows * CH]) \
                  .then_inc(etab_done, 16)
                at += n
            sp.wait_ge(dst_conv, 1)
            sp.dma_start(dstflat[1:TPAD * T + 1].rearrange("(c s e) -> s c e", s=P, e=T), st_f[:, :, 1, :]) \
              .then_inc(dst_out, 16)
            sp.dma_start(dstflat[0:1].rearrange("(a c) -> a c", a=1), path[0:1, 3:4]).then_inc(dst_out, 16)
            sp.dma_start(dstflat[TPAD * T + 1:TPAD * T + 2].rearrange("(a c) -> a c", a=1), path[0:1, 3:4]) \
              .then_inc(dst_out, 16)
            sp.wait_ge(dst_out, 48)
            sp.dma_start(st_prev, dstflat[0:TPAD * T].rearrange("(c s e) -> s c e", s=P, e=T)).then_inc(dst_back, 16)
            sp.dma_start(st_next, dstflat[2:TPAD * T + 2].rearrange("(c s e) -> s c e", s=P, e=T)).then_inc(dst_back, 16)
            sp.wait_ge(start_made, 1)
            sp.dma_start(startflat.rearrange("(c s) e -> s c e", s=P), st_neg).then_inc(start_out, 16)
            sp.wait_ge(wparts_made, 1)
            at = 0
            for q, rows in ((0, CH + 1), (1, CH + 1), (2, CH + 1), (0, CH), (1, CH), (0, CH)):
                sp.dma_start(wstack[at:at + rows, :], wpart[0:rows, q, :]).then_inc(wstack_in, 16)
                at += rows
            for q in range(3):
                sp.dma_start(rep3[q * CH:(q + 1) * CH, :], rep[:, :]).then_inc(wstack_in, 16)

            def write_table(to, nodes, nth):
                sp.wait_ge(table_made, nth)
                sp.dma_start(to.rearrange("(b p) c -> p b c", p=P), nodes).then_inc(table_out, 16)

            write_table(conv_tab[0], hid, 1)
            sp.wait_ge(etab_done, 16 * N_ETAB)
            def load_features(t, s):
                sp.dma_start(efrow[:, s, :, :],
                             efpad_rows[bass.ds(t, 1), :, :, :].rearrange("a p k c -> (a p) k c")).then_inc(parts_in[s], 16)

            def store_parts(t, s):
                lit(sp, F["copied"], t + 1)
                sp.nop(nofuse=True)
                sp.dma_start(parts[bass.ds(t, 1), :, :].rearrange("a r e -> (a r) e"), stackT[:, s, :]) \
                  .then_inc(parts_out[s], 16)

            for s in range(2):
                load_features(s, s)
            with sp.Fori(0, TRIPS - 1) as j:
                tiles = [sp.snap(j * 2 + q) for q in range(4)]
                for s in range(2):
                    lit(sp, F["split"], tiles[s] + 1)
                    sp.nop(nofuse=True)
                    load_features(tiles[s + 2], s)
                    store_parts(tiles[s], s)
            for s in range(2):
                store_parts(TURNS - 2 + s, s)
            for s in range(2):
                lit(sp, parts_out[s], 16 * TRIPS)
            write_table(conv_tab[1], hid, 2)
            write_table(conv_tab[2], hid, 3)
            write_table(h_tab[0], att_rows, 4)
            sp.wait_ge(start_out, 16)
            with sp.Fori(0, TRIPS) as j:
                for s in range(2):
                    g = sp.snap(j * 2 + s)
                    t = tile_of(sp, g)
                    lit(sp, A["product"], g - 1)
                    sp.nop(nofuse=True)
                    sp.dma_start(stackT[:, s, :], parts[bass.ds(t, 1), :, :].rearrange("a r e -> (a r) e")) \
                      .then_inc(att_in[s], 16)
                    lit(sp, A["scanned"], g - 1)
                    sp.nop(nofuse=True)
                    sp.dma_start(starts[:, s, :], startflat[bass.ds(g, 1), :].to_broadcast([P, T])) \
                      .then_inc(att_in[s], 16)
            sp.wait_ge(max_made, 1)
            sp.dma_start(max_tab[0:BLOCKS * P, :].rearrange("(b p) c -> p b c", p=P), att_max).then_inc(max_out, 16)
            sp.dma_start(max_tab[BLOCKS * P:BLOCKS * P + 1, :], zeros[0:1, 0:ATT]).then_inc(max_out, 16)
            sp.wait_ge(att_in[0], 32 * TRIPS)
            sp.wait_ge(att_in[1], 32 * TRIPS)
            lit(sp, A["product"], TURNS)
            sp.nop(nofuse=True)
            with sp.Fori(0, TRIPS) as j:
                for s in range(2):
                    g = sp.snap(j * 2 + s)
                    t = tile_of(sp, g)
                    lit(sp, B["product"], g * 2 - 1)
                    sp.nop(nofuse=True)
                    sp.dma_start(stackT[:, s, :], parts[bass.ds(t, 1), :, :].rearrange("a r e -> (a r) e")) \
                      .then_inc(sum_in[s], 16)
            for l in range(1, 4):
                write_table(h_tab[l], hs[:, :, :], 4 + l)
            sp.wait_ge(x_done, 1)
            sp.dma_start(out[0:NODES_FULL, :].rearrange("(b p) c -> p b c", p=P), xs[:, 0:BLOCKS - 1, :]).then_inc(stored, 16)
            sp.dma_start(out[NODES_FULL:N, :], xs[0:N - NODES_FULL, BLOCKS - 1, :]).then_inc(stored, 16)
            sp.wait_ge(stored, 32)
            sp.wait_ge(table_out, 16 * 7)
            sp.wait_ge(max_out, 32)
            sp.wait_ge(start_out, 16)

        @block.gpsimd
        def _(pool):
            nc.gpsimd.iota(iota_i, [[1, TPAD]], base=0, channel_multiplier=0).then_inc(iota_done, 1)
            nc.gpsimd.iota(part_i[:, :], [[0, 1]], base=0, channel_multiplier=1).then_inc(iota_done, 1)
            pool.wait_ge(tcol_done, 1)
            pool.wait_ge(etab_done, 16 * N_ETAB)
            for c in range(SCH):
                at = bass.IndirectOffsetOnAxis(tcol[:, c:c + 1], axis=0)
                nc.gpsimd.indirect_dma_start(st_i[:, c, :, :].rearrange("p k e -> p (k e)"), None, etab_flat, at) \
                    .then_inc(rows_got, 16)
                nc.gpsimd.indirect_dma_start(st_f[:, c, 3, :], None, wtab, at).then_inc(rows_got, 16)
            pool.wait_ge(idx_done, 1)
            known, laid = [0], [0]

            def gather_known(rows, dest, got):
                with pool.Fori(0, TRIPS) as j:
                    for s in range(2):
                        pool.wait_ge(rows_laid, laid[0] + j * 2 + (s + 1))
                        pool.nop(nofuse=True)
                        for k in range(GRP):
                            nc.gpsimd.indirect_dma_start(
                                dest(s, k), None, rows,
                                bass.IndirectOffsetOnAxis(rows_at[:, s, k:k + 1], axis=0)).then_inc(got[s], 16)
                laid[0] += 2 * TRIPS

            def gather_rows(rows, index, dest, got, free):
                with pool.Fori(0, TRIPS) as j:
                    for s in range(2):
                        if free is None:
                            lit(pool, B["weighted"], j * 2 + (s - 1))
                        else:
                            lit(pool, free[s], j)
                            if rows is h_tab[0]:
                                lit(pool, A["turned"], j * 2 + (s - 1))
                        nc.gpsimd.tensor_copy(rows_at[:, s, :], index[:, bass.ds(j * (2 * GRP) + s * GRP, GRP)]) \
                            .then_inc(rows_known, 1)
                        pool.wait_ge(rows_known, known[0] + j * 2 + (s + 1))
                        pool.nop(nofuse=True)
                        for k in range(GRP):
                            nc.gpsimd.indirect_dma_start(
                                dest(s, k), None, rows,
                                bass.IndirectOffsetOnAxis(rows_at[:, s, k:k + 1], axis=0)).then_inc(got[s], 16)
                known[0] += 2 * TRIPS

            def wide(s, k):
                return gbuf[:, s, k, :]

            def narrow(s, k):
                return gbuf[:, s, k, 0:CH]

            for l in range(3):
                pool.wait_ge(table_out, 16 * (l + 1))
                if l == 0:
                    gather_rows(conv_tab[0], src_i, wide, gathered["conv0"], S["conv0"]["mm_done"])
                else:
                    gather_known(conv_tab[l], wide, gathered[f"conv{l}"])
            pool.wait_ge(table_out, 16 * 4)
            gather_rows(h_tab[0], src_i, lambda s, k: gbuf[:, s, k, 0:ROW], gathered["att"], used["att"])
            pool.wait_ge(max_out, 32)
            gather_rows(max_tab, dst_i, lambda s, k: gmax[:, s, k, :], gathered["max"], None)
            for l in range(2):
                pool.wait_ge(table_out, 16 * (5 + l))
                gather_known(h_tab[1 + l], narrow, gathered[f"rel{l + 1}"])
            pool.wait_ge(table_out, 16 * 7)
            gather_rows(h_tab[3], src_i, narrow, gathered["rea"], used["rea"])

        @block.tensor
        def _(pe):
            pe.wait_ge(consts_done, 1)
            pe.wait_ge(path_cmp, 1)
            pe.matmul(ps[0:BLOCKS - 1, 0, 0:TILES], ones[0:1, 0:BLOCKS - 1], lastd_f, start=True, stop=True) \
              .then_inc(path_mm, 1)
            pe.wait_ge(path_cmp, 2)
            pe.matmul(ps[:, 2, 0:TPAD], ones[0:BLOCKS - 1, :], past[0:BLOCKS - 1, :], start=True, stop=True)
            for c in range(SCH):
                mm = pe.matmul(ps[:, 4, c:c + 1], past[0:BLOCKS - 1, c * P:(c + 1) * P], ones[0:BLOCKS - 1, 0:1],
                               start=True, stop=True)
            mm.then_inc(path_blk_mm, 1)
            dense_count = [0]

            def dense(xin, K, w, bias, C, ready):
                n = dense_count[0]
                dense_count[0] += 1
                pe.wait_ge(*ready)
                for g in range(5):
                    if n or g:
                        pe.wait_ge(dense_copied, 5 * n + g)
                    for k in range(5):
                        mm = pe.transpose(ps[0:K, k // 4, (k % 4) * P:(k % 4 + 1) * P], xin[:, 5 * g + k, :], ident[:, :])
                    mm.then_inc(dense_turned, 1)
                    pe.wait_ge(dense_copied, 5 * n + g + 1)
                    if n or g:
                        pe.wait_ge(dense_out, 5 * n + g)
                    for k in range(5):
                        o = ps[:, 2 + k // 4, (k % 4) * C:(k % 4 + 1) * C]
                        mm = pe.matmul(o, xT[0:K, k, :], w, start=True, stop=bias is None)
                        if bias is not None:
                            mm = pe.matmul(o, ones[0:1, :], bias, start=False, stop=True)
                    mm.then_inc(dense_mul, 1)

            pe.wait_ge(loaded, 16 * N_LOADS)
            pe.wait_ge(tcol_done, 1)
            pe.wait_ge(path_taken, 1)
            dense(hs, CH, small["e0"][:, :], small["be0"][:, :], HID, (dense_in, 1))
            dense(hid, HID, small["e1"][:, :], small["be1"][:, :], HID, (dense_out, 5))
            dense(state, HID, small["cv"][:, :], None, HID, (dense_out, 10))
            pe.wait_ge(dense_out, 15)
            pe.wait_ge(start_made, 1)
            for n in range(5 * SCH):
                if n >= 2:
                    pe.wait_ge(idx_copied, n - 1)
                for k in range(GRP):
                    mm = pe.transpose(ps[:, n % 2, k * P:(k + 1) * P], st_f[:, n // 5, n % 5, k * P:(k + 1) * P], ident[:, :])
                mm.then_inc(idx_turned, 1)
            pe.wait_ge(idx_copied, 5 * SCH)
            def seg_sum(name, j, s, rhs, C):
                q = S[name]
                lit(pe, q["oh_ready"][s], j + 1)
                if name.startswith("conv"):
                    pe.wait_ge(gathered[name][s], (j + 1) * (16 * GRP))
                else:
                    lit(pe, q["rhs_ready"][s], j + 1)
                lit(pe, q["added"][s], j)
                lhs = count_dst if name == "count" else onehot
                for k in range(GRP):
                    mm = pe.matmul(ps[:, 4 + s, 0:C], lhs[:, s, k, :], rhs(s, k), start=k == 0, stop=k == GRP - 1)
                mm.then_inc(q["mm_done"][s], 1)

            pe.wait_ge(idx_done, 1)
            with pe.Fori(0, TRIPS) as j:
                for s in range(2):
                    seg_sum("count", j, s, lambda s, k: count_type[:, s, k, :], REL)
            for l in range(3):
                if l:
                    dense(state, HID, small["cv"][:, :], None, HID, (dense_in, 1 + l))
                with pe.Fori(0, TRIPS) as j:
                    for s in range(2):
                        seg_sum(f"conv{l}", j, s, lambda s, k: gbuf[:, s, k, :], HID)
                        if l == 0:
                            t = j * 2 + s
                            lit(pe, F["split"], t + 1)
                            lit(pe, F["copied"], t - 1)
                            for k in range(GRP):
                                mm = pe.transpose(bank_b(6 + s)[0:KS, k * P:(k + 1) * P], stack[:, k, :], ident_b[:, :])
                            mm.then_inc(F["turned"], 1)
            dense(state, HID, small["d0"][:, :], small["bd0"][:, :], HID, (dense_in, 4))
            dense(hid, HID, small["d1"][:, :], small["bd1"][:, :], CH, (dense_out, 5 * 6))

            def turn_rows(g, j, s):
                pe.wait_ge(gathered["att"][s], (j + 1) * (16 * GRP))
                lit(pe, A["copied"], g)
                for k in range(GRP):
                    mm = pe.transpose(bank_b(0)[:, k * P:(k + 1) * P], gbuf[:, s, k, CH:ROW].bitcast(BF16), ident_b[:, :])
                mm.then_inc(A["turned"], 1)

            def products(g, j, s):
                pe.wait_ge(att_in[s], (j + 1) * 32)
                lit(pe, A["copied"], g + 1)
                lit(pe, A["rep_copied"], g)
                lit(pe, A["e2_made"], g)
                for h in range(2):
                    pe.matmul(ps[:, 1 + h, :], rep3[:, h * P:(h + 1) * P], hpartsT[:, :], start=True, stop=True)
                for h in range(2):
                    mm = pe.matmul(ps[:, 3 + h, :], wstack[:, h * P:(h + 1) * P], stackT[:, s, :], start=True, stop=True)
                mm.then_inc(A["product"], 1)

            def turn_max(g, s):
                lit(pe, A["scanned"], g + 1)
                lit(pe, A["max_copied"], g)
                for k in range(GRP):
                    for h in range(2):
                        at = (k % 2) * ATT + h * P
                        mm = pe.transpose(ps[:, 5 + k // 2, at:at + P], runmax[:, s, h, k * P:(k + 1) * P], ident[:, :])
                mm.then_inc(A["max_turned"], 1)

            def max_rows(g, s):
                lit(pe, A["max_copied"], g + 1)
                lit(pe, A["lastoh"], g + 1)
                lit(pe, A["max_added"], g)
                for k in range(GRP):
                    mm = pe.matmul(ps[:, 7, 0:ATT], onehot[:, s, k, :], maxE[:, k, :],
                                   start=k == 0, stop=k == GRP - 1)
                mm.then_inc(A["max_rows"], 1)

            pe.wait_ge(wstack_in, 16 * 9)
            pe.wait_ge(dense_out, 5 * dense_count[0])
            turn_rows(0, 0, 0)
            products(0, 0, 0)
            turn_rows(1, 0, 1)
            products(1, 0, 1)
            turn_rows(2, 1, 0)
            turn_max(0, 0)
            with pe.Fori(0, TRIPS - 2) as j:
                products(j * 2 + 2, j + 1, 0)
                turn_rows(j * 2 + 3, j + 1, 1)
                max_rows(j * 2, 0)
                turn_max(j * 2 + 1, 1)
                products(j * 2 + 3, j + 1, 1)
                turn_rows(j * 2 + 4, j + 2, 0)
                max_rows(j * 2 + 1, 1)
                turn_max(j * 2 + 2, 0)
            products(TURNS - 2, TRIPS - 1, 0)
            turn_rows(TURNS - 1, TRIPS - 1, 1)
            max_rows(TURNS - 4, 0)
            turn_max(TURNS - 3, 1)
            products(TURNS - 1, TRIPS - 1, 1)
            max_rows(TURNS - 3, 1)
            turn_max(TURNS - 2, 0)
            max_rows(TURNS - 2, 0)
            turn_max(TURNS - 1, 1)
            max_rows(TURNS - 1, 1)

            def weights(g, j, s):
                pe.wait_ge(sum_in[s], (j + 1) * 16)
                for q in range(2):
                    lit(pe, B["made"], g * 2 + (q - 1))
                    for k in (2 * q, 2 * q + 1):
                        mm = pe.matmul(ps[:, k, :], stackT[:, s, k * P:(k + 1) * P], wmix[:, :], start=True, stop=True)
                    mm.then_inc(B["product"], 1)

            def node_sums(g, s):
                lit(pe, B["weighted"], g + 1)
                lit(pe, B["oh"], g + 1)
                lit(pe, B["added"], g - 1)
                for k in range(GRP):
                    mm = pe.matmul(ps[:, 4 + s, :], onehot[:, s, k, :], terms[:, s, k * T:(k + 1) * T],
                                   start=k == 0, stop=k == GRP - 1)
                mm.then_inc(B["summed"], 1)

            pe.wait_ge(wmix_done, 1)
            weights(0, 0, 0)
            with pe.Fori(0, TRIPS - 1) as j:
                weights(j * 2 + 1, j, 1)
                node_sums(j * 2, 0)
                weights(j * 2 + 2, j + 1, 0)
                node_sums(j * 2 + 1, 1)
            weights(TURNS - 1, TRIPS - 1, 1)
            node_sums(TURNS - 2, 0)
            node_sums(TURNS - 1, 1)

            lit(pe, B["added"], TURNS)
            for l in range(2):
                with pe.Fori(0, TRIPS) as j:
                    for s in range(2):
                        seg_sum(f"rel{l + 1}", j, s, lambda s, k: spread[:, s, k, :], HID)
                dense(hid, HID, small[f"w{l + 1}"][:, :], small[f"b{l + 1}"][:, :], CH, (dense_in, 5 + l))
                dense(hs, CH, small[f"r{l + 1}"][:, :], None, CH, (table_made, 5 + l))

            def turn_onehot(g, s):
                lit(pe, R["oh"], g + 1)
                lit(pe, R["copied"], g - 1)
                for k in range(GRP):
                    mm = pe.transpose(ps[:, s, k * P:(k + 1) * P], onehot[:, s, k, :], ident[:, :])
                mm.then_inc(R["turned"], 1)

            def dst_rows(g, s):
                lit(pe, R["copied"], g + 1)
                lit(pe, R["spread"], g - 1)
                for k in range(GRP):
                    mm = pe.matmul(ps[:, 2 + s, k * CH:(k + 1) * CH], rea_onehotT[:, s, k * P:(k + 1) * P],
                                   rea_rows[:, s, :], start=True, stop=True)
                mm.then_inc(R["xj"], 1)

            def scatter(g, s):
                lit(pe, R["spread"], g + 1)
                lit(pe, R["srcoh"], g + 1)
                for k in range(GRP):
                    mm = pe.matmul(ps[:, 6, 0:BLOCKS * CH], spread[:, s, k, :], rea_spread[:, s, k, :],
                                   start=False, stop=False, skip_group_check=True)
                mm.then_inc(R["scattered"], 1)

            pe.wait_ge(dense_out, 5 * dense_count[0])
            pe.matmul(ps[:, 6, 0:BLOCKS * CH], zeros[:, 0:P], zeros[:, 0:BLOCKS * CH], start=True, stop=False,
                      skip_group_check=True)
            turn_onehot(0, 0)
            turn_onehot(1, 1)
            dst_rows(0, 0)
            with pe.Fori(0, TRIPS - 1) as j:
                turn_onehot(j * 2 + 2, 0)
                dst_rows(j * 2 + 1, 1)
                scatter(j * 2, 0)
                turn_onehot(j * 2 + 3, 1)
                dst_rows(j * 2 + 2, 0)
                scatter(j * 2 + 1, 1)
            dst_rows(TURNS - 1, 1)
            scatter(TURNS - 2, 0)
            scatter(TURNS - 1, 1)
            pe.matmul(ps[:, 6, 0:BLOCKS * CH], zeros[:, 0:P], zeros[:, 0:BLOCKS * CH], start=False, stop=True,
                      skip_group_check=True).then_inc(rea_all, 1)

        @block.scalar
        def _(act):
            dense_count = [0]

            def dense(K, C, func, dest):
                n = dense_count[0]
                dense_count[0] += 1
                for g in range(5):
                    act.wait_ge(dense_turned, 5 * n + g + 1)
                    if n or g:
                        act.wait_ge(dense_mul, 5 * n + g)
                    nc.scalar.copy(xT[0:K, 0:4, :], ps[0:K, 0, :].rearrange("p (k e) -> p k e", k=4))
                    nc.scalar.copy(xT[0:K, 4, :], ps[0:K, 1, 0:P]).then_inc(dense_copied, 1)
                    act.wait_ge(dense_mul, 5 * n + g + 1)
                    nc.scalar.activation(dest[:, 5 * g:5 * g + 4, :],
                                         ps[:, 2, 0:4 * C].rearrange("p (k c) -> p k c", k=4), func)
                    nc.scalar.activation(dest[:, 5 * g + 4, :], ps[:, 3, 0:C], func).then_inc(dense_out, 1)

            roots = [0]

            def root():
                roots[0] += 1
                act.wait_ge(root_in, roots[0])
                nc.scalar.activation(stat[:, 1, :], stat[:, 1, :], ACT.Sqrt).then_inc(root_out, 1)

            def one_hots(to, index, g, n, distance, measured, made, free, freed):
                lit(act, made, n)
                for k in range(GRP):
                    ins = nc.scalar.activation(distance[:, k, :], iota_row, ACT.Abs, scale=-1.0,
                                               bias=index[:, bass.ds(g * GRP + k, 1)])
                ins.then_inc(measured, 1)
                lit(act, measured, n + 1)
                lit(act, free, freed)
                nc.scalar.activation(to, distance, ACT.Relu, scale=-1.0, bias=ones[:, 0:1]).then_inc(made, 1)

            def lay_rows(j, s, free):
                lit(act, free[s], j)
                act.nop(nofuse=True)
                nc.scalar.copy(rows_at[:, s, :], src_i[:, bass.ds((j * 2 + s) * GRP, GRP)]).then_inc(rows_laid, 1)

            root()
            dense(CH, HID, ACT.Relu, hid)
            dense(HID, HID, ACT.Copy, state)
            dense(HID, HID, ACT.Copy, hid)
            for n in range(5 * SCH):
                turns = min(P, TURNS - n // 5 * P)
                to = idx_raw[:, n % 5, :].rearrange("p (i k) -> p k i", k=GRP)[:, :, n // 5 * P:n // 5 * P + turns]
                act.wait_ge(idx_turned, n + 1)
                nc.scalar.copy(to, ps[:, n % 2, :].rearrange("p (k i) -> p k i", k=GRP)[:, :, 0:turns]) \
                    .then_inc(idx_copied, 1)
            act.wait_ge(idx_done, 1)
            with act.Fori(0, TRIPS) as j:
                one_hots(count_dst[:, 1, :, :], dstloc, j * 2 + 1, j, count_distance, count_measured,
                         S["count"]["oh_ready"][1], S["count"]["mm_done"][1], j)
            root()
            for l in range(3):
                if l:
                    dense(HID, HID, ACT.Copy, hid)
                if l == 0:
                    with act.Fori(0, TRIPS) as j:
                        for s in range(2):
                            t = j * 2 + s
                            lit(act, F["turned"], t + 1)
                            lit(act, parts_out[s], j * 16)
                            nc.scalar.copy(stackT[:, s, :], bank_b(6 + s)[0:KS, 0:T]).then_inc(F["copied"], 1)
                else:
                    with act.Fori(0, TRIPS) as j:
                        for s in range(2):
                            lay_rows(j, s, S[f"conv{l}"]["mm_done"])
                root()
            dense(HID, HID, ACT.Relu, hid)
            dense(HID, CH, ACT.Copy, ys)
            root()

            def copy_turned(g):
                lit(act, A["turned"], g + 1)
                lit(act, A["product"], g)
                nc.scalar.copy(hpartsT[:, :], bank_b(0)[0:3 * CH, 0:T]).then_inc(A["copied"], 1)

            def copy_rep(g):
                lit(act, A["product"], g + 1)
                lit(act, A["e2_made"], g)
                nc.scalar.copy(hrep, ps[:, 1:3, :]).then_inc(A["rep_copied"], 1)

            def copy_max(g):
                lit(act, A["max_turned"], g + 1)
                lit(act, A["max_rows"], g)
                nc.scalar.copy(maxE.rearrange("p (q k) c -> p q (k c)", q=2), ps[:, 5:7, :]).then_inc(A["max_copied"], 1)

            copy_turned(0)
            copy_rep(0)
            copy_turned(1)
            with act.Fori(0, TRIPS - 1) as j:
                for s in range(2):
                    g = j * 2 + s
                    copy_rep(g + 1)
                    copy_turned(g + 2)
                    copy_max(g)
            copy_rep(TURNS - 1)
            copy_max(TURNS - 2)
            copy_max(TURNS - 1)

            with act.Fori(0, TRIPS) as j:
                for s in range(2):
                    g = j * 2 + s
                    one_hots(onehot[:, s, :, :], dstloc, g, g, spread[:, 0, :, :], B["distance"], B["oh"],
                             B["summed"], g - 1)
                    logits = terms[:, s, :].rearrange("p (h ki q o) -> p h ki q o", h=2, q=2, o=CH)
                    for h in range(2):
                        lit(act, B["diff"], j * 4 + (2 * s + h + 1))
                        nc.scalar.activation(logits[:, h, :, 0, :], logits[:, h, :, 0, :], ACT.Exp).then_inc(B["exp"], 1)
            root()

            for l in range(2):
                with act.Fori(0, TRIPS) as j:
                    for s in range(2):
                        lay_rows(j, s, S[f"rel{l + 1}"]["rhs_ready"])
                dense(HID, CH, ACT.Copy, ys)
                dense(CH, CH, ACT.Copy, zs)
            act.wait_ge(lse_in, 1)
            nc.scalar.activation(zs[:, :, :], ys[:, :, :], ACT.Exp).then_inc(lse_exp, 1)
            act.wait_ge(lse_sum, 1)
            nc.scalar.activation(stat[:, 2, :], stat[:, 1, :], ACT.Ln).then_inc(lse_ln, 1)
            root()

            with act.Fori(0, TRIPS) as j:
                for s in range(2):
                    g = j * 2 + s
                    lit(act, R["turned"], g + 1)
                    lit(act, R["xj"], g - 1)
                    nc.scalar.copy(rea_onehotT[:, s, :], ps[:, s, :])
                    b = block_of(act, g)
                    nc.scalar.copy(rea_rows[:, s, :], flat(hs[:, bass.ds(b, 1), :])).then_inc(R["copied"], 1)
                    one_hots(spread[:, s, :, :], srclo, g, g, rea_distance, R["distance"], R["srcoh"],
                             R["scattered"], g - 1)

        @block.vector
        def _(dve):
            v = nc.vector
            ch = Chain(dve, dve_step)

            def bc(ap, shape):
                return ap.to_broadcast(shape)

            v.memset(ones[:, :], 1.0)
            v.memset(zeros[:, :], 0.0)
            v.memset(stack[:, :, :], 1.0)
            v.memset(padi, 0)
            ch.link(v.memset(xs[:, BLOCKS - 1, :], 0.0))
            v.memset(padi[0:1, T:2 * T], -1).then_inc(pads_done, 1)
            v.memset(path[:, 3:4], -2.0)
            dve.wait_ge(iota_done, 2)
            v.tensor_copy(iota_f[:, :], iota_i)
            ch.link(v.tensor_copy(part_f[:, :], part_i[:, :]))
            v.tensor_copy(iota_b[:, :], iota_row)
            v.tensor_scalar(ident[:, :], iota_row, part_f[:, 0:1], None, ALU.is_equal)
            v.tensor_scalar(ident_b[:, :], iota_row, part_f[:, 0:1], None, ALU.is_equal)
            v.tensor_scalar(rep[:, :].rearrange("p (i o) -> p i o", i=CH),
                            bc(iota_f[0:CH, 0:CH].unsqueeze(2), [CH, CH, CH]),
                            part_f[0:CH, 0:1], None, ALU.is_equal)
            v.tensor_scalar(path[:, 0:1], part_f[:, :], 1.0, float(P), ALU.add, ALU.mult).then_inc(consts_done, 1)
            dve.wait_ge(last_loaded, 32)
            v.tensor_copy(lastd_f, lastd_i).then_inc(path_cmp, 1)
            dve.wait_ge(consts_done, 1)
            dve.wait_ge(path_mm, 1)
            ch.link(v.tensor_scalar(stepblk[0:BLOCKS - 1, 0:TILES], ps[0:BLOCKS - 1, 0, 0:TILES],
                                    path[0:BLOCKS - 1, 0:1], None, ALU.is_lt))
            ch.link(v.tensor_reduce(dtmp[0:BLOCKS - 1, 0:1], stepblk[0:BLOCKS - 1, 0:TILES], AX.X, ALU.add))
            ch.link(v.tensor_tensor(path[0:BLOCKS - 1, 2:3], dtmp[0:BLOCKS - 1, 0:1], part_f[0:BLOCKS - 1, :], ALU.add))
            v.tensor_scalar(past[0:BLOCKS - 1, :], iota_f[0:BLOCKS - 1, :], path[0:BLOCKS - 1, 2:3], None, ALU.is_gt) \
             .then_inc(path_cmp, 1)
            dve.wait_ge(path_blk_mm, 1)
            v.tensor_copy(stepblk, ps[:, 2, 0:TPAD])
            ch.link(v.tensor_scalar(tcol_f[:, :], iota_f[:, 0:TPAD:P], part_f[:, 0:1], None, ALU.add))
            ch.link(v.tensor_tensor(tcol_f[:, :], tcol_f[:, :], ps[:, 4, 0:SCH], ALU.subtract))
            ch.link(v.tensor_scalar(tcol_f[:, :], tcol_f[:, :], float(ROWS - 1), None, ALU.min))
            v.tensor_copy(tcol[:, :], tcol_f[:, :]).then_inc(tcol_done, 1)
            v.tensor_copy(blk_row[:, :], stepblk[0:1, :])
            ch.link(v.tensor_tensor(past[0:1, :], iota_f[0:1, :], stepblk[0:1, :], ALU.subtract))
            ch.link(v.tensor_copy(tile_row[:, :], past[0:1, :]))
            v.memset(cnt[:, :, :], 0.0).then_inc(path_taken, 1)
            roots = [0]

            def inverse_root(to):
                roots[0] += 1
                dve.wait_ge(root_out, roots[0])
                ch.link(v.reciprocal(to, stat[:, 1, :]))

            def per_node(ap, C):
                return bc(ap.unsqueeze(2), [P, BLOCKS, C])

            def layer_norm(xin, xc, C):
                sq = tmp[:, :, 0:C] if C == HID else zs[:, :, :]
                ch.link(v.tensor_reduce(stat[:, 0, :], xin, AX.X, ALU.add))
                ch.link(v.tensor_scalar(stat[:, 0, :], stat[:, 0, :], 1.0 / C, None, ALU.mult))
                ch.link(v.tensor_tensor(xc, xin, per_node(stat[:, 0, :], C), ALU.subtract))
                ch.link(v.tensor_tensor(sq, xc, xc, ALU.mult))
                ch.link(v.tensor_reduce(stat[:, 1, :], sq, AX.X, ALU.add))
                v.tensor_scalar(stat[:, 1, :], stat[:, 1, :], 1.0 / C, EPS, ALU.mult, ALU.add).then_inc(root_in, 1)
                inverse_root(stat[:, 1, :])
                ch.link(v.tensor_tensor(xc, xc, per_node(stat[:, 1, :], C), ALU.mult))

            def layer_input(signal):
                layer_norm(xs[:, :, :], hs[:, :, :], CH)
                v.tensor_scalar(hs[:, :, :], hs[:, :, :], 0.0, None, ALU.max).then_inc(signal, 1)

            dve.wait_ge(loaded, 16 * N_LOADS)
            layer_input(dense_in)
            dve.wait_ge(rows_got, 16 * 2 * SCH)
            v.tensor_copy(st_f[:, :, 0:3, :], st_i).then_inc(dst_conv, 1)
            dve.wait_ge(dst_back, 32)
            dve.wait_ge(dst_conv, 1)
            ch.link(v.tensor_tensor(st_f[:, :, 4, :], st_f[:, :, 1, :], st_next, ALU.not_equal))
            ch.link(v.tensor_tensor(st_prev, st_f[:, :, 1, :], st_prev, ALU.not_equal))
            v.tensor_scalar(st_neg, st_prev, -BIG, None, ALU.mult).then_inc(start_made, 1)
            dve.wait_ge(loaded, 16 * N_LOADS)
            ch.link(v.tensor_copy(wpart[:, 0, :], wm[:, :]))
            ch.link(v.tensor_tensor(wres, wm[:, :], wpart[:, 0, :], ALU.subtract))
            ch.link(v.tensor_copy(wpart[:, 1, :], wres))
            ch.link(v.tensor_tensor(wres, wres, wpart[:, 1, :], ALU.subtract))
            v.tensor_copy(wpart[:, 2, :], wres).then_inc(wparts_made, 1)
            dve.wait_ge(wstack_in, 16 * 9)
            for q in range(2):
                ins = v.tensor_copy(wmix[:, :].rearrange("p (i q o) -> p i q o", q=2, o=CH)[:, :, q, :],
                                    wstack[:, q * ATT:(q + 1) * ATT].rearrange("p (i o) -> p i o", o=CH))
            ins.then_inc(wmix_done, 1)
            dve.wait_ge(idx_copied, 5 * SCH)
            ch.link(v.scalar_tensor_tensor(setup_tmp.rearrange("p (i k) -> p i k", k=GRP),
                                           bc(stepblk[:, 0:TURNS].unsqueeze(2), [P, TURNS, GRP]), -float(P),
                                           idx_raw[:, 1, :].rearrange("p (i k) -> p i k", k=GRP), ALU.mult, ALU.add))
            v.tensor_copy(dstloc[:, :], setup_tmp)
            ch.link(v.tensor_scalar(setup_tmp2, setup_tmp, 0.0, None, ALU.is_ge))
            ch.link(v.scalar_tensor_tensor(setup_tmp2, setup_tmp, float(P), setup_tmp2, ALU.is_lt, ALU.mult))
            v.tensor_copy(inblk[:, :], setup_tmp2)
            ch.link(v.scalar_tensor_tensor(setup_tmp, setup_tmp, 1.0, idx_raw[:, 4, :], ALU.add, ALU.mult))
            v.tensor_scalar(lastloc[:, :], setup_tmp, -1.0, None, ALU.add)
            ch.link(v.scalar_tensor_tensor(idx_raw[:, 1, :], idx_raw[:, 1, :], -float(BLOCKS * P), setup_tmp2,
                                           ALU.add, ALU.mult))
            ch.link(v.tensor_scalar(dst_i[:, :], idx_raw[:, 1, :], float(BLOCKS * P), None, ALU.add))
            ch.link(v.tensor_copy(src_i[:, :], idx_raw[:, 0, :]))
            v.tensor_copy(type_f[:, :], idx_raw[:, 2, :])
            v.tensor_tensor(weight[:, :], idx_raw[:, 3, :], setup_tmp2, ALU.mult)
            shifted = setup_tmp.bitcast(I32)
            ch.link(v.tensor_single_scalar(shifted, src_i[:, :], 7, ALU.arith_shift_right))
            ch.link(v.tensor_copy(setup_tmp2, shifted))
            v.tensor_copy(srcblk[:, :], setup_tmp2)
            v.scalar_tensor_tensor(srclo[:, :], setup_tmp2, -float(P), idx_raw[:, 0, :], ALU.mult, ALU.add) \
             .then_inc(idx_done, 1)
            dve.wait_ge(idx_done, 1)

            def equal_to(to, index, turn):
                return v.tensor_tensor(to, bc(iota_row.unsqueeze(1), [P, GRP, P]),
                                       bc(index[:, bass.ds(turn * GRP, GRP)].unsqueeze(2), [P, GRP, P]), ALU.is_equal)

            def types(s, g):
                return v.tensor_tensor(typeoh[:, s, :, :], bc(iota_f[:, 0:REL].unsqueeze(1), [P, GRP, REL]),
                                       bc(type_f[:, bass.ds(g * GRP, GRP)].unsqueeze(2), [P, GRP, REL]), ALU.is_equal)

            def make_onehot(name, j, s):
                lit(dve, S[name]["mm_done"][s], j)
                equal_to(onehot[:, s, :, :], dstloc, j * 2 + s).then_inc(S[name]["oh_ready"][s], 1)

            def add_block(name, j, s, into, C):
                b = block_of(dve, j * 2 + s)
                lit(dve, S[name]["mm_done"][s], j + 1)
                lit(dve, S[name]["added"][1 - s], j + s)
                row = flat(into[:, bass.ds(b, 1), :])
                v.tensor_tensor(row, row, ps[:, 4 + s, 0:C], ALU.add).then_inc(S[name]["added"][s], 1)

            def all_added(name):
                for s in range(2):
                    lit(dve, S[name]["added"][s], TRIPS)

            def count_onehots(j, s):
                g = j * 2 + s
                lit(dve, S["count"]["mm_done"][s], j)
                if s == 0:
                    v.tensor_tensor(count_dst[:, s, :, :], bc(iota_b[:, :].unsqueeze(1), [P, GRP, P]),
                                    bc(dstloc[:, bass.ds(g * GRP, GRP)].unsqueeze(2), [P, GRP, P]), ALU.is_equal) \
                     .then_inc(S["count"]["oh_ready"][s], 1)
                v.tensor_tensor(count_type[:, s, :, :], bc(iota_b[:, 0:REL].unsqueeze(1), [P, GRP, REL]),
                                bc(type_f[:, bass.ds(g * GRP, GRP)].unsqueeze(2), [P, GRP, REL]), ALU.is_equal) \
                 .then_inc(S["count"]["rhs_ready"][s], 1)

            for s in range(2):
                count_onehots(0, s)
            with dve.Fori(0, TRIPS - 1) as j:
                for s in range(2):
                    count_onehots(j + 1, s)
                    add_block("count", j, s, cnt, REL)
            for s in range(2):
                add_block("count", TRIPS - 1, s, cnt, REL)
            all_added("count")

            ch.link(v.tensor_reduce(dtmp[:, :], cnt[:, :, :], AX.X, ALU.add))
            v.tensor_scalar(stat[:, 1, :], dtmp[:, :], 1.0, None, ALU.add).then_inc(root_in, 1)
            inverse_root(dinv[:, :])
            ch.link(v.tensor_scalar(invcnt[:, :, :], cnt[:, :, :], 1.0, None, ALU.max))
            ch.link(v.reciprocal(invcnt[:, :, :], invcnt[:, :, :]))

            for l in range(3):
                name = f"conv{l}"
                dve.wait_ge(dense_out, 5 * (3 + l))
                v.tensor_tensor(hid, hid, per_node(dinv[:, :], HID), ALU.mult).then_inc(table_made, 1)
                dve.wait_ge(table_made, l + 1)
                ch.link(v.tensor_copy(acc, hid))
                cf = Chain(dve, chains["conv0"])
                with dve.Fori(0, TRIPS) as j:
                    if l == 0:
                        cf.enter(j, 2 * 4)
                    for s in range(2):
                        make_onehot(name, j, s)
                    for s in range(2):
                        if l == 0:
                            row = efrow[:, s, :, :]
                            first = stack[:, :, 0:3 * (CH + 1)].rearrange("p k (r c) -> p k r c", r=3)[:, :, :, 0:CH]
                            second = stack[:, :, 3 * (CH + 1):KS - CH].rearrange("p k (r c) -> p k r c", r=2)
                            dve.wait_ge(parts_in[s], (j + 1) * 16)
                            lit(dve, F["turned"], j * 2 + s)
                            cf.link(v.tensor_copy(first, bc(row.unsqueeze(2), [P, GRP, 3, CH])))
                            cf.link(v.tensor_tensor(efres[:, :, :], row, stack[:, :, 0:CH], ALU.subtract))
                            cf.link(v.tensor_copy(second, bc(efres[:, :, :].unsqueeze(2), [P, GRP, 2, CH])))
                            cf.link(v.tensor_tensor(efres[:, :, :], efres[:, :, :], second[:, :, 0, :], ALU.subtract))
                            v.tensor_copy(stack[:, :, KS - CH:KS], efres[:, :, :]).then_inc(F["split"], 1)
                            lit(dve, F["split"], j * 2 + (s + 1))
                    for s in range(2):
                        add_block(name, j, s, acc, HID)
                all_added(name)
                ch.link(v.tensor_tensor(acc, acc, per_node(dinv[:, :], HID), ALU.mult))
                ch.link(v.tensor_tensor(acc, acc, bc(small["bcv"].unsqueeze(1), [P, BLOCKS, HID]), ALU.add))
                ch.link(v.tensor_tensor(acc, acc, state, ALU.add))
                layer_norm(acc, state, HID)
                ch.link(v.tensor_tensor(state, state, bc(small["lg"].unsqueeze(1), [P, BLOCKS, HID]), ALU.mult))
                v.tensor_tensor(state, state, bc(small["lb"].unsqueeze(1), [P, BLOCKS, HID]), ALU.add) \
                 .then_inc(dense_in, 1)
            dve.wait_ge(dense_out, 5 * 7)
            ch.link(v.tensor_tensor(xs[:, :, :], xs[:, :, :], ys[:, :, :], ALU.add))
            v.memset(att_rows, 0.0)
            layer_input(att_input)
            dve.wait_ge(att_input, 1)
            res = zs[:, :, :]
            v.tensor_copy(att_rows[:, :, 0:CH], hs[:, :, :])
            ch.link(v.tensor_copy(att_parts[:, :, 0:CH], hs[:, :, :]))
            ch.link(v.tensor_tensor(res, hs[:, :, :], att_parts[:, :, 0:CH], ALU.subtract))
            ch.link(v.tensor_copy(att_parts[:, :, CH:2 * CH], res))
            ch.link(v.tensor_tensor(res, res, att_parts[:, :, CH:2 * CH], ALU.subtract))
            v.tensor_copy(att_parts[:, :, 2 * CH:3 * CH], res).then_inc(table_made, 1)

            v.memset(runmax[:, 1, :, :], -BIG)
            ch.link(v.memset(att_max, 0.0))

            def keep_rows(g, j, s):
                dve.wait_ge(gathered["att"][s], (j + 1) * (16 * GRP))
                v.tensor_tensor(hsrc[:, bass.ds(g * GRP, GRP), :], gbuf[:, s, :, 0:CH],
                                bc(inblk[:, bass.ds(g * GRP, GRP)].unsqueeze(2), [P, GRP, CH]), ALU.mult) \
                 .then_inc(used["att"][s], 1)

            def add_max(g):
                lit(dve, A["max_rows"], g + 1)
                b = block_of(dve, g)
                row = flat(att_max[:, bass.ds(b, 1), :])
                v.tensor_tensor(row, row, ps[:, 7, 0:ATT], ALU.add).then_inc(A["max_added"], 1)
                lit(dve, A["max_added"], g + 1)

            def scan(g, j, s, before):
                lit(dve, A["rep_copied"], g + 1)
                lit(dve, A["scanned"], g)
                v.tensor_tensor(e2, ps[:, 3:5, :], hrep, ALU.mult).then_inc(A["e2_made"], 1)
                if before is not None:
                    add_max(before)
                lit(dve, A["max_rows"], g - 1)
                equal_to(onehot[:, s, :, :], lastloc, g).then_inc(A["lastoh"], 1)
                lit(dve, A["e2_made"], g + 1)
                lit(dve, A["max_turned"], g - 1)
                dve.wait_ge(att_in[s], (j + 1) * 32)
                for h in range(2):
                    ins = v.tensor_tensor_scan(runmax[:, s, h, :], starts[:, s, :], e2[:, h, :],
                                               runmax[:, 1 - s, h, T - 1:T], ALU.add, ALU.max)
                ins.then_inc(A["scanned"], 1)

            for s in range(2):
                keep_rows(s, 0, s)
            for s in range(2):
                scan(s, 0, s, None)
                keep_rows(s + 2, 1, s)
            with dve.Fori(1, TRIPS - 1) as j:
                for s in range(2):
                    g = j * 2 + s
                    scan(g, j, s, g - 2)
                    keep_rows(g + 2, j + 1, s)
            for s in range(2):
                scan(TURNS - 2 + s, TRIPS - 1, s, TURNS - 4 + s)
            add_max(TURNS - 2)
            lit(dve, A["max_rows"], TURNS)
            ch.link(v.tensor_copy(dtmp[:, :], dinv[:, :]))
            b = block_of(dve, TURNS - 1)
            row = flat(att_max[:, bass.ds(b, 1), :])
            v.tensor_tensor(row, row, ps[:, 7, 0:ATT], ALU.add).then_inc(max_made, 1)

            dve.wait_ge(max_made, 1)
            ch.link(v.memset(big[:, :], 0.0))
            dve.wait_ge(max_out, 32)

            def edge_terms(g, j, s, before):
                parts_of = terms[:, s, :].rearrange("p (ki q o) -> p ki q o", q=2, o=CH)
                b = block_of(dve, before) if before is not None else None
                lit(dve, B["summed"], g - 1)
                for q in range(2):
                    lit(dve, B["product"], g * 2 + (q + 1))
                    v.tensor_tensor(terms[:, s, 2 * q * T:2 * (q + 1) * T].rearrange("p (k i c) -> p k i c", k=2, i=CH),
                                    ps[:, 2 * q:2 * q + 2, :].rearrange("p k (i c) -> p k i c", i=CH),
                                    bc(hsrc[:, bass.ds(g * GRP + 2 * q, 2), :].unsqueeze(3), [P, 2, CH, 2 * CH]),
                                    ALU.mult).then_inc(B["made"], 1)
                dve.wait_ge(gathered["max"][s], (j + 1) * (16 * GRP))
                for q in range(2):
                    half = slice(2 * q * CH, 2 * (q + 1) * CH)
                    lit(dve, B["made"], g * 2 + (q + 1))
                    v.tensor_tensor(parts_of[:, half, 0, :], parts_of[:, half, 0, :],
                                    gmax[:, s, 2 * q:2 * q + 2, :].rearrange("p k (i o) -> p (k i) o", o=CH),
                                    ALU.subtract).then_inc(B["diff"], 1)
                if before is not None:
                    add_sums(before, s, b)
                for q in range(2):
                    half = slice(2 * q * CH, 2 * (q + 1) * CH)
                    lit(dve, B["exp"], g * 2 + (q + 1))
                    ins = v.tensor_tensor(parts_of[:, half, 1, :], parts_of[:, half, 1, :], parts_of[:, half, 0, :],
                                          ALU.mult)
                ins.then_inc(B["weighted"], 1)

            def add_sums(g, s, b):
                lit(dve, B["summed"], g + 1)
                lit(dve, B["added"], g)
                row = flat(att_acc[:, bass.ds(b, 1), :])
                v.tensor_tensor(row, row, ps[:, 4 + s, :], ALU.add).then_inc(B["added"], 1)

            for s in range(2):
                edge_terms(s, 0, s, None)
            with dve.Fori(1, TRIPS) as j:
                for s in range(2):
                    edge_terms(j * 2 + s, j, s, j * 2 + (s - 2))
            for s in range(2):
                add_sums(TURNS - 2 + s, s, block_of(dve, TURNS - 2 + s))
            lit(dve, B["added"], TURNS)
            sums = big[:, :].rearrange("p (bi q o) -> p bi q o", q=2, o=CH)
            den, num = sums[:, :, 0, :], sums[:, :, 1, :]
            ch.link(v.tensor_scalar(den, den, 1e-30, None, ALU.max))
            ch.link(v.reciprocal(den, den))
            ch.link(v.tensor_tensor(num, num, den, ALU.mult))
            ch.link(v.tensor_reduce(ys[:, :, :],
                                    big[:, :].rearrange("p (b i q o) -> p b q o i", b=BLOCKS, i=CH, q=2)[:, :, 1, :, :],
                                    AX.X, ALU.add))
            ch.link(v.tensor_tensor(xs[:, :, :], xs[:, :, :], ys[:, :, :], ALU.add))
            layer_input(table_made)
            dve.wait_ge(table_made, 5)

            for l in range(2):
                name = f"rel{l + 1}"
                ch.link(v.memset(acc, 0.0))
                cr = Chain(dve, chains[name])
                with dve.Fori(0, TRIPS) as j:
                    cr.enter(j, 2)
                    for s in range(2):
                        make_onehot(name, j, s)
                        cr.link(types(s, j * 2 + s))
                        dve.wait_ge(gathered[name][s], (j + 1) * (16 * GRP))
                        v.tensor_tensor(spread[:, s, :, :].rearrange("p k (r c) -> p k r c", r=REL),
                                        bc(typeoh[:, s, :, :].unsqueeze(3), [P, GRP, REL, CH]),
                                        bc(gbuf[:, s, :, 0:CH].unsqueeze(2), [P, GRP, REL, CH]),
                                        ALU.mult).then_inc(S[name]["rhs_ready"][s], 1)
                    for s in range(2):
                        add_block(name, j, s, acc, HID)
                all_added(name)
                v.tensor_tensor(hid.rearrange("p b (r c) -> p b r c", r=REL), acc.rearrange("p b (r c) -> p b r c", r=REL),
                                bc(invcnt[:, :, :].unsqueeze(3), [P, BLOCKS, REL, CH]), ALU.mult).then_inc(dense_in, 1)
                dve.wait_ge(dense_in, 5 + l)
                dve.wait_ge(dense_out, 5 * (9 + 2 * l))
                ch.link(v.tensor_tensor(ys[:, :, :], ys[:, :, :], zs[:, :, :], ALU.add))
                if l == 0:
                    v.tensor_scalar(hs[:, :, :], ys[:, :, :], 0.0, None, ALU.max).then_inc(table_made, 1)
                    dve.wait_ge(table_made, 6)
            ch.link(v.tensor_reduce(stat[:, 0, :], ys[:, :, :], AX.X, ALU.max))
            v.tensor_tensor(ys[:, :, :], ys[:, :, :], per_node(stat[:, 0, :], CH), ALU.subtract).then_inc(lse_in, 1)
            dve.wait_ge(lse_exp, 1)
            v.tensor_reduce(stat[:, 1, :], zs[:, :, :], AX.X, ALU.add).then_inc(lse_sum, 1)
            dve.wait_ge(lse_ln, 1)
            dve.wait_ge(lse_in, 1)
            ch.link(v.tensor_tensor(ys[:, :, :], ys[:, :, :], per_node(stat[:, 2, :], CH), ALU.subtract))
            ch.link(v.tensor_tensor(xs[:, :, :], xs[:, :, :], ys[:, :, :], ALU.add))
            layer_input(table_made)

            cx = Chain(dve, chains["rea"])

            def dst_onehot(g, s):
                lit(dve, R["turned"], g - 1)
                equal_to(onehot[:, s, :, :], dstloc, g).then_inc(R["oh"], 1)

            def messages(g, j, s, ahead):
                lit(dve, R["scattered"], g - 1)
                lit(dve, R["spread"], g)
                v.tensor_tensor(blkoh, bc(iota_f[:, 0:BLOCKS].unsqueeze(1), [P, GRP, BLOCKS]),
                                bc(srcblk[:, bass.ds(g * GRP, GRP)].unsqueeze(2), [P, GRP, BLOCKS]), ALU.is_equal)
                dve.wait_ge(gathered["rea"][s], (j + 1) * (16 * GRP))
                lit(dve, R["xj"], g + 1)
                xi = gbuf[:, s, :, 0:CH]
                xj = ps[:, 2 + s, 0:GRP * CH].rearrange("p (k c) -> p k c", k=GRP)
                t0, t1 = (rea_tmp[:, q, :].rearrange("p (k c) -> p k c", k=GRP) for q in range(2))
                v.tensor_scalar(t0, xj, 0.1, 5.0, ALU.mult, ALU.add)
                cx.link(v.tensor_tensor(t1, xi, xj, ALU.mult))
                v.scalar_tensor_tensor(t0, xi, 0.9, t0, ALU.mult, ALU.add).then_inc(used["rea"][s], 1)
                cx.link(v.tensor_tensor(t1, t1, bc(weight[:, bass.ds(g * GRP, GRP)].unsqueeze(2), [P, GRP, CH]), ALU.mult))
                cx.step(v.reciprocal(t0, t0))
                if ahead is not None:
                    dst_onehot(ahead, s)
                cx.wait()
                cx.link(v.tensor_tensor(t1, t1, t0, ALU.mult))
                v.tensor_tensor(rea_spread[:, s, :, :].rearrange("p k (b c) -> p k b c", b=BLOCKS),
                                bc(blkoh.unsqueeze(3), [P, GRP, BLOCKS, CH]),
                                bc(t1.unsqueeze(2), [P, GRP, BLOCKS, CH]), ALU.mult).then_inc(R["spread"], 1)

            dst_onehot(0, 0)
            dst_onehot(1, 1)
            messages(0, 0, 0, 2)
            with dve.Fori(0, TRIPS - 2) as j:
                cx.enter(j, 2 * 4)
                messages(j * 2 + 1, j, 1, j * 2 + 3)
                messages(j * 2 + 2, j + 1, 0, j * 2 + 4)
            cx.leave(TRIPS - 2)
            messages(TURNS - 3, TRIPS - 2, 1, TURNS - 1)
            messages(TURNS - 2, TRIPS - 1, 0, None)
            messages(TURNS - 1, TRIPS - 1, 1, None)
            ch.link(v.tensor_scalar(ys[:, :, :], hs[:, :, :], -1.0 / 5.0, 1.0, ALU.mult, ALU.add))
            ch.link(v.tensor_tensor(ys[:, :, :], ys[:, :, :], hs[:, :, :], ALU.mult))
            ch.link(v.scalar_tensor_tensor(zs[:, :, :], hs[:, :, :], -1.0, ys[:, :, :], ALU.add, ALU.mult))
            ch.link(v.scalar_tensor_tensor(xs[:, :, :], zs[:, :, :], 0.1, xs[:, :, :], ALU.add, ALU.add))
            dve.wait_ge(rea_all, 1)
            v.tensor_tensor(xs[:, :, :], xs[:, :, :], ps[:, 6, 0:BLOCKS * CH].rearrange("p (b c) -> p b c", b=BLOCKS),
                            ALU.add).then_inc(x_done, 1)


_INS = ['x', 'src', 'dst', 'edge_attr_16', 'edge_type_8', 'edge_weight',
        'L0_gnn_W_enc0', 'L0_gnn_b_enc0', 'L0_gnn_W_enc1', 'L0_gnn_b_enc1', 'L0_gnn_W_conv', 'L0_gnn_b_conv',
        'L0_gnn_ln_g', 'L0_gnn_ln_b', 'L0_gnn_W_dec0', 'L0_gnn_b_dec0', 'L0_gnn_W_dec1', 'L0_gnn_b_dec1',
        'L1_gnn_W_msg', 'L1_gnn_b_msg', 'L1_gnn_W_attn', 'L1_gnn_b_attn',
        'L2_gnn_W1', 'L2_gnn_root1', 'L2_gnn_b1', 'L2_gnn_W2', 'L2_gnn_root2', 'L2_gnn_b2']
_OUTS = [((3125, 16), 'float32')]


def kernel(**inputs):
    import numpy as _np
    import concourse.bacc as _bacc
    from concourse import mybir as _mybir
    from concourse.bass_utils import run_bass_kernel_spmd as _run

    nc = _bacc.Bacc("TRN2", target_bir_lowering=False, num_devices=1)
    arrays, args = {}, []
    for name in _INS:
        a = _np.ascontiguousarray(inputs[name])
        arrays[f"in_{name}_dram"] = a
        args.append(nc.dram_tensor(f"in_{name}_dram", a.shape, _mybir.dt.from_np(a.dtype), kind="ExternalInput").ap())
    for i, (shape, dtype) in enumerate(_OUTS):
        dt = _mybir.dt.from_np(_np.dtype(dtype))
        args.append(nc.dram_tensor(f"out_{i}_dram", shape, dt, kind="ExternalOutput").ap())
    gnn_program(nc, *args)
    r = _run(nc, [arrays], core_ids=[0])
    return r.results[0]["out_0_dram"]
```
